# Optimizing a Trainium2 kernel written in Bass

```python
import numpy as np
import jax
import jax.numpy as jnp

def _softmax(x, axis=-1):
    return jax.nn.softmax(x, axis=axis)

def _gelu(x):
    return jax.nn.gelu(x, approximate=True)

def _silu(x):
    return jax.nn.silu(x)

def _sigmoid(x):
    return jax.nn.sigmoid(x)

def _layernorm(x, axis=-1, eps=1e-05):
    m = jnp.mean(x, axis=axis, keepdims=True)
    v = jnp.var(x, axis=axis, keepdims=True)
    return (x - m) / jnp.sqrt(v + eps)

def _scatter_add(tgt, idx, src, axis=0):
    return tgt.at[idx].add(src)

def _segment_sum(src, seg, n):
    return jax.ops.segment_sum(src, seg, n)
kernel_name = 'mk_perceiver_d1_seqx_r4_2f5d79'

def setup_inputs(seed: int=0):
    np.random.seed(seed)
    _w = jnp.asarray

    def _rec_inputs():
        import jax
        import jax.numpy as jnp
        _rk = jax.random.key(seed)
        x = -0.0003929 + 0.9999 * jax.random.normal(jax.random.fold_in(_rk, 1), (4, 256, 256), jnp.float32)
        _lenS = 256 - jax.random.randint(jax.random.fold_in(_rk, 7), (4,), 0, max(1, 256 // 4) + 1, jnp.int32)
        _lenS2 = 4096 - jax.random.randint(jax.random.fold_in(_rk, 8), (4,), 0, max(1, 4096 // 4) + 1, jnp.int32)
        _ctx_1024P = jax.random.normal(jax.random.fold_in(_rk, 11), (4, 16, 256), jnp.float32)
        _ctx_1024c = jax.random.dirichlet(jax.random.fold_in(_rk, 511), 0.3 * jnp.ones((16,), jnp.float32), (4, 4096))
        _ctx_1024t = jnp.einsum('bsk,bkd->bsd', _ctx_1024c, _ctx_1024P)
        _ctx_1024t = _ctx_1024t * jax.lax.rsqrt(jnp.mean(jnp.square(_ctx_1024t)) + 1e-12) * 0.953939
        ctx_1024 = 2.81802e-05 + 1.00001 * (_ctx_1024t + 0.3 * jax.random.normal(jax.random.fold_in(_rk, 611), (4, 4096, 256), jnp.float32))
        _validS = jnp.arange(256)[None, :] < _lenS[:, None]
        _validS2 = jnp.arange(4096)[None, :] < _lenS2[:, None]
        _causal = jnp.tril(jnp.ones((256, 256), dtype=bool))
        mask_BxSxS2_fk0 = jnp.where(jnp.broadcast_to(_validS2[:, None, :], (4, 256, 4096)), 1.4285714626312256, 0.0).astype(jnp.float32)
        return (x, ctx_1024, mask_BxSxS2_fk0)
    x, ctx_1024, mask_BxSxS2_fk0 = _rec_inputs()

    def _L0_xattn_setup():
        import jax, jax.numpy as jnp
        import numpy as np
        B, SQ, SKV, D = (8, 512, 512, 256)
        DROP_P = 0.3
        key = jax.random.key(seed)
        k1, k2, k3, k4, k5, k6 = jax.random.split(key, 6)
        q1 = jax.random.normal(k1, (B, SQ, D), dtype=jnp.float32)
        k_ = jax.random.normal(k2, (B, SKV, D), dtype=jnp.float32)
        v_ = jax.random.normal(k3, (B, SKV, D), dtype=jnp.float32)
        weights = jax.random.normal(k4, (D, D), dtype=jnp.float32)
        bias = jax.random.normal(k5, (D,), dtype=jnp.float32)
        keep = jax.random.uniform(k6, (B, SQ, SKV)) >= DROP_P
        drop_mask = keep.astype(jnp.float32) / (1.0 - DROP_P)
        return {'q1': q1, 'key': k_, 'value': v_, 'weights': weights, 'bias': bias, 'drop_mask': drop_mask}
    _L0_xattn_all = _L0_xattn_setup()
    _L0_xattn_in = {k: v for k, v in _L0_xattn_all.items() if k in ('weights', 'bias')}
    del _L0_xattn_all

    def _L0_attn_setup():
        import jax, jax.numpy as jnp
        import numpy as np
        HEADS = 16
        key = jax.random.key(seed)
        ks = jax.random.split(key, 6)
        b, n, c = (4, 512, 256)
        h = 256
        s = 0.02
        return {'x': jax.random.normal(ks[0], (b, n, c), jnp.float32), 'Wq': jax.random.normal(ks[1], (h, c), jnp.float32) * s, 'Wk': jax.random.normal(ks[2], (h, c), jnp.float32) * s, 'Wv': jax.random.normal(ks[3], (h, c), jnp.float32) * s, 'Wout': jax.random.normal(ks[4], (c, h), jnp.float32) * s, 'bout': jnp.zeros((c,), jnp.float32)}
    _L0_attn_all = _L0_attn_setup()
    _L0_attn_in = {k: v for k, v in _L0_attn_all.items() if k in ('Wq', 'Wk', 'Wv', 'Wout', 'bout')}
    del _L0_attn_all

    def _L0_ffn_setup():
        import jax, jax.numpy as jnp
        import numpy as np
        B, L, D = (1, 512, 256)
        E, H, G, K = (64, 64, 64, 16)

        def _grouped_routing_scores(router_scores):
            T, En = router_scores.shape
            Tq = T // G
            budget = Tq * K
            order = jnp.argsort(-router_scores, axis=0)
            sorted_vals = jnp.take_along_axis(router_scores, order, axis=0)
            group_score = sorted_vals.reshape(Tq, G, En).sum(axis=1)
            _, top_flat = jax.lax.top_k(group_score.reshape(-1), budget)
            gmask = jnp.zeros((Tq * En,), bool).at[top_flat].set(True).reshape(Tq, En)
            mask_sorted = jnp.broadcast_to(gmask[:, None, :], (Tq, G, En)).reshape(T, En)
            mask = jnp.zeros((T, En), bool).at[order, jnp.arange(En)[None, :]].set(mask_sorted)
            fs = jnp.where(mask, router_scores, 0.0)
            return fs / (fs.sum(axis=-1, keepdims=True) + 1e-06)
        key = jax.random.key(seed)
        ks = jax.random.split(key, 6)
        s = lambda k, shape, scale: jax.random.normal(k, shape, jnp.float32) * scale
        return {'x': jax.random.normal(ks[0], (B, L, D), jnp.float32), 'Wr': s(ks[1], (D, E), D ** (-0.5)), 'br': jnp.zeros((E,), jnp.float32), 'Wup': s(ks[2], (E, D, H), D ** (-0.5)), 'bup': jnp.zeros((E, H), jnp.float32), 'Wgate': s(ks[3], (E, D, H), D ** (-0.5)), 'bgate': jnp.zeros((E, H), jnp.float32), 'Wdown': s(ks[4], (E, H, D), H ** (-0.5)), 'bdown': jnp.zeros((E, D), jnp.float32)}
    _L0_ffn_all = _L0_ffn_setup()
    _L0_ffn_in = {k: v for k, v in _L0_ffn_all.items() if k in ('Wr', 'br', 'Wup', 'bup', 'Wgate', 'bgate', 'Wdown', 'bdown')}
    del _L0_ffn_all
    return {'x': x, 'ctx_1024': ctx_1024, 'mask_BxSxS2_fk0': mask_BxSxS2_fk0, 'L0_xattn_weights': _L0_xattn_in['weights'], 'L0_xattn_bias': _L0_xattn_in['bias'], 'L0_attn_Wq': _L0_attn_in['Wq'], 'L0_attn_Wk': _L0_attn_in['Wk'], 'L0_attn_Wv': _L0_attn_in['Wv'], 'L0_attn_Wout': _L0_attn_in['Wout'], 'L0_attn_bout': _L0_attn_in['bout'], 'L0_ffn_Wr': _L0_ffn_in['Wr'], 'L0_ffn_br': _L0_ffn_in['br'], 'L0_ffn_Wup': _L0_ffn_in['Wup'], 'L0_ffn_bup': _L0_ffn_in['bup'], 'L0_ffn_Wgate': _L0_ffn_in['Wgate'], 'L0_ffn_bgate': _L0_ffn_in['bgate'], 'L0_ffn_Wdown': _L0_ffn_in['Wdown'], 'L0_ffn_bdown': _L0_ffn_in['bdown']}

def reference(x, ctx_1024, mask_BxSxS2_fk0, L0_xattn_weights, L0_xattn_bias, L0_attn_Wq, L0_attn_Wk, L0_attn_Wv, L0_attn_Wout, L0_attn_bout, L0_ffn_Wr, L0_ffn_br, L0_ffn_Wup, L0_ffn_bup, L0_ffn_Wgate, L0_ffn_bgate, L0_ffn_Wdown, L0_ffn_bdown):
    import jax
    import jax.numpy as jnp

    def _L0_xattn_ref(q1, key, value, weights, bias, drop_mask):
        import jax, jax.numpy as jnp
        import numpy as np
        B, SQ, SKV, D = (8, 512, 512, 256)
        DROP_P = 0.3
        scores = jnp.einsum('bqd,bkd->bqk', q1, key) / 0.72
        attn = jax.nn.softmax(scores, axis=-1) * drop_mask
        o = jnp.einsum('bqk,bkd->bqd', attn, value) + bias
        return jnp.einsum('bqd,de->bqe', o, weights)

    def _L0_attn_ref(x, Wq, Wk, Wv, Wout, bout):
        import jax, jax.numpy as jnp
        import numpy as np
        HEADS = 16
        b, n, c = x.shape
        m = HEADS
        d = Wq.shape[0] // m
        q = jnp.einsum('bnc,hc->bnh', x, Wq).reshape(b, n, m, d)
        k = jnp.einsum('bnc,hc->bnh', x, Wk).reshape(b, n, m, d)
        v = jnp.einsum('bnc,hc->bnh', x, Wv).reshape(b, n, m, d)
        scale = d ** (-0.25)
        weight = jnp.einsum('bimd,bjmd->bmij', q * scale, k * scale)
        weight = jax.nn.softmax(weight, axis=-1)
        a = jnp.einsum('bmij,bjmd->bimd', weight, v).reshape(b, n, m * d)
        return jnp.einsum('bnh,ch->bnc', a, Wout) + bout

    def _L0_ffn_ref(x, Wr, br, Wup, bup, Wgate, bgate, Wdown, bdown):
        import jax, jax.numpy as jnp
        import numpy as np
        B, L, D = (1, 512, 256)
        E, H, G, K = (64, 64, 64, 16)

        def _grouped_routing_scores(router_scores):
            T, En = router_scores.shape
            Tq = T // G
            budget = Tq * K
            order = jnp.argsort(-router_scores, axis=0)
            sorted_vals = jnp.take_along_axis(router_scores, order, axis=0)
            group_score = sorted_vals.reshape(Tq, G, En).sum(axis=1)
            _, top_flat = jax.lax.top_k(group_score.reshape(-1), budget)
            gmask = jnp.zeros((Tq * En,), bool).at[top_flat].set(True).reshape(Tq, En)
            mask_sorted = jnp.broadcast_to(gmask[:, None, :], (Tq, G, En)).reshape(T, En)
            mask = jnp.zeros((T, En), bool).at[order, jnp.arange(En)[None, :]].set(mask_sorted)
            fs = jnp.where(mask, router_scores, 0.0)
            return fs / (fs.sum(axis=-1, keepdims=True) + 1e-06)
        Bx, Lx, Dx = x.shape
        xt = x.reshape(-1, Dx)
        router_scores = jax.nn.softmax(xt @ Wr + br, axis=-1)
        fs = _grouped_routing_scores(router_scores)
        up = jnp.einsum('td,edh->teh', xt, Wup) + bup
        gate = jnp.einsum('td,edh->teh', xt, Wgate) + bgate
        h = jax.nn.silu(up) * gate * fs[:, :, None]
        out = jnp.einsum('teh,ehd->td', h, Wdown) + fs @ bdown
        return out.reshape(Bx, Lx, Dx)
    x = x + _L0_xattn_ref(_layernorm(x, axis=-1), ctx_1024, ctx_1024, L0_xattn_weights, L0_xattn_bias, mask_BxSxS2_fk0)
    x = x + _L0_attn_ref(_layernorm(x, axis=-1), L0_attn_Wq, L0_attn_Wk, L0_attn_Wv, L0_attn_Wout, L0_attn_bout)
    x = x + _L0_ffn_ref(_layernorm(x, axis=-1), L0_ffn_Wr, L0_ffn_br, L0_ffn_Wup, L0_ffn_bup, L0_ffn_Wgate, L0_ffn_bgate, L0_ffn_Wdown, L0_ffn_bdown)
    return x

_drawn_inputs = setup_inputs


def setup_inputs(seed=0):
    import zlib

    import numpy as np

    out = dict(_drawn_inputs(seed))
    spreads = {'L0_attn_bout': (0.0, 0.8),
     'L0_ffn_br': (0.0, 0.8),
     'L0_ffn_bup': (0.0, 0.8),
     'L0_ffn_bgate': (0.0, 0.8),
     'L0_ffn_bdown': (0.0, 0.8)}
    factors = {'L0_attn_Wq': 8.0,
     'L0_attn_Wk': 8.0,
     'L0_attn_Wv': 8.0,
     'L0_attn_Wout': 8.0,
     'L0_ffn_Wr': 8.0,
     'L0_ffn_Wup': 8.0,
     'L0_ffn_Wgate': 8.0,
     'L0_ffn_Wdown': 8.0}
    for name, (base, spread) in spreads.items():
        noise = np.random.default_rng([zlib.crc32(name.encode()), seed]).standard_normal(out[name].shape)
        drawn = base * np.exp(spread * noise) if base else spread * noise
        out[name] = jnp.asarray(drawn.astype(out[name].dtype))
    for name, factor in factors.items():
        out[name] = (out[name] * factor).astype(out[name].dtype)
    return out
```

```python
from contextlib import ExitStack

import concourse.bass as bass
from concourse import mybir

F32 = mybir.dt.float32
F32R = mybir.dt.float32r
ALU = mybir.AluOpType
ACT = mybir.ActivationFunctionType
AX = mybir.AxisListType

P = 128
BANK = 512
EPS = 1e-5


def wait(eng, sem, n):
    if isinstance(n, int) and n <= 0:
        return
    eng.wait_ge(sem, n)


def ln_transpose(nc, X, XNT, ident, tag, split=None):
    NT, D = X.shape[1], X.shape[2]
    DC = D // P
    with ExitStack() as ctx:
        def sb(name, shape, dt=F32):
            return ctx.enter_context(nc.sbuf_tensor(f"{tag}_{name}", shape, dt))

        def sem(name):
            return ctx.enter_context(nc.semaphore(f"{tag}_{name}"))

        stats = sb("stats", [P, NT, 6])
        mv = sb("mv", [P, NT, 2])
        vare = sb("vare", [P, NT])
        std = sb("std", [P, NT])
        rstd = sb("rstd", [P, NT])
        newt = sb("newt", [P, NT])
        XN = sb("XN", [P, NT, D])
        psT = [[ctx.enter_context(nc.psum_tensor(f"{tag}_psT{k}_{c}", [P, 2 * P], F32)) for c in range(DC)]
               for k in range(NT // 2)]

        stats_done = sem("stats_done")
        mv_done = sem("mv_done")
        vare_done = sem("vare_done")
        std_done = sem("std_done")
        newton = sem("newton")
        xn_done = sem("xn_done")
        transposed = sem("transposed")
        hi_done = sem("hi_done")

        block = ctx.enter_context(nc.Block())

        @block.vector
        def _(dve):
            for t in range(NT):
                nc.vector.bn_stats(stats[:, t, :], X[:, t, :]).then_inc(stats_done, 1)
            for t in range(NT):
                dve.wait_ge(stats_done, t + 1)
                nc.vector.bn_aggr(mv[:, t, :], stats[:, t, :]).then_inc(mv_done, 1)
            dve.wait_ge(mv_done, NT)
            nc.vector.tensor_scalar(vare[:], mv[:, :, 1], EPS, None, ALU.add).then_inc(vare_done, 1)
            dve.wait_ge(std_done, 1)
            nc.vector.reciprocal(rstd[:], std[:]).then_inc(newton, 1)
            dve.wait_ge(newton, 1)
            nc.vector.tensor_tensor(newt[:], rstd[:], rstd[:], ALU.mult).then_inc(newton, 1)
            dve.wait_ge(newton, 2)
            nc.vector.tensor_tensor(newt[:], newt[:], vare[:], ALU.mult).then_inc(newton, 1)
            dve.wait_ge(newton, 3)
            nc.vector.tensor_scalar(newt[:], newt[:], -0.5, 1.5, ALU.mult, ALU.add).then_inc(newton, 1)
            dve.wait_ge(newton, 4)
            nc.vector.tensor_tensor(rstd[:], rstd[:], newt[:], ALU.mult).then_inc(newton, 1)
            dve.wait_ge(newton, 5)
            for t in range(NT):
                nc.vector.tensor_scalar(XN[:, t, :], X[:, t, :], mv[:, t, 0:1], rstd[:, t:t + 1],
                                        ALU.subtract, ALU.mult).then_inc(xn_done, 1)
            for k in range(NT // 2):
                for c in range(DC):
                    cols = slice(2 * k * P, 2 * (k + 1) * P)
                    if split is not None:
                        dve.wait_ge(hi_done, DC * k + c + 1)
                        nc.vector.tensor_tensor(split[1][:, c, cols], psT[k][c][:], split[0][:, c, cols].bitcast(F32),
                                                ALU.subtract)
                    elif c == 1:
                        dve.wait_ge(transposed, 2 * (k + 1))
                        nc.vector.tensor_copy(XNT[:, c, cols], psT[k][c][:])

        @block.scalar
        def _(act):
            act.wait_ge(vare_done, 1)
            nc.scalar.activation(std[:], vare[:], ACT.Sqrt).then_inc(std_done, 1)
            for k in range(NT // 2):
                act.wait_ge(transposed, 2 * (k + 1))
                for c in range(DC):
                    cols = slice(2 * k * P, 2 * (k + 1) * P)
                    if split is not None:
                        nc.scalar.activation(split[0][:, c, cols], psT[k][c][:], ACT.Copy).then_inc(hi_done, 1)
                    elif c == 0:
                        nc.scalar.activation(XNT[:, c, cols], psT[k][c][:], ACT.Copy)

        @block.tensor
        def _(pe):
            for t in range(NT):
                pe.wait_ge(xn_done, t + 1)
                for c in range(DC):
                    last = nc.tensor.transpose(psT[t // 2][c][:, (t % 2) * P:(t % 2 + 1) * P], XN[:, t, c * P:(c + 1) * P], ident[:])
                last.then_inc(transposed, 1)


def project_add(nc, X, A, w_dram, bias_dram, ident, tag):
    NT, D = X.shape[1], X.shape[2]
    DC = D // P
    with ExitStack() as ctx:
        def sb(name, shape, dt=F32):
            return ctx.enter_context(nc.sbuf_tensor(f"{tag}_{name}", shape, dt))

        def sem(name):
            return ctx.enter_context(nc.semaphore(f"{tag}_{name}"))

        w_raw = sb("w_raw", [P, DC, D])
        w_hi = sb("w_hi", [P, DC, D], F32R)
        w_lo = sb("w_lo", [P, DC, D], F32R)
        at_hi = sb("at_hi", [P, 2, DC, P], F32R)
        at_lo = sb("at_lo", [P, 2, DC, P], F32R)
        bias = sb("bias", [P, D])
        psT = [ctx.enter_context(nc.psum_tensor(f"{tag}_psT{k}", [P, DC, P], F32)) for k in range(2)]
        psO = [ctx.enter_context(nc.psum_tensor(f"{tag}_psO{k}", [P, BANK], F32)) for k in range(2)]

        w_in = sem("w_in")
        bias_in = sem("bias_in")
        whi_done = sem("whi_done")
        wlo_done = sem("wlo_done")
        transposed = sem("transposed")
        athi_done = sem("athi_done")
        atlo_done = sem("atlo_done")
        product_done = sem("product_done")
        bias_added = sem("bias_added")
        added = sem("added")

        block = ctx.enter_context(nc.Block())

        @block.sync
        def _(sp):
            sp.dma_start(w_raw[:], w_dram.rearrange("(c p) n -> p c n", p=P)).then_inc(w_in, 16)
            if bias_dram is not None:
                sp.dma_start(bias[:], bias_dram.rearrange("(a n) -> a n", a=1).to_broadcast([P, D])).then_inc(bias_in, 16)

        @block.scalar
        def _(act):
            act.wait_ge(w_in, 16)
            nc.scalar.activation(w_hi[:], w_raw[:], ACT.Copy).then_inc(whi_done, 1)
            for t in range(NT):
                act.wait_ge(transposed, t + 1)
                if t >= 2:
                    act.wait_ge(product_done, t - 1)
                nc.scalar.activation(at_hi[:, t % 2], psT[t % 2][:], ACT.Copy).then_inc(athi_done, 1)

        @block.vector
        def _(dve):
            if bias_dram is not None:
                dve.wait_ge(bias_in, 16)
                for t in range(NT):
                    nc.vector.tensor_tensor(X[:, t, :], X[:, t, :], bias[:], ALU.add).then_inc(bias_added, 1)
            dve.wait_ge(whi_done, 1)
            nc.vector.tensor_tensor(w_lo[:], w_raw[:], w_hi[:].bitcast(F32), ALU.subtract).then_inc(wlo_done, 1)
            for t in range(NT + 1):
                if t < NT:
                    dve.wait_ge(athi_done, t + 1)
                    nc.vector.tensor_tensor(at_lo[:, t % 2], psT[t % 2][:], at_hi[:, t % 2].bitcast(F32),
                                            ALU.subtract).then_inc(atlo_done, 1)
                if t >= 1:
                    u = t - 1
                    dve.wait_ge(product_done, u + 1)
                    if bias_dram is not None:
                        dve.wait_ge(bias_added, u + 1)
                    nc.vector.tensor_tensor(X[:, u, :], psO[u % 2][:, 0:D], X[:, u, :], ALU.add).then_inc(added, 1)

        @block.tensor
        def _(pe):
            for t in range(NT + 1):
                if t < NT:
                    if t >= 2:
                        pe.wait_ge(atlo_done, t - 1)
                    for c in range(DC):
                        last = nc.tensor.transpose(psT[t % 2][:, c, :], A[:, t, c * P:(c + 1) * P], ident[:])
                    last.then_inc(transposed, 1)
                if t >= 1:
                    u = t - 1
                    pe.wait_ge(atlo_done, u + 1)
                    if u == 0:
                        pe.wait_ge(wlo_done, 1)
                    if u >= 2:
                        pe.wait_ge(added, u - 1)
                    n = 0
                    for a, w in ((at_hi, w_hi), (at_hi, w_lo), (at_lo, w_hi)):
                        for c in range(DC):
                            last = nc.tensor.matmul(psO[u % 2][:, 0:D], a[:, u % 2, c, :], w[:, c, :],
                                                    start=(n == 0), stop=(n == 3 * DC - 1))
                            n += 1
                    last.then_inc(product_done, 1)


def cross_attention(nc, XNT, ctxT_dram, ctx_dram, mask_dram, bias_dram, ident, O):
    TEMP = 0.72
    B, D, SK = ctxT_dram.shape
    DC = D // P
    KB = BANK
    NJ = SK // KB
    KC = KB // P
    NQ = mask_dram.shape[1] // P

    ctxT_v = ctxT_dram.rearrange("b (c p) k -> b p c k", p=P)
    ctx_v = ctx_dram.rearrange("b (j c p) d -> b j p c d", p=P, c=KC)
    mask_v = mask_dram.rearrange("b (q p) k -> b p q k", p=P)

    with ExitStack() as ctx:
        def sb(name, shape, dt=F32):
            return ctx.enter_context(nc.sbuf_tensor(f"xa_{name}", shape, dt))

        def ps(name, shape):
            return ctx.enter_context(nc.psum_tensor(f"xa_{name}", shape, F32))

        def sem(name):
            return ctx.enter_context(nc.semaphore(f"xa_{name}"))

        keysT_raw = sb("keysT_raw", [P, 2, DC, KB])
        keysT_hi = sb("keysT_hi", [P, 2, DC, KB], F32R)
        keysT_lo = sb("keysT_lo", [P, 2, DC, KB], F32R)
        vals_raw = sb("vals_raw", [P, 2, KC, D])
        vals = sb("vals", [P, 2, KC, 2, D], F32R)
        mask = sb("mask", [P, 2, NQ, KB])
        S = sb("S", [P, NJ, NQ, KB])
        probs = sb("probs", [P, 2, NQ, KB])
        pT_hi = sb("pT_hi", [P, NQ, KC, P], F32R)
        pT_lo = sb("pT_lo", [P, NQ, KC, P], F32R)
        q_hi = sb("q_hi", [P, DC, NQ * P], F32R)
        q_lo = sb("q_lo", [P, DC, NQ * P], F32R)
        bias = sb("bias", [P, D])
        blockmax = sb("blockmax", [P, NQ, NJ])
        rowmax = sb("rowmax", [P, NQ])
        expbias = sb("expbias", [P, NQ])
        blocksum = sb("blocksum", [P, NQ, NJ])
        rowsum = sb("rowsum", [P, NQ])
        rinv = sb("rinv", [P, NQ])
        olo = sb("olo", [P, NQ, D])
        psS = [ps(f"psS{q}", [P, KB]) for q in range(NQ)]
        psP = [ps(f"psP{q}", [P, KC, P]) for q in range(NQ)]
        psO = [ps(f"psO{q}", [P, 2 * D]) for q in range(NQ)]

        keysT_in = [sem(f"keysT_in{s}") for s in range(2)]
        vals_in = [sem(f"vals_in{s}") for s in range(2)]
        mask_in = [sem(f"mask_in{s}") for s in range(2)]
        bias_in = sem("bias_in")
        khi_done = sem("khi_done")
        klo_done = sem("klo_done")
        vhi_done = sem("vhi_done")
        vlo_done = sem("vlo_done")
        qhi_done = sem("qhi_done")
        qlo_done = sem("qlo_done")
        scores_done = sem("scores_done")
        scores_saved = sem("scores_saved")
        rowmax_done = sem("rowmax_done")
        expbias_done = sem("expbias_done")
        exp_done = sem("exp_done")
        masked = sem("masked")
        pT_done = sem("pT_done")
        phi_done = sem("phi_done")
        plo_done = sem("plo_done")
        pv_done = sem("pv_done")
        rowsum_done = sem("rowsum_done")
        rinv_done = sem("rinv_done")
        olo_done = sem("olo_done")
        o_done = sem("o_done")

        def blocks(b, j):
            return NJ * b + j + 1

        def tiles(b, j, q):
            return NQ * (NJ * b + j) + q + 1

        def slot_loads(b, j):
            return 16 * ((NJ // 2) * b + j // 2 + 1)

        def turns(eng, turn):
            turn(0, True, False)
            turn(1, True, True)
            with eng.Fori(2, B) as i:
                turn(i, True, True)
            turn(B, False, True)

        block = ctx.enter_context(nc.Block())

        @block.sync
        def _(sp):
            sp.dma_start(bias[:], bias_dram.rearrange("(a n) -> a n", a=1).to_broadcast([P, D])).then_inc(bias_in, 16)

            def turn(i, scoring, weighing):
                for j in range(NJ):
                    if scoring:
                        wait(sp, khi_done, blocks(i, j - 2))
                        wait(sp, klo_done, blocks(i, j - 2))
                        sp.dma_start(keysT_raw[:, j % 2], ctxT_v[i, :, :, j * KB:(j + 1) * KB]).then_inc(keysT_in[j % 2], 16)
                    if weighing:
                        wait(sp, vhi_done, blocks(i - 1, j - 2))
                        wait(sp, vlo_done, blocks(i - 1, j - 2))
                        sp.dma_start(vals_raw[:, j % 2], ctx_v[i - 1, j]).then_inc(vals_in[j % 2], 16)
                        wait(sp, masked, tiles(i - 1, j - 2, NQ - 1))
                        sp.dma_start(mask[:, j % 2], mask_v[i - 1, :, :, j * KB:(j + 1) * KB]).then_inc(mask_in[j % 2], 16)
            turns(sp, turn)

        @block.scalar
        def _(act):
            def split_queries(b):
                wait(act, scores_done, tiles(b, -1, NQ - 1))
                nc.scalar.activation(q_hi[:], XNT[:, :, bass.ds(b * (NQ * P), NQ * P)], ACT.Copy).then_inc(qhi_done, 1)

            def split_keys(b, j):
                act.wait_ge(keysT_in[j % 2], slot_loads(b, j))
                wait(act, scores_done, tiles(b, j - 2, NQ - 1))
                nc.scalar.activation(keysT_hi[:, j % 2], keysT_raw[:, j % 2], ACT.Copy).then_inc(khi_done, 1)

            def split_values(b, j):
                act.wait_ge(vals_in[j % 2], slot_loads(b, j))
                wait(act, pv_done, tiles(b, j - 2, NQ - 1))
                nc.scalar.activation(vals[:, j % 2, :, 0, :], vals_raw[:, j % 2], ACT.Copy).then_inc(vhi_done, 1)

            def exponentials(b, j):
                if j == 0:
                    act.wait_ge(expbias_done, b + 1)
                    wait(act, rowsum_done, b)
                wait(act, pT_done, tiles(b, j - 2, NQ - 1))
                for q in range(NQ):
                    nc.scalar.activation(probs[:, j % 2, q, :], S[:, j, q, :], ACT.Exp, bias=expbias[:, q:q + 1],
                                         scale=1.0 / TEMP, accum_out=blocksum[:, q, j:j + 1]).then_inc(exp_done, 1)

            def split_probs(b, j):
                for q in range(NQ):
                    act.wait_ge(pT_done, tiles(b, j, q))
                    wait(act, pv_done, tiles(b, j - 1, q))
                    nc.scalar.activation(pT_hi[:, q], psP[q][:], ACT.Copy).then_inc(phi_done, 1)

            def turn(i, scoring, weighing):
                if scoring:
                    split_queries(i)
                    split_keys(i, 0)
                if weighing:
                    exponentials(i - 1, 0)
                    split_values(i - 1, 0)
                for j in range(NJ):
                    if weighing:
                        if j + 1 < NJ:
                            exponentials(i - 1, j + 1)
                        split_probs(i - 1, j)
                    if j + 1 < NJ:
                        if scoring:
                            split_keys(i, j + 1)
                        if weighing:
                            split_values(i - 1, j + 1)
            turns(act, turn)

        @block.vector
        def _(dve):
            def split_queries(b):
                dve.wait_ge(qhi_done, b + 1)
                nc.vector.tensor_tensor(q_lo[:], XNT[:, :, bass.ds(b * (NQ * P), NQ * P)], q_hi[:].bitcast(F32),
                                        ALU.subtract).then_inc(qlo_done, 1)

            def split_keys(b, j):
                dve.wait_ge(khi_done, blocks(b, j))
                nc.vector.tensor_tensor(keysT_lo[:, j % 2], keysT_raw[:, j % 2], keysT_hi[:, j % 2].bitcast(F32),
                                        ALU.subtract).then_inc(klo_done, 1)

            def split_probs(b, j):
                for q in range(NQ):
                    dve.wait_ge(phi_done, tiles(b, j, q))
                    nc.vector.tensor_tensor(pT_lo[:, q], psP[q][:], pT_hi[:, q].bitcast(F32),
                                            ALU.subtract).then_inc(plo_done, 1)

            def save_scores(b, j):
                for q in range(NQ):
                    dve.wait_ge(scores_done, tiles(b, j, q))
                    wait(dve, exp_done, tiles(b - 1, j, q))
                    nc.vector.tensor_scalar(S[:, j, q, :], psS[q][:], 1.0, None, ALU.mult, ALU.max,
                                            accum_out=blockmax[:, q, j:j + 1]).then_inc(scores_saved, 1)

            def row_maximum(b):
                dve.wait_ge(scores_saved, tiles(b, NJ - 1, NQ - 1))
                nc.vector.tensor_reduce(rowmax[:], blockmax[:], AX.X, ALU.max).then_inc(rowmax_done, 1)
                dve.wait_ge(rowmax_done, b + 1)
                wait(dve, exp_done, tiles(b, -1, NQ - 1))
                nc.vector.tensor_scalar(expbias[:], rowmax[:], -1.0 / TEMP, None, ALU.mult).then_inc(expbias_done, 1)

            def row_sums(b):
                dve.wait_ge(exp_done, tiles(b, NJ - 1, NQ - 1))
                nc.vector.tensor_reduce(rowsum[:], blocksum[:], AX.X, ALU.add).then_inc(rowsum_done, 1)
                dve.wait_ge(rowsum_done, b + 1)
                nc.vector.reciprocal(rinv[:], rowsum[:]).then_inc(rinv_done, 1)

            def outputs(b):
                dve.wait_ge(rinv_done, b + 1)
                for q in range(NQ):
                    dve.wait_ge(pv_done, tiles(b, NJ - 1, q))
                    nc.vector.scalar_tensor_tensor(olo[:, q], psO[q][:, D:2 * D], rinv[:, q:q + 1], bias[:],
                                                   ALU.mult, ALU.add).then_inc(olo_done, 1)
                for q in range(NQ):
                    dve.wait_ge(olo_done, NQ * b + q + 1)
                    nc.vector.scalar_tensor_tensor(O[:, bass.ds(b * NQ + q, 1), :].rearrange("p a d -> p (a d)"),
                                                   psO[q][:, 0:D], rinv[:, q:q + 1], olo[:, q],
                                                   ALU.mult, ALU.add).then_inc(o_done, 1)

            dve.wait_ge(bias_in, 16)

            def turn(i, scoring, weighing):
                if scoring:
                    split_queries(i)
                    split_keys(i, 0)
                for j in range(NJ):
                    if weighing:
                        split_probs(i - 1, j)
                    if scoring:
                        save_scores(i, j)
                        if j + 1 < NJ:
                            split_keys(i, j + 1)
                    if weighing and j == NJ - 2:
                        row_sums(i - 1)
                if scoring:
                    row_maximum(i)
                if weighing:
                    outputs(i - 1)
            turns(dve, turn)

        @block.gpsimd
        def _(pool):
            def apply_mask(b, j):
                pool.wait_ge(mask_in[j % 2], slot_loads(b, j))
                for q in range(NQ):
                    pool.wait_ge(exp_done, tiles(b, j, q))
                    nc.gpsimd.tensor_tensor(probs[:, j % 2, q, :], probs[:, j % 2, q, :], mask[:, j % 2, q, :],
                                            ALU.mult).then_inc(masked, 1)

            def split_values(b, j):
                pool.wait_ge(vhi_done, blocks(b, j))
                nc.gpsimd.tensor_tensor(vals[:, j % 2, :, 1, :], vals_raw[:, j % 2],
                                        vals[:, j % 2, :, 0, :].bitcast(F32), ALU.subtract).then_inc(vlo_done, 1)

            def turn(i, scoring, weighing):
                if weighing:
                    for j in range(NJ):
                        apply_mask(i - 1, j)
                        split_values(i - 1, j)
            turns(pool, turn)

        @block.tensor
        def _(pe):
            def transpose_probs(b, j):
                for q in range(NQ):
                    pe.wait_ge(masked, tiles(b, j, q))
                    wait(pe, phi_done, tiles(b, j - 1, q))
                    wait(pe, plo_done, tiles(b, j - 1, q))
                    for c in range(KC):
                        last = nc.tensor.transpose(psP[q][:, c, :], probs[:, j % 2, q, c * P:(c + 1) * P], ident[:])
                    last.then_inc(pT_done, 1)

            def scores(b, j):
                if j == 0:
                    pe.wait_ge(qlo_done, b + 1)
                pe.wait_ge(klo_done, blocks(b, j))
                for q in range(NQ):
                    wait(pe, scores_saved, tiles(b, j - 1, q))
                    n = 0
                    for a, k in ((q_hi, keysT_hi), (q_lo, keysT_hi), (q_hi, keysT_lo)):
                        for c in range(DC):
                            last = nc.tensor.matmul(psS[q][:], a[:, c, q * P:(q + 1) * P], k[:, j % 2, c, :],
                                                    start=(n == 0), stop=(n == 3 * DC - 1))
                            n += 1
                    last.then_inc(scores_done, 1)

            def weigh(b, j):
                pe.wait_ge(vlo_done, blocks(b, j))
                for q in range(NQ):
                    pe.wait_ge(plo_done, tiles(b, j, q))
                    if j == 0:
                        wait(pe, o_done, NQ * b)
                    for c in range(KC):
                        wide_first = j == 0 and c == 0
                        for wide in ((True, False) if wide_first else (False, True)):
                            if wide:
                                last = nc.tensor.matmul(psO[q][:], pT_hi[:, q, c, :], vals[:, j % 2, c, :, :],
                                                        start=wide_first, stop=(j == NJ - 1 and c == KC - 1),
                                                        skip_group_check=True)
                            else:
                                last = nc.tensor.matmul(psO[q][:, 0:D], pT_lo[:, q, c, :], vals[:, j % 2, c, 0, :],
                                                        start=False, stop=False, skip_group_check=True)
                    last.then_inc(pv_done, 1)

            def turn(i, scoring, weighing):
                for j in range(NJ):
                    if weighing:
                        transpose_probs(i - 1, j)
                    if scoring:
                        scores(i, j)
                    if weighing:
                        weigh(i - 1, j)
            turns(pe, turn)


def self_attention(nc, XNT, wqkv_dram, pick_dram, ident, O):
    HEADS, DH = 16, 16
    DC = XNT.shape[1]
    D = DC * P
    SQ = 2 * P
    NQ = SQ // P
    B = XNT.shape[2] // SQ
    PAIRS = HEADS // 2
    ROWS = 4 * DH
    SCALE = float(DH) ** -0.5
    RING = 3
    with ExitStack() as ctx:
        def sb(name, shape, dt=F32):
            return ctx.enter_context(nc.sbuf_tensor(f"sa_{name}", shape, dt))

        def sem(name):
            return ctx.enter_context(nc.semaphore(f"sa_{name}"))

        w_raw = sb("w_raw", [P, DC, 3 * D])
        w_hi = sb("w_hi", [P, DC, 3 * D], F32R)
        w_lo = sb("w_lo", [P, DC, 3 * D], F32R)
        pick = sb("pick", [P, HEADS])
        sel = sb("sel", [P, HEADS, P], F32R)
        identr = sb("identr", [P, P], F32R)
        x_hi = sb("x_hi", [P, DC, SQ], F32R)
        x_lo = sb("x_lo", [P, DC, SQ], F32R)
        q4 = sb("q4", [P, NQ, HEADS, 4, DH], F32R)
        k4 = sb("k4", [P, NQ, HEADS, 4, DH], F32R)
        v4 = sb("v4", [P, NQ, HEADS, ROWS], F32R)
        qz = sb("qz", [P, HEADS, SQ], F32R)
        kT = sb("kT", [P, PAIRS, SQ], F32R)
        negmax = sb("negmax", [P, NQ, HEADS])
        one = sb("one", [P, 1, 1])
        mz = sb("mz", [P, NQ, P], F32R)
        mT = sb("mT", [P, SQ], F32R)
        probs = sb("probs", [P, RING, NQ, SQ])
        p_hi = sb("p_hi", [P, RING, NQ, SQ], F32R)
        p_lo = sb("p_lo", [P, RING, NQ, SQ], F32R)
        aT = sb("aT", [P, 2, SQ])
        rinv = sb("rinv", [P, 2, HEADS // 2])
        num = sb("num", [P, 2, HEADS // 2, DH])

        bank = [ctx.enter_context(nc.psum_tensor(f"sa_bank{k}", [P, BANK], F32)) for k in range(8)]
        psQK, psV, psT, psM = bank[0:2], bank[2], bank[3:5], bank[2]
        psS, psO, psB, psE = bank[0:2], bank[3:5], bank[0:2], bank[5:8]

        w_in = sem("w_in")
        pick_in = sem("pick_in")
        whi_done = sem("whi_done")
        wlo_done = sem("wlo_done")
        constants = sem("constants")
        one_done = sem("one_done")
        xhi_done = sem("xhi_done")
        xlo_done = sem("xlo_done")
        qk_done = sem("qk_done")
        v_done = sem("v_done")
        qkhi_done = sem("qkhi_done")
        qklo_done = sem("qklo_done")
        vhi_done = sem("vhi_done")
        vlo_done = sem("vlo_done")
        turned = sem("turned")
        kT_done = sem("kT_done")
        qz_done = sem("qz_done")
        smax_done = sem("smax_done")
        max_done = sem("max_done")
        mhi_done = sem("mhi_done")
        mlo_done = sem("mlo_done")
        m_turned = sem("m_turned")
        mT_done = sem("mT_done")
        st_done = sem("st_done")
        exp_done = sem("exp_done")
        phi_done = sem("phi_done")
        plo_done = sem("plo_done")
        pv_done = sem("pv_done")
        aT_done = sem("aT_done")
        back_done = sem("back_done")
        rinv_done = sem("rinv_done")
        num_done = sem("num_done")
        norm_done = sem("norm_done")

        def turns(eng, turn):
            turn(0)
            with eng.Fori(1, B) as b:
                turn(b)

        def ring_free(b, h):
            return HEADS * b + (h + 1 - RING if h >= RING else 0)

        PV_LAG = 3
        COPY_LAG = PV_LAG + 2
        BACK_LAG = PV_LAG + 3
        SLOTS = 2 * (PAIRS - 1) + BACK_LAG + 1
        GROUP = PAIRS // 2

        block = ctx.enter_context(nc.Block())

        @block.sync
        def _(sp):
            sp.dma_start(w_raw[:], wqkv_dram.rearrange("(c p) n -> p c n", p=P)).then_inc(w_in, 16)
            sp.dma_start(pick[:], pick_dram).then_inc(pick_in, 16)

        @block.gpsimd
        def _(pool):
            nc.gpsimd.memset(qz[:].bitcast(F32), 0.0).then_inc(constants, 1)
            nc.gpsimd.memset(mz[:].bitcast(F32), 0.0).then_inc(constants, 1)
            nc.gpsimd.memset(one[:], 1.0).then_inc(one_done, 1)
            pool.wait_ge(one_done, 1)

            def turn(b):
                for h in range(HEADS):
                    r = h % RING
                    pool.wait_ge(exp_done, HEADS * b + h + 1)
                    wait(pool, pv_done, ring_free(b, h))
                    nc.gpsimd.tensor_tensor(p_hi[:, r], probs[:, r], one[:].to_broadcast([P, NQ, SQ]), ALU.mult).then_inc(phi_done, 1)
            turns(pool, turn)

        @block.scalar
        def _(act):
            act.wait_ge(w_in, 16)
            nc.scalar.activation(w_hi[:], w_raw[:], ACT.Copy).then_inc(whi_done, 1)

            def turn(b):
                wait(act, qk_done, NQ * b)
                wait(act, v_done, b)
                nc.scalar.activation(x_hi[:], XNT[:, :, bass.ds(b * SQ, SQ)], ACT.Copy).then_inc(xhi_done, 1)
                for t in range(NQ):
                    act.wait_ge(qk_done, NQ * b + t + 1)
                    wait(act, turned, PAIRS * b)
                    for half, (x4, slots) in enumerate(((q4, slice(0, 2)), (k4, slice(0, 4, 2)))):
                        src = psQK[t][:, half * D:(half + 1) * D].rearrange("p (h a d) -> p h a d", a=1, d=DH)
                        nc.scalar.activation(x4[:, t, :, slots, :], src.to_broadcast([P, HEADS, 2, DH]),
                                             ACT.Copy).then_inc(qkhi_done, 1)
                act.wait_ge(v_done, b + 1)
                wait(act, pv_done, HEADS * b)
                nc.scalar.activation(v4[:, :, :, 0:DH], psV[:].rearrange("p (t h d) -> p t h d", t=NQ, d=DH),
                                     ACT.Copy).then_inc(vhi_done, 1)
                for u in range(PAIRS // 2):
                    act.wait_ge(turned, PAIRS * b + 2 * u + 2)
                    if isinstance(b, int) and b == 0 and u == 0:
                        act.wait_ge(constants, 3)
                    for s in range(2):
                        rows = slice(ROWS * s, ROWS * (s + 1))
                        nc.scalar.activation(qz[rows, 4 * u + s:4 * u + s + 3:2, :],
                                             psT[1][rows, :].rearrange("p (g q) -> p g q", g=2),
                                             ACT.Copy).then_inc(qz_done, 1)
                act.wait_ge(m_turned, b + 1)
                nc.scalar.activation(mT[:], psM[:, 0:SQ], ACT.Copy).then_inc(mT_done, 1)
                for k in range(SLOTS):
                    if k < HEADS:
                        act.wait_ge(st_done, HEADS * b + k + 1)
                        wait(act, plo_done, ring_free(b, k))
                        nc.scalar.activation(probs[:, k % RING], psE[k % RING][:].rearrange("p (t q) -> p t q", t=NQ),
                                             ACT.Exp, scale=SCALE).then_inc(exp_done, 1)
                    g, odd = divmod(k - COPY_LAG, 2)
                    if 0 <= g < PAIRS and not odd:
                        act.wait_ge(pv_done, HEADS * b + 2 * g + 2)
                        wait(act, back_done, PAIRS * b + g - 1)
                        for s in range(2):
                            nc.scalar.activation(aT[ROWS * s:ROWS * (s + 1), g % 2, :],
                                                 psO[g % 2][0:ROWS, s * SQ:(s + 1) * SQ], ACT.Copy).then_inc(aT_done, 1)
            turns(act, turn)

        @block.vector
        def _(dve):
            nc.vector.tensor_copy(identr[:], ident[:]).then_inc(constants, 1)
            dve.wait_ge(pick_in, 16)
            nc.vector.tensor_copy(sel[:], pick[:].rearrange("p (h a) -> p h a", a=1).to_broadcast([P, HEADS, P])).then_inc(constants, 1)
            nc.vector.memset(v4[:, :, :, 2 * DH:ROWS].bitcast(F32), 1.0).then_inc(constants, 1)
            dve.wait_ge(whi_done, 1)
            nc.vector.tensor_tensor(w_lo[:], w_raw[:], w_hi[:].bitcast(F32), ALU.subtract).then_inc(wlo_done, 1)

            def normalize(b, grp):
                dve.wait_ge(back_done, PAIRS * b + GROUP * (grp + 1))
                for t in range(NQ):
                    out = psB[t][:].rearrange("p (h r) -> p h r", r=ROWS)
                    n = NQ * (2 * b + grp) + t + 1
                    nc.vector.reciprocal(rinv[:, t], out[:, :, 2 * DH]).then_inc(rinv_done, 1)
                    nc.vector.tensor_reduce(num[:, t], out[:, :, 0:2 * DH].rearrange("p h (u d) -> p h d u", u=2),
                                            AX.X, ALU.add).then_inc(num_done, 1)
                for t in range(NQ):
                    n = NQ * (2 * b + grp) + t + 1
                    dve.wait_ge(rinv_done, n)
                    dve.wait_ge(num_done, n)
                    cols = slice(grp * GROUP * 2 * DH, (grp + 1) * GROUP * 2 * DH)
                    dst = O[:, bass.ds(NQ * b + t, 1), cols].rearrange("p a (h d) -> p (a h) d", d=DH)
                    scale = rinv[:, t].rearrange("p (h a) -> p h a", a=1).to_broadcast([P, 2 * GROUP, DH])
                    nc.vector.tensor_tensor(dst, num[:, t], scale, ALU.mult).then_inc(norm_done, 1)

            def turn(b):
                dve.wait_ge(xhi_done, b + 1)
                nc.vector.tensor_tensor(x_lo[:], XNT[:, :, bass.ds(b * SQ, SQ)], x_hi[:].bitcast(F32),
                                        ALU.subtract).then_inc(xlo_done, 1)
                for t in range(NQ):
                    dve.wait_ge(qkhi_done, 2 * (NQ * b + t) + 2)
                    for half, (x4, hi, slots) in enumerate(((q4, 0, slice(2, 4)), (k4, 0, slice(1, 4, 2)))):
                        src = psQK[t][:, half * D:(half + 1) * D].rearrange("p (h a d) -> p h a d", a=1, d=DH)
                        nc.vector.tensor_tensor(x4[:, t, :, slots, :], src.to_broadcast([P, HEADS, 2, DH]),
                                                x4[:, t, :, hi:hi + 1, :].bitcast(F32).to_broadcast([P, HEADS, 2, DH]),
                                                ALU.subtract).then_inc(qklo_done, 1)
                dve.wait_ge(vhi_done, b + 1)
                nc.vector.tensor_tensor(v4[:, :, :, DH:2 * DH], psV[:].rearrange("p (t h d) -> p t h d", t=NQ, d=DH),
                                        v4[:, :, :, 0:DH].bitcast(F32), ALU.subtract).then_inc(vlo_done, 1)
                for u in range(PAIRS // 2):
                    dve.wait_ge(turned, PAIRS * b + 2 * u + 1)
                    nc.vector.tensor_copy(kT[:, 2 * u:2 * u + 2, :], psT[0][:].rearrange("p (g k) -> p g k", g=2)).then_inc(kT_done, 1)
                for n in range(NQ * PAIRS):
                    t, g = divmod(n, PAIRS)
                    dve.wait_ge(smax_done, NQ * PAIRS * b + n + 1)
                    nc.vector.tensor_reduce(negmax[:, t, 2 * g:2 * g + 2], psS[n % 2][:].rearrange("p (h k) -> p h k", h=2),
                                            AX.X, ALU.max, negate=True).then_inc(max_done, 1)
                dve.wait_ge(max_done, NQ * PAIRS * (b + 1))
                wait(dve, m_turned, b)
                nc.vector.tensor_copy(mz[:, :, 0:HEADS], negmax[:]).then_inc(mhi_done, 1)
                dve.wait_ge(mhi_done, b + 1)
                nc.vector.tensor_tensor(mz[:, :, HEADS:2 * HEADS], negmax[:], mz[:, :, 0:HEADS].bitcast(F32),
                                        ALU.subtract).then_inc(mlo_done, 1)
                for h in range(HEADS):
                    dve.wait_ge(phi_done, HEADS * b + h + 1)
                    nc.vector.tensor_tensor(p_lo[:, h % RING], probs[:, h % RING], p_hi[:, h % RING].bitcast(F32),
                                            ALU.subtract).then_inc(plo_done, 1)
                    if h == 2 * (GROUP - 1) + BACK_LAG + 1:
                        normalize(b, 0)
                normalize(b, 1)
            turns(dve, turn)

        @block.tensor
        def _(pe):
            pe.wait_ge(constants, 5)
            pe.wait_ge(wlo_done, 1)

            def project(b, t, ps, cols):
                n = 0
                for x, w in ((x_hi, w_hi), (x_lo, w_hi), (x_hi, w_lo)):
                    for c in range(DC):
                        last = nc.tensor.matmul(ps, x[:, c, t * P:(t + 1) * P], w[:, c, cols],
                                                start=(n == 0), stop=(n == 3 * DC - 1), skip_group_check=True)
                        n += 1
                return last

            def turn(b):
                pe.wait_ge(xlo_done, b + 1)
                wait(pe, norm_done, 2 * NQ * b)
                for t in range(NQ):
                    project(b, t, psQK[t][:], slice(0, 2 * D)).then_inc(qk_done, 1)
                for t in range(NQ):
                    last = project(b, t, psV[:, t * D:(t + 1) * D], slice(2 * D, 3 * D))
                last.then_inc(v_done, 1)
                pe.wait_ge(qklo_done, 2 * NQ * (b + 1))
                wait(pe, aT_done, 2 * PAIRS * b)
                for u in range(PAIRS // 2):
                    for half, x4 in enumerate((k4, q4)):
                        wait(pe, (kT_done, qz_done)[half], (1, 2)[half] * ((PAIRS // 2) * b + u))
                        for g in range(2):
                            for t in range(NQ):
                                pair = x4[:, t, 4 * u + 2 * g:4 * u + 2 * g + 2].rearrange("p h a d -> p (h a d)")
                                last = nc.tensor.transpose(psT[half][:, (NQ * g + t) * P:(NQ * g + t + 1) * P].bitcast(F32R),
                                                           pair, identr[:])
                        last.then_inc(turned, 1)
                for n in range(NQ * PAIRS):
                    t, g = divmod(n, PAIRS)
                    pe.wait_ge(kT_done, (PAIRS // 2) * b + g // 2 + 1)
                    pe.wait_ge(qz_done, PAIRS * b + 2 * (g // 2) + 2)
                    wait(pe, max_done, NQ * PAIRS * b + n - 1)
                    for s in range(2):
                        last = nc.tensor.matmul(psS[n % 2][:, s * SQ:(s + 1) * SQ], qz[:, 2 * g + s, t * P:(t + 1) * P],
                                                kT[:, g, :], start=True, stop=True)
                    last.then_inc(smax_done, 1)
                pe.wait_ge(mlo_done, b + 1)
                pe.wait_ge(vlo_done, b + 1)
                for t in range(NQ):
                    last = nc.tensor.transpose(psM[:, t * P:(t + 1) * P].bitcast(F32R), mz[:, t, :], identr[:])
                last.then_inc(m_turned, 1)
                pe.wait_ge(mT_done, b + 1)
                for k in range(SLOTS):
                    if k < HEADS:
                        h = k
                        wait(pe, exp_done, ring_free(b, h))
                        for t in range(NQ):
                            ps = psE[h % RING][:, t * SQ:(t + 1) * SQ]
                            nc.tensor.matmul(ps, kT[:, h // 2, t * P:(t + 1) * P], qz[:, h, :], start=True, stop=False)
                            last = nc.tensor.matmul(ps, sel[:, h, :], mT[:], start=False, stop=True)
                        last.then_inc(st_done, 1)
                    h = k - PV_LAG
                    if 0 <= h < HEADS:
                        pe.wait_ge(plo_done, HEADS * b + h + 1)
                        if h % 2 == 0:
                            wait(pe, aT_done, 2 * (PAIRS * b + h // 2 - 1))
                        n = 0
                        for part in (p_hi, p_lo):
                            for t in range(NQ):
                                last = nc.tensor.matmul(psO[(h // 2) % 2][0:ROWS, (h % 2) * SQ:(h % 2 + 1) * SQ],
                                                        v4[:, t, h, :], part[:, h % RING, t, :],
                                                        start=(n == 0), stop=(n == 3))
                                n += 1
                        last.then_inc(pv_done, 1)
                    g, odd = divmod(k - BACK_LAG, 2)
                    if 0 <= g < PAIRS and not odd:
                        pe.wait_ge(aT_done, 2 * (PAIRS * b + g + 1))
                        if g % GROUP == 0:
                            pe.wait_ge(max_done, NQ * PAIRS * (b + 1))
                            wait(pe, norm_done, NQ * (2 * b + g // GROUP))
                        for t in range(NQ):
                            last = nc.tensor.transpose(psB[t][:, (g % GROUP) * P:(g % GROUP + 1) * P],
                                                       aT[:, g % 2, t * P:(t + 1) * P], ident[:])
                        last.then_inc(back_done, 1)
            turns(pe, turn)


def routed_ffn(nc, X, xT_hi, xT_lo, w, out_v, ident):
    NT, D = X.shape[1], X.shape[2]
    DC = D // P
    T = NT * P
    E = 64
    NG = 64
    TQ = T // NG
    BUDGET = TQ * 16
    NC = w["up_gate"].shape[0]
    HT = T // 2
    TH = T // BANK
    BIG = 3.0e38

    with ExitStack() as ctx:
        def sb(name, shape, dt=F32, ctx=ctx):
            return ctx.enter_context(nc.sbuf_tensor(f"ff_{name}", shape, dt))

        def sem(name, ctx=ctx):
            return ctx.enter_context(nc.semaphore(f"ff_{name}"))

        G = sb("G", [P, NC, T])
        FT = sb("FT", [E, T])
        fs_dram = nc.dram_tensor("fs_scratch", (E, T), F32, kind="Internal").ap()
        fnorm = sb("fnorm", [P, NT])

        with ExitStack() as one:
            def sb1(name, shape, dt=F32):
                return sb(name, shape, dt, one)

            def sem1(name):
                return sem(name, one)

            wr_raw = sb1("wr_raw", [P, DC, E])
            wr_hi = sb1("wr_hi", [P, DC, E], F32R)
            wr_lo = sb1("wr_lo", [P, DC, E], F32R)
            br = sb1("br", [E, 1])
            bup = sb1("bup", [P, NC])
            bgate = sb1("bgate", [P, NC])
            diag = sb1("diag", [P, E])
            tq_of = sb1("tq_of", [P, TQ // 2])
            w_raw = sb1("w_raw", [P, 2, 2, DC, P])
            w_hi = sb1("w_hi", [P, 2, 2, DC, P], F32R)
            w_lo = sb1("w_lo", [P, 2, 2, DC, P], F32R)
            gate = sb1("gate", [P, 2, T])
            buf_a = sb1("buf_a", [P, T])
            buf_b = sb1("buf_b", [P, T])
            buf_c = sb1("buf_c", [P, T])
            buf_d = sb1("buf_d", [P, T])
            RT = sb1("RT", [E, T])
            R = sb1("R", [P, NT, E])
            sort_x = sb1("sort_x", [P, HT])
            sort_y = sb1("sort_y", [P, HT])
            small = sb1("small", [P, 16, 8])
            ones = sb1("ones", [P, P])
            rowcount = sb1("rowcount", [P, E])
            psU = one.enter_context(nc.psum_tensor("ff_psU", [P, T], F32))
            psG = one.enter_context(nc.psum_tensor("ff_psG", [P, T], F32))
            psR = one.enter_context(nc.psum_tensor("ff_psR", [P, T], F32))
            psL = one.enter_context(nc.psum_tensor("ff_psL", [P, BANK], F32))
            psD = one.enter_context(nc.psum_tensor("ff_psD", [P, BANK], F32))

            small_in = sem1("small_in")
            w_in = [sem1(f"w_in{s}") for s in range(2)]
            wr_hi_done = sem1("wr_hi_done")
            wr_lo_done = sem1("wr_lo_done")
            ones_done = sem1("ones_done")
            whi_done = sem1("whi_done")
            wlo_done = sem1("wlo_done")
            up_done = sem1("up_done")
            gate_done = sem1("gate_done")
            silu_done = sem1("silu_done")
            biased_done = sem1("biased_done")
            gated = sem1("gated")
            logits_done = sem1("logits_done")
            logits_saved = sem1("logits_saved")
            logits_turned = sem1("logits_turned")
            shifted = sem1("shifted")
            router_exp = sem1("router_exp")
            scores_ready = sem1("scores_ready")
            scores_turned = sem1("scores_turned")
            step = sem1("step")
            spread_ready = sem1("spread_ready")
            spread_done = sem1("spread_done")
            kept_ready = sem1("kept_ready")
            fsum_done = sem1("fsum_done")
            fs_stored = sem1("fs_stored")

            SPREAD, SPREAD_MAX, SUM = 12, 16, 24

            block = one.enter_context(nc.Block())

            @block.sync
            def _(sp):
                sp.dma_start(wr_raw[:], w["router"].rearrange("(c p) e -> p c e", p=P)).then_inc(small_in, 16)
                for dst, src in ((br, "router_bias"), (bup, "up_bias"), (bgate, "gate_bias"), (diag, "diag"), (tq_of, "tq_of")):
                    sp.dma_start(dst[:], w[src]).then_inc(small_in, 16)

                def load(c):
                    wait(sp, whi_done, c - 1)
                    wait(sp, wlo_done, c - 1)
                    s = c % 2
                    sp.dma_start(w_raw[:, s], w["up_gate"][c]).then_inc(w_in[s], 16)

                load(0)
                load(1)
                with sp.Fori(1, NC // 2) as pair:
                    c = 2 * pair
                    for s in range(2):
                        sp.wait_ge(whi_done, c + s - 1)
                        sp.wait_ge(wlo_done, c + s - 1)
                        sp.dma_start(w_raw[:, s], w["up_gate"][c + s]).then_inc(w_in[s], 16)
                sp.wait_ge(kept_ready, 1)
                sp.dma_start(fs_dram, FT[:]).then_inc(fs_stored, 16)
                sp.wait_ge(fs_stored, 16)

            @block.scalar
            def _(act):
                def split(c, s):
                    act.wait_ge(w_in[s], 8 * (c - s) + 16)
                    wait(act, gate_done, c - 1)
                    nc.scalar.activation(w_hi[:, s], w_raw[:, s], ACT.Copy).then_inc(whi_done, 1)

                def gates(c, s):
                    act.wait_ge(up_done, c + 1)
                    nc.scalar.activation(G[:, bass.ds(c, 1), :].rearrange("p a t -> p (a t)"), psU[:], ACT.Silu,
                                         bias=bup[:, bass.ds(c, 1)]).then_inc(silu_done, 1)
                    act.wait_ge(gate_done, c + 1)
                    wait(act, gated, c - 1)
                    nc.scalar.activation(gate[:, s], psG[:], ACT.Identity, bias=bgate[:, bass.ds(c, 1)]).then_inc(biased_done, 1)

                act.wait_ge(small_in, 96)
                nc.scalar.activation(wr_hi[:], wr_raw[:], ACT.Copy).then_inc(wr_hi_done, 1)
                split(0, 0)
                act.wait_ge(logits_done, 1)
                nc.scalar.activation(buf_a[0:E, :], psR[0:E, :], ACT.Identity, bias=br[:]).then_inc(logits_saved, 1)
                split(1, 1)
                act.wait_ge(shifted, 1)
                nc.scalar.activation(R[:], R[:], ACT.Exp).then_inc(router_exp, 1)
                gates(0, 0)
                split(2, 0)
                gates(1, 1)
                with act.Fori(1, (NC - 2) // 2) as pair:
                    c = 2 * pair
                    split(c + 1, 1)
                    gates(c, 0)
                    split(c + 2, 0)
                    gates(c + 1, 1)
                split(NC - 1, 1)
                gates(NC - 2, 0)
                gates(NC - 1, 1)

            @block.gpsimd
            def _(pool):
                nc.gpsimd.memset(ones[:], 1.0).then_inc(ones_done, 1)

                def split(c, s):
                    pool.wait_ge(whi_done, c + 1)
                    nc.gpsimd.tensor_tensor(w_lo[:, s], w_raw[:, s], w_hi[:, s].bitcast(F32), ALU.subtract).then_inc(wlo_done, 1)

                def product(c, s):
                    pool.wait_ge(silu_done, c + 1)
                    pool.wait_ge(biased_done, c + 1)
                    row = G[:, bass.ds(c, 1), :].rearrange("p a t -> p (a t)")
                    nc.gpsimd.tensor_tensor(row, row, gate[:, s], ALU.mult).then_inc(gated, 1)

                split(0, 0)
                split(1, 1)
                product(0, 0)
                split(2, 0)
                product(1, 1)
                with pool.Fori(1, (NC - 2) // 2) as pair:
                    c = 2 * pair
                    split(c + 1, 1)
                    product(c, 0)
                    split(c + 2, 0)
                    product(c + 1, 1)
                split(NC - 1, 1)
                product(NC - 2, 0)
                product(NC - 1, 1)

            @block.tensor
            def _(pe):
                def hidden(c, s):
                    pe.wait_ge(wlo_done, c + 1)
                    for u, (ps, done, left) in enumerate(((psU, up_done, silu_done), (psG, gate_done, biased_done))):
                        wait(pe, left, c)
                        for h in range(TH):
                            cols = slice(h * BANK, (h + 1) * BANK)
                            n = 0
                            for a, b in ((w_hi, xT_hi), (w_hi, xT_lo), (w_lo, xT_hi)):
                                for k in range(DC):
                                    last = nc.tensor.matmul(ps[:, cols], a[:, s, u, k, :], b[:, k, cols],
                                                            start=(n == 0), stop=(n == 3 * DC - 1))
                                    n += 1
                        last.then_inc(done, 1)

                def run(first, last):
                    with pe.Fori(first // 2, last // 2) as pair:
                        c = 2 * pair
                        hidden(c, 0)
                        hidden(c + 1, 1)

                pe.wait_ge(wr_lo_done, 1)
                for h in range(TH):
                    cols = slice(h * BANK, (h + 1) * BANK)
                    n = 0
                    for a, b in ((wr_hi, xT_hi), (wr_hi, xT_lo), (wr_lo, xT_hi)):
                        for k in range(DC):
                            last = nc.tensor.matmul(psR[0:E, cols], a[:, k, :], b[:, k, cols],
                                                    start=(n == 0), stop=(n == 3 * DC - 1))
                            n += 1
                last.then_inc(logits_done, 1)
                pe.wait_ge(logits_saved, 1)
                for t in range(NT):
                    last = nc.tensor.transpose(psL[:, t * E:(t + 1) * E], buf_a[0:E, t * P:(t + 1) * P], ident[0:E, 0:E])
                last.then_inc(logits_turned, 1)
                hidden(0, 0)
                pe.wait_ge(scores_ready, 1)
                for t in range(NT):
                    last = nc.tensor.transpose(psR[0:E, t * P:(t + 1) * P], R[:, t, :], ident[:])
                last.then_inc(scores_turned, 1)
                hidden(1, 1)
                run(2, SPREAD)
                pe.wait_ge(ones_done, 1)
                pe.wait_ge(spread_ready, 1)
                for h in range(TH):
                    cols = slice(h * BANK, (h + 1) * BANK)
                    last = nc.tensor.matmul(psR[:, cols], ones[:], buf_b[:, cols], start=True, stop=True)
                last.then_inc(spread_done, 1)
                run(SPREAD, SPREAD_MAX)
                pe.wait_ge(spread_ready, 2)
                nc.tensor.matmul(psL[:, 0:P], ones[:], buf_b[:, 0:P], start=True, stop=True).then_inc(spread_done, 1)
                run(SPREAD_MAX, SUM)
                pe.wait_ge(kept_ready, 1)
                for t in range(NT):
                    last = nc.tensor.matmul(psD[:, 2 * t:2 * t + 2], FT[:, t * P:(t + 1) * P], ones[0:E, 0:2],
                                            start=True, stop=True)
                last.then_inc(fsum_done, 1)
                run(SUM, NC)

            @block.vector
            def _(dve):
                steps = [0]

                def tick():
                    steps[0] += 1
                    return 1

                def col(k, n=1):
                    return small[:, k, 0:n]

                dve.wait_ge(wr_hi_done, 1)
                nc.vector.tensor_tensor(wr_lo[:], wr_raw[:], wr_hi[:].bitcast(F32), ALU.subtract).then_inc(wr_lo_done, 1)

                dve.wait_ge(logits_turned, 1)
                logits = psL[:].rearrange("p (t e) -> p t e", e=E)

                def over_experts(k):
                    return small[:, k, 0:NT].rearrange("p (t a) -> p t a", a=1).to_broadcast([P, NT, E])

                nc.vector.tensor_reduce(small[:, 0, 0:NT], logits, AX.X, ALU.max).then_inc(step, tick())
                dve.wait_ge(step, steps[0])
                nc.vector.tensor_tensor(R[:], logits, over_experts(0), ALU.subtract).then_inc(shifted, 1)
                dve.wait_ge(router_exp, 1)
                nc.vector.tensor_reduce(small[:, 1, 0:NT], R[:], AX.X, ALU.add).then_inc(step, tick())
                dve.wait_ge(step, steps[0])
                nc.vector.reciprocal(small[:, 2, 0:NT], small[:, 1, 0:NT]).then_inc(step, tick())
                dve.wait_ge(step, steps[0])
                nc.vector.tensor_tensor(R[:], R[:], over_experts(2), ALU.mult).then_inc(scores_ready, 1)

                dve.wait_ge(scores_turned, 1)
                nc.vector.tensor_copy(RT[:], psR[0:E, :]).then_inc(step, tick())
                nc.vector.tensor_copy(sort_x[0:E, :], psR[0:E, 0:HT]).then_inc(step, tick())
                nc.vector.tensor_copy(sort_x[E:P, :], psR[0:E, HT:T]).then_inc(step, tick())

                src, dst = sort_x, sort_y

                def compare(a, b, big, less):
                    nonlocal src, dst
                    dve.wait_ge(step, steps[0])
                    nc.vector.tensor_tensor(big, a, b, ALU.max).then_inc(step, tick())
                    nc.vector.tensor_tensor(less, a, b, ALU.min).then_inc(step, tick())
                    src, dst = dst, src

                def by_distance(j):
                    a = src[:].rearrange("p (n u j) -> p n u j", u=2, j=j)
                    b = dst[:].rearrange("p (n u j) -> p n u j", u=2, j=j)
                    compare(a[:, :, 0, :], a[:, :, 1, :], b[:, :, 0, :], b[:, :, 1, :])

                k = 2
                while k <= HT:
                    a = src[:].rearrange("p (n k) -> p n k", k=k)
                    b = dst[:].rearrange("p (n k) -> p n k", k=k)
                    mirrored = slice(k - 1, k // 2 - 1, -1)
                    compare(a[:, :, 0:k // 2], a[:, :, mirrored], b[:, :, 0:k // 2], b[:, :, mirrored])
                    j = k // 4
                    while j:
                        by_distance(j)
                        j //= 2
                    k *= 2
                dve.wait_ge(step, steps[0])
                nc.vector.tensor_copy(dst[0:E, :], src[E:P, :]).then_inc(step, tick())
                nc.vector.tensor_copy(dst[E:P, :], src[0:E, :]).then_inc(step, tick())
                dve.wait_ge(step, steps[0])
                nc.vector.tensor_tensor(buf_a[0:E, 0:HT], src[0:E, :], dst[0:E, ::-1], ALU.max).then_inc(step, tick())
                nc.vector.tensor_tensor(buf_a[E:P, 0:HT], src[E:P, :], dst[E:P, ::-1], ALU.min).then_inc(step, tick())
                src = buf_a[:, 0:HT]
                ring = [sort_x[:], sort_y[:], sort_x[:]]
                for n, j in enumerate((HT // 2, HT // 4, NG)):
                    a = src.rearrange("p (n u j) -> p n u j", u=2, j=j)
                    b = ring[n].rearrange("p (n u j) -> p n u j", u=2, j=j)
                    dve.wait_ge(step, steps[0])
                    nc.vector.tensor_tensor(b[:, :, 0, :], a[:, :, 0, :], a[:, :, 1, :], ALU.max).then_inc(step, tick())
                    nc.vector.tensor_tensor(b[:, :, 1, :], a[:, :, 0, :], a[:, :, 1, :], ALU.min).then_inc(step, tick())
                    src = ring[n]
                dve.wait_ge(step, steps[0])
                H8 = TQ // 2
                groups = src.rearrange("p (g n) -> p g n", n=NG)
                gsum, gmin = small[:, 3, 0:H8], small[:, 4, 0:H8]
                nc.vector.tensor_reduce(gmin, groups, AX.X, ALU.min).then_inc(step, tick())
                dve.wait_ge(step, steps[0])
                nc.vector.tensor_reduce(gsum, groups, AX.X, ALU.add).then_inc(step, tick())
                dve.wait_ge(step, steps[0])

                nc.vector.tensor_tensor(buf_b[:].rearrange("p (g q) -> p g q", g=H8),
                                        gsum.rearrange("p (g a) -> p g a", a=1).to_broadcast([P, H8, P]),
                                        ident[:].rearrange("p (a q) -> p a q", a=1).to_broadcast([P, H8, P]),
                                        ALU.mult).then_inc(spread_ready, 1)
                dve.wait_ge(spread_done, 1)
                allsums = buf_c
                nc.vector.tensor_copy(allsums[:].rearrange("p (h g e) -> p h g e", h=2, g=H8),
                                      psR[:].rearrange("p (g h e) -> p h g e", h=2, g=H8)).then_inc(step, tick())
                dve.wait_ge(step, steps[0])
                for g in range(H8):
                    nc.vector.tensor_scalar(buf_d[:], allsums[:], small[:, 3, g:g + 1], None, ALU.is_ge, ALU.add,
                                            accum_out=small[:, 5, g:g + 1]).then_inc(step, tick())
                    dve.wait_ge(step, steps[0])
                nc.vector.scalar_tensor_tensor(small[:, 6, 0:H8], small[:, 5, 0:H8], float(BUDGET), gsum,
                                               ALU.is_ge, ALU.mult).then_inc(step, tick())
                dve.wait_ge(step, steps[0])
                nc.vector.tensor_reduce(col(7), small[:, 6, 0:H8], AX.X, ALU.max).then_inc(step, tick())
                dve.wait_ge(step, steps[0])
                nc.vector.tensor_scalar(buf_b[:, 0:P], ident[:], col(7), None, ALU.mult).then_inc(spread_ready, 1)
                dve.wait_ge(spread_done, 2)
                threshold = col(8)
                nc.vector.tensor_reduce(threshold, psL[:, 0:P], AX.X, ALU.max).then_inc(step, tick())
                dve.wait_ge(step, steps[0])
                above, equal, upto = buf_d, buf_a, buf_b
                nc.vector.tensor_scalar(above[:], allsums[:], threshold, None, ALU.is_gt, ALU.add, accum_out=col(10)).then_inc(step, tick())
                nc.vector.tensor_scalar(equal[:], allsums[:], threshold, None, ALU.is_equal).then_inc(step, tick())
                dve.wait_ge(step, steps[0])
                nc.vector.tensor_scalar(col(11), col(10), -1.0, float(BUDGET), ALU.mult, ALU.add).then_inc(step, tick())
                nc.vector.tensor_tensor_scan(upto[:], equal[:], equal[:], 0.0, ALU.add, ALU.max).then_inc(step, tick())
                dve.wait_ge(step, steps[0])
                nc.vector.scalar_tensor_tensor(equal[:], upto[:], col(11), equal[:], ALU.is_le, ALU.mult).then_inc(step, tick())
                dve.wait_ge(step, steps[0])
                nc.vector.tensor_tensor(above[:], above[:], equal[:], ALU.add).then_inc(step, tick())
                dve.wait_ge(step, steps[0])
                nc.vector.tensor_reduce(rowcount[:], above[:].rearrange("p (q e) -> p e q", e=E), AX.X, ALU.add).then_inc(step, tick())
                dve.wait_ge(step, steps[0])
                nc.vector.tensor_tensor(rowcount[:], rowcount[:], diag[:], ALU.mult).then_inc(step, tick())
                dve.wait_ge(step, steps[0])
                nc.vector.tensor_reduce(col(12), rowcount[:], AX.X, ALU.add).then_inc(step, tick())
                dve.wait_ge(step, steps[0])
                nc.vector.tensor_scalar(small[:, 13, 0:H8], tq_of[:], col(12), BIG, ALU.is_ge, ALU.mult).then_inc(step, tick())
                dve.wait_ge(step, steps[0])
                nc.vector.tensor_tensor(small[:, 13, 0:H8], small[:, 13, 0:H8], gmin, ALU.max).then_inc(step, tick())
                dve.wait_ge(step, steps[0])
                nc.vector.tensor_reduce(col(14), small[:, 13, 0:H8], AX.X, ALU.min).then_inc(step, tick())
                dve.wait_ge(step, steps[0])
                nc.vector.tensor_copy(small[0:E, 15, 0:1], small[E:P, 14, 0:1]).then_inc(step, tick())
                dve.wait_ge(step, steps[0])
                nc.vector.tensor_tensor(small[0:E, 15, 1:2], small[0:E, 15, 0:1], small[0:E, 14, 0:1], ALU.min).then_inc(step, tick())
                dve.wait_ge(step, steps[0])
                least = small[0:E, 15, 1:2]
                nc.vector.tensor_scalar(above[0:E, :], RT[:], least, None, ALU.is_gt, ALU.add, accum_out=small[0:E, 15, 2:3]).then_inc(step, tick())
                nc.vector.tensor_scalar(equal[0:E, :], RT[:], least, None, ALU.is_equal).then_inc(step, tick())
                nc.vector.tensor_scalar(small[0:E, 15, 3:4], small[0:E, 12, 0:1], float(NG), None, ALU.mult).then_inc(step, tick())
                dve.wait_ge(step, steps[0])
                nc.vector.tensor_tensor(small[0:E, 15, 4:5], small[0:E, 15, 3:4], small[0:E, 15, 2:3], ALU.subtract).then_inc(step, tick())
                nc.vector.tensor_tensor_scan(upto[0:E, :], equal[0:E, :], equal[0:E, :], 0.0, ALU.add, ALU.max).then_inc(step, tick())
                dve.wait_ge(step, steps[0])
                nc.vector.scalar_tensor_tensor(equal[0:E, :], upto[0:E, :], small[0:E, 15, 4:5], equal[0:E, :],
                                               ALU.is_le, ALU.mult).then_inc(step, tick())
                dve.wait_ge(step, steps[0])
                nc.vector.tensor_tensor(above[0:E, :], above[0:E, :], equal[0:E, :], ALU.add).then_inc(step, tick())
                dve.wait_ge(step, steps[0])
                nc.vector.tensor_tensor(FT[:], RT[:], above[0:E, :], ALU.mult).then_inc(kept_ready, 1)
                dve.wait_ge(fsum_done, 1)
                nc.vector.tensor_scalar(small[:, 0, 0:NT], psD[:, 0:2 * NT:2], 1e-6, None, ALU.add).then_inc(step, tick())
                dve.wait_ge(step, steps[0])
                nc.vector.reciprocal(fnorm[:], small[:, 0, 0:NT])

        with ExitStack() as two:
            def sb2(name, shape, dt=F32):
                return sb(name, shape, dt, two)

            def sem2(name):
                return sem(name, two)

            bdown = sb2("bdown", [E, D])
            scores = sb2("scores", [P, 2, T])
            d_raw = sb2("d_raw", [P, 2, D])
            d_hi = sb2("d_hi", [P, 2, D], F32R)
            d_lo = sb2("d_lo", [P, 2, D], F32R)
            h_hi = sb2("h_hi", [P, 2, T], F32R)
            h_lo = sb2("h_lo", [P, 2, T], F32R)
            outT = sb2("outT", [P, DC, T])
            psOut = [[two.enter_context(nc.psum_tensor(f"ff_psOut{d}_{h}", [P, BANK], F32)) for h in range(TH)]
                     for d in range(DC)]
            psX = [two.enter_context(nc.psum_tensor(f"ff_psX{k}", [P, D], F32)) for k in range(4)]

            bdown_in = sem2("bdown_in")
            scores_in = [sem2(f"scores_in{s}") for s in range(2)]
            d_in = [sem2(f"d_in{s}") for s in range(2)]
            dhi_done = sem2("dhi_done")
            dlo_done = sem2("dlo_done")
            scaled = sem2("scaled")
            hhi_done = sem2("hhi_done")
            hlo_done = sem2("hlo_done")
            down_done = sem2("down_done")
            all_done = sem2("all_done")
            outT_done = sem2("outT_done")
            x_turned = sem2("x_turned")
            x_done = sem2("x_done")
            out_stored = sem2("out_stored")

            block = two.enter_context(nc.Block())

            @block.sync
            def _(sp):
                sp.dma_start(bdown[:], w["down_bias"]).then_inc(bdown_in, 16)

                def load(c, s):
                    wait(sp, scaled, c - 1)
                    for e in range(2):
                        sp.dma_start(scores[e * NG:(e + 1) * NG, s], fs_dram[bass.ds(2 * c + e, 1), :].to_broadcast([NG, T])
                                     ).then_inc(scores_in[s], 16)
                    wait(sp, dhi_done, c - 1)
                    wait(sp, dlo_done, c - 1)
                    sp.dma_start(d_raw[:, s], w["down"][c]).then_inc(d_in[s], 16)

                load(0, 0)
                load(1, 1)
                with sp.Fori(1, NC // 2) as pair:
                    c = 2 * pair
                    load(c, 0)
                    load(c + 1, 1)
                for t in range(NT):
                    sp.wait_ge(x_done, t + 1)
                    sp.dma_start(out_v[:, t, :], X[:, t, :]).then_inc(out_stored, 16)
                sp.wait_ge(out_stored, 16 * NT)

            @block.vector
            def _(dve):
                def turn(c, s):
                    row = G[:, bass.ds(c, 1), :].rearrange("p a t -> p (a t)")
                    dve.wait_ge(scores_in[s], 16 * (c - s) + 32)
                    nc.vector.tensor_tensor(row, row, scores[:, s], ALU.mult).then_inc(scaled, 1)
                    dve.wait_ge(hhi_done, c + 1)
                    wait(dve, down_done, c - 1)
                    nc.vector.tensor_tensor(h_lo[:, s], row, h_hi[:, s].bitcast(F32), ALU.subtract).then_inc(hlo_done, 1)

                turn(0, 0)
                turn(1, 1)
                with dve.Fori(1, NC // 2) as pair:
                    c = 2 * pair
                    turn(c, 0)
                    turn(c + 1, 1)
                dve.wait_ge(all_done, 1)
                nc.vector.tensor_copy(outT[:, 1, 0:BANK], psOut[1][0][:]).then_inc(outT_done, 1)
                nc.vector.tensor_copy(outT[:, 1, BANK:T], psOut[1][1][:]).then_inc(outT_done, 1)
                for t in range(NT):
                    dve.wait_ge(x_turned, t + 1)
                    nc.vector.scalar_tensor_tensor(X[:, t, :], psX[t % 4][:], fnorm[:, t:t + 1], X[:, t, :],
                                                   ALU.mult, ALU.add).then_inc(x_done, 1)

            @block.scalar
            def _(act):
                def turn(c, s):
                    act.wait_ge(d_in[s], 8 * (c - s) + 16)
                    wait(act, down_done, c - 1)
                    nc.scalar.activation(d_hi[:, s], d_raw[:, s], ACT.Copy).then_inc(dhi_done, 1)
                    act.wait_ge(scaled, c + 1)
                    row = G[:, bass.ds(c, 1), :].rearrange("p a t -> p (a t)")
                    nc.scalar.activation(h_hi[:, s], row, ACT.Copy).then_inc(hhi_done, 1)

                turn(0, 0)
                turn(1, 1)
                with act.Fori(1, NC // 2) as pair:
                    c = 2 * pair
                    turn(c, 0)
                    turn(c + 1, 1)
                act.wait_ge(all_done, 1)
                nc.scalar.activation(outT[:, 0, 0:BANK], psOut[0][0][:], ACT.Copy).then_inc(outT_done, 1)
                nc.scalar.activation(outT[:, 0, BANK:T], psOut[0][1][:], ACT.Copy).then_inc(outT_done, 1)

            @block.gpsimd
            def _(pool):
                def turn(c, s):
                    pool.wait_ge(dhi_done, c + 1)
                    nc.gpsimd.tensor_tensor(d_lo[:, s], d_raw[:, s], d_hi[:, s].bitcast(F32), ALU.subtract).then_inc(dlo_done, 1)

                with pool.Fori(0, NC // 2) as pair:
                    c = 2 * pair
                    turn(c, 0)
                    turn(c + 1, 1)

            @block.tensor
            def _(pe):
                pe.wait_ge(bdown_in, 16)
                for d in range(DC):
                    for h in range(TH):
                        nc.tensor.matmul(psOut[d][h][:], bdown[:, d * P:(d + 1) * P], FT[:, h * BANK:(h + 1) * BANK],
                                         start=True, stop=False)

                def turn(s, c, last_one=False):
                    pe.wait_ge(dlo_done, c + 1)
                    pe.wait_ge(hhi_done, c + 1)
                    for n, (a, b) in enumerate(((d_hi, h_hi), (d_lo, h_hi), (d_hi, h_lo))):
                        if n == 2:
                            pe.wait_ge(hlo_done, c + 1)
                        for d in range(DC):
                            for h in range(TH):
                                last = nc.tensor.matmul(psOut[d][h][:], a[:, s, d * P:(d + 1) * P],
                                                        b[:, s, h * BANK:(h + 1) * BANK],
                                                        start=False, stop=(last_one and n == 2))
                    last.then_inc(all_done if last_one else down_done, 1)

                with pe.Fori(0, (NC - 2) // 2) as pair:
                    c = 2 * pair
                    turn(0, c)
                    turn(1, c + 1)
                turn(0, NC - 2)
                turn(1, NC - 1, last_one=True)
                pe.wait_ge(outT_done, 2 * DC)
                for t in range(NT):
                    wait(pe, x_done, t - 3)
                    for d in range(DC):
                        last = nc.tensor.transpose(psX[t % 4][:, d * P:(d + 1) * P], outT[:, d, t * P:(t + 1) * P], ident[:])
                    last.then_inc(x_turned, 1)


def perceiver_kernel(nc, x, ctx_, ctxT, mask, xw, xb, wqkv, wout, bout, ident_c, pick_c, ffn, out, stages=9):
    B, S, D = x.shape
    NT = B * S // P
    with ExitStack() as ctx:
        X = ctx.enter_context(nc.sbuf_tensor("X", [P, NT, D], F32))
        ident = ctx.enter_context(nc.sbuf_tensor("ident", [P, P], F32))
        x_in = ctx.enter_context(nc.semaphore("x_in"))
        out_done = ctx.enter_context(nc.semaphore("out_done"))
        x_v = x.rearrange("b (q p) d -> p (b q) d", p=P)
        out_v = out.rearrange("b (q p) d -> p (b q) d", p=P)
        with nc.Block() as block:
            @block.sync
            def _(sp):
                sp.dma_start(X[:], x_v).then_inc(x_in, 16)
                sp.dma_start(ident[:], ident_c).then_inc(x_in, 16)
                sp.wait_ge(x_in, 32)
        with nc.sbuf_tensor("O", [P, NT, D], F32) as O:
            with nc.sbuf_tensor("XNT1", [P, D // P, NT * P], F32) as XNT:
                ln_transpose(nc, X, XNT, ident, "ln1")
                cross_attention(nc, XNT, ctxT, ctx_, mask, xb, ident, O)
            project_add(nc, X, O, xw, None, ident, "xo")
            if stages > 1:
                with nc.sbuf_tensor("XNT2", [P, D // P, NT * P], F32) as XNT:
                    ln_transpose(nc, X, XNT, ident, "ln2")
                    self_attention(nc, XNT, wqkv, pick_c, ident, O)
                project_add(nc, X, O, wout, bout, ident, "so")
        if stages > 2:
            with nc.sbuf_tensor("xT_hi", [P, D // P, NT * P], F32R) as xT_hi, \
                    nc.sbuf_tensor("xT_lo", [P, D // P, NT * P], F32R) as xT_lo:
                ln_transpose(nc, X, None, ident, "ln3", split=(xT_hi, xT_lo))
                routed_ffn(nc, X, xT_hi, xT_lo, ffn, out_v, ident)
            return
        with nc.Block() as block:
            @block.sync
            def _(sp):
                sp.dma_start(out_v, X[:]).then_inc(out_done, 16)
                sp.wait_ge(out_done, 16)


FFN_INPUTS = ("router", "router_bias", "up_bias", "gate_bias", "diag", "tq_of", "up_gate", "down", "down_bias")


def kernel(**inputs):
    import numpy as np
    import concourse.bacc as bacc
    from concourse.bass_utils import run_bass_kernel_spmd

    i = {name: np.asarray(a) for name, a in inputs.items()}

    def ffn(name):
        return i[f"L0_ffn_{name}"]

    E, D, H = ffn("Wup").shape
    NC = E * H // P
    EC = P // H
    heads = 16
    tokens = i["x"].shape[0] * i["x"].shape[1]
    pick = np.zeros((P, heads), np.float32)
    for h in range(heads):
        pick[h, h] = pick[heads + h, h] = 1
    up_gate = np.stack([ffn("Wup"), ffn("Wgate")]).reshape(2, NC, EC, D // P, P, H)
    arrays = {
        "x": i["x"],
        "ctx_": i["ctx_1024"],
        "ctxT": i["ctx_1024"].transpose(0, 2, 1),
        "mask": i["mask_BxSxS2_fk0"],
        "xw": i["L0_xattn_weights"],
        "xb": i["L0_xattn_bias"],
        "wqkv": np.concatenate([i["L0_attn_Wq"].T, i["L0_attn_Wk"].T, i["L0_attn_Wv"].T], 1),
        "wout": i["L0_attn_Wout"].T,
        "bout": i["L0_attn_bout"],
        "ident_c": np.eye(P, dtype=np.float32),
        "pick_c": pick,
        "router": ffn("Wr"),
        "router_bias": ffn("br").reshape(E, 1),
        "up_bias": ffn("bup").reshape(NC, P).T,
        "gate_bias": ffn("bgate").reshape(NC, P).T,
        "diag": np.tile(np.eye(E, dtype=np.float32), (2, 1)),
        "tq_of": ((np.arange(P) // E)[:, None] * (tokens // 128) + np.arange(tokens // 128)).astype(np.float32),
        "up_gate": up_gate.transpose(1, 4, 0, 3, 2, 5).reshape(NC, P, 2, D // P, P),
        "down": ffn("Wdown").reshape(NC, P, D),
        "down_bias": ffn("bdown"),
    }
    nc = bacc.Bacc("TRN2", target_bir_lowering=False, num_devices=1)
    feeds, args = {}, {}
    for name, a in arrays.items():
        a = np.ascontiguousarray(a)
        feeds[f"in_{name}"] = a
        args[name] = nc.dram_tensor(f"in_{name}", a.shape, mybir.dt.from_np(a.dtype), kind="ExternalInput").ap()
    args["out"] = nc.dram_tensor("out_0", i["x"].shape, F32, kind="ExternalOutput").ap()
    args["ffn"] = {name: args.pop(name) for name in FFN_INPUTS}
    perceiver_kernel(nc, **args)
    result = run_bass_kernel_spmd(nc, [feeds], core_ids=[0])
    return result.results[0]["out_0"]
```

```python
from contextlib import ExitStack

import concourse.bass as bass
from concourse import mybir

F32 = mybir.dt.float32
F32R = mybir.dt.float32r
ALU = mybir.AluOpType
ACT = mybir.ActivationFunctionType
AX = mybir.AxisListType

P = 128
BANK = 512
EPS = 1e-5


def wait(eng, sem, n):
    if isinstance(n, int) and n <= 0:
        return
    eng.wait_ge(sem, n)


def ln_transpose(nc, X, XNT, ident, tag, split=None):
    NT, D = X.shape[1], X.shape[2]
    DC = D // P
    with ExitStack() as ctx:
        def sb(name, shape, dt=F32):
            return ctx.enter_context(nc.sbuf_tensor(f"{tag}_{name}", shape, dt))

        def sem(name):
            return ctx.enter_context(nc.semaphore(f"{tag}_{name}"))

        stats = sb("stats", [P, NT, 6])
        mv = sb("mv", [P, NT, 2])
        vare = sb("vare", [P, NT])
        std = sb("std", [P, NT])
        rstd = sb("rstd", [P, NT])
        newt = sb("newt", [P, NT])
        XN = sb("XN", [P, NT, D])
        psT = [[ctx.enter_context(nc.psum_tensor(f"{tag}_psT{k}_{c}", [P, 2 * P], F32)) for c in range(DC)]
               for k in range(NT // 2)]

        stats_done = sem("stats_done")
        mv_done = sem("mv_done")
        vare_done = sem("vare_done")
        std_done = sem("std_done")
        newton = sem("newton")
        xn_done = sem("xn_done")
        transposed = sem("transposed")
        hi_done = sem("hi_done")

        block = ctx.enter_context(nc.Block())

        @block.vector
        def _(dve):
            for t in range(NT):
                nc.vector.bn_stats(stats[:, t, :], X[:, t, :]).then_inc(stats_done, 1)
            for t in range(NT):
                dve.wait_ge(stats_done, t + 1)
                nc.vector.bn_aggr(mv[:, t, :], stats[:, t, :]).then_inc(mv_done, 1)
            dve.wait_ge(mv_done, NT)
            nc.vector.tensor_scalar(vare[:], mv[:, :, 1], EPS, None, ALU.add).then_inc(vare_done, 1)
            dve.wait_ge(std_done, 1)
            nc.vector.reciprocal(rstd[:], std[:]).then_inc(newton, 1)
            dve.wait_ge(newton, 1)
            nc.vector.tensor_tensor(newt[:], rstd[:], rstd[:], ALU.mult).then_inc(newton, 1)
            dve.wait_ge(newton, 2)
            nc.vector.tensor_tensor(newt[:], newt[:], vare[:], ALU.mult).then_inc(newton, 1)
            dve.wait_ge(newton, 3)
            nc.vector.tensor_scalar(newt[:], newt[:], -0.5, 1.5, ALU.mult, ALU.add).then_inc(newton, 1)
            dve.wait_ge(newton, 4)
            nc.vector.tensor_tensor(rstd[:], rstd[:], newt[:], ALU.mult).then_inc(newton, 1)
            dve.wait_ge(newton, 5)
            for t in range(NT):
                nc.vector.tensor_scalar(XN[:, t, :], X[:, t, :], mv[:, t, 0:1], rstd[:, t:t + 1],
                                        ALU.subtract, ALU.mult).then_inc(xn_done, 1)
            for k in range(NT // 2):
                for c in range(DC):
                    cols = slice(2 * k * P, 2 * (k + 1) * P)
                    if split is not None:
                        dve.wait_ge(hi_done, DC * k + c + 1)
                        nc.vector.tensor_tensor(split[1][:, c, cols], psT[k][c][:], split[0][:, c, cols].bitcast(F32),
                                                ALU.subtract)
                    elif c == 1:
                        dve.wait_ge(transposed, 2 * (k + 1))
                        nc.vector.tensor_copy(XNT[:, c, cols], psT[k][c][:])

        @block.scalar
        def _(act):
            act.wait_ge(vare_done, 1)
            nc.scalar.activation(std[:], vare[:], ACT.Sqrt).then_inc(std_done, 1)
            for k in range(NT // 2):
                act.wait_ge(transposed, 2 * (k + 1))
                for c in range(DC):
                    cols = slice(2 * k * P, 2 * (k + 1) * P)
                    if split is not None:
                        nc.scalar.activation(split[0][:, c, cols], psT[k][c][:], ACT.Copy).then_inc(hi_done, 1)
                    elif c == 0:
                        nc.scalar.activation(XNT[:, c, cols], psT[k][c][:], ACT.Copy)

        @block.tensor
        def _(pe):
            for t in range(NT):
                pe.wait_ge(xn_done, t + 1)
                for c in range(DC):
                    last = nc.tensor.transpose(psT[t // 2][c][:, (t % 2) * P:(t % 2 + 1) * P], XN[:, t, c * P:(c + 1) * P], ident[:])
                last.then_inc(transposed, 1)


def project_add(nc, X, A, w_dram, bias_dram, ident, tag):
    NT, D = X.shape[1], X.shape[2]
    DC = D // P
    with ExitStack() as ctx:
        def sb(name, shape, dt=F32):
            return ctx.enter_context(nc.sbuf_tensor(f"{tag}_{name}", shape, dt))

        def sem(name):
            return ctx.enter_context(nc.semaphore(f"{tag}_{name}"))

        w_raw = sb("w_raw", [P, DC, D])
        w_hi = sb("w_hi", [P, DC, D], F32R)
        w_lo = sb("w_lo", [P, DC, D], F32R)
        at_hi = sb("at_hi", [P, 2, DC, P], F32R)
        at_lo = sb("at_lo", [P, 2, DC, P], F32R)
        bias = sb("bias", [P, D])
        psT = [ctx.enter_context(nc.psum_tensor(f"{tag}_psT{k}", [P, DC, P], F32)) for k in range(2)]
        psO = [ctx.enter_context(nc.psum_tensor(f"{tag}_psO{k}", [P, BANK], F32)) for k in range(2)]

        w_in = sem("w_in")
        bias_in = sem("bias_in")
        whi_done = sem("whi_done")
        wlo_done = sem("wlo_done")
        transposed = sem("transposed")
        athi_done = sem("athi_done")
        atlo_done = sem("atlo_done")
        product_done = sem("product_done")
        bias_added = sem("bias_added")
        added = sem("added")

        block = ctx.enter_context(nc.Block())

        @block.sync
        def _(sp):
            sp.dma_start(w_raw[:], w_dram.rearrange("(c p) n -> p c n", p=P)).then_inc(w_in, 16)
            if bias_dram is not None:
                sp.dma_start(bias[:], bias_dram.rearrange("(a n) -> a n", a=1).to_broadcast([P, D])).then_inc(bias_in, 16)

        @block.scalar
        def _(act):
            act.wait_ge(w_in, 16)
            nc.scalar.activation(w_hi[:], w_raw[:], ACT.Copy).then_inc(whi_done, 1)
            for t in range(NT):
                act.wait_ge(transposed, t + 1)
                if t >= 2:
                    act.wait_ge(product_done, t - 1)
                nc.scalar.activation(at_hi[:, t % 2], psT[t % 2][:], ACT.Copy).then_inc(athi_done, 1)

        @block.vector
        def _(dve):
            if bias_dram is not None:
                dve.wait_ge(bias_in, 16)
                for t in range(NT):
                    nc.vector.tensor_tensor(X[:, t, :], X[:, t, :], bias[:], ALU.add).then_inc(bias_added, 1)
            dve.wait_ge(whi_done, 1)
            nc.vector.tensor_tensor(w_lo[:], w_raw[:], w_hi[:].bitcast(F32), ALU.subtract).then_inc(wlo_done, 1)
            for t in range(NT + 1):
                if t < NT:
                    dve.wait_ge(athi_done, t + 1)
                    nc.vector.tensor_tensor(at_lo[:, t % 2], psT[t % 2][:], at_hi[:, t % 2].bitcast(F32),
                                            ALU.subtract).then_inc(atlo_done, 1)
                if t >= 1:
                    u = t - 1
                    dve.wait_ge(product_done, u + 1)
                    if bias_dram is not None:
                        dve.wait_ge(bias_added, u + 1)
                    nc.vector.tensor_tensor(X[:, u, :], psO[u % 2][:, 0:D], X[:, u, :], ALU.add).then_inc(added, 1)

        @block.tensor
        def _(pe):
            for t in range(NT + 1):
                if t < NT:
                    if t >= 2:
                        pe.wait_ge(atlo_done, t - 1)
                    for c in range(DC):
                        last = nc.tensor.transpose(psT[t % 2][:, c, :], A[:, t, c * P:(c + 1) * P], ident[:])
                    last.then_inc(transposed, 1)
                if t >= 1:
                    u = t - 1
                    pe.wait_ge(atlo_done, u + 1)
                    if u == 0:
                        pe.wait_ge(wlo_done, 1)
                    if u >= 2:
                        pe.wait_ge(added, u - 1)
                    n = 0
                    for a, w in ((at_hi, w_hi), (at_hi, w_lo), (at_lo, w_hi)):
                        for c in range(DC):
                            last = nc.tensor.matmul(psO[u % 2][:, 0:D], a[:, u % 2, c, :], w[:, c, :],
                                                    start=(n == 0), stop=(n == 3 * DC - 1))
                            n += 1
                    last.then_inc(product_done, 1)


def cross_attention(nc, XNT, ctxT_dram, ctx_dram, mask_dram, bias_dram, ident, O):
    TEMP = 0.72
    B, D, SK = ctxT_dram.shape
    DC = D // P
    KB = BANK
    NJ = SK // KB
    KC = KB // P
    NQ = mask_dram.shape[1] // P

    ctxT_v = ctxT_dram.rearrange("b (c p) k -> b p c k", p=P)
    ctx_v = ctx_dram.rearrange("b (j c p) d -> b j p c d", p=P, c=KC)
    mask_v = mask_dram.rearrange("b (q p) k -> b p q k", p=P)

    with ExitStack() as ctx:
        def sb(name, shape, dt=F32):
            return ctx.enter_context(nc.sbuf_tensor(f"xa_{name}", shape, dt))

        def ps(name, shape):
            return ctx.enter_context(nc.psum_tensor(f"xa_{name}", shape, F32))

        def sem(name):
            return ctx.enter_context(nc.semaphore(f"xa_{name}"))

        keysT_raw = sb("keysT_raw", [P, 2, DC, KB])
        keysT_hi = sb("keysT_hi", [P, 2, DC, KB], F32R)
        keysT_lo = sb("keysT_lo", [P, 2, DC, KB], F32R)
        vals_raw = sb("vals_raw", [P, 2, KC, D])
        vals = sb("vals", [P, 2, KC, 2, D], F32R)
        mask = sb("mask", [P, 2, NQ, KB])
        S = sb("S", [P, NJ, NQ, KB])
        probs = sb("probs", [P, 2, NQ, KB])
        pT_hi = sb("pT_hi", [P, NQ, KC, P], F32R)
        pT_lo = sb("pT_lo", [P, NQ, KC, P], F32R)
        q_hi = sb("q_hi", [P, DC, NQ * P], F32R)
        q_lo = sb("q_lo", [P, DC, NQ * P], F32R)
        bias = sb("bias", [P, D])
        blockmax = sb("blockmax", [P, NQ, NJ])
        rowmax = sb("rowmax", [P, NQ])
        expbias = sb("expbias", [P, NQ])
        blocksum = sb("blocksum", [P, NQ, NJ])
        rowsum = sb("rowsum", [P, NQ])
        rinv = sb("rinv", [P, NQ])
        olo = sb("olo", [P, NQ, D])
        psS = [ps(f"psS{q}", [P, KB]) for q in range(NQ)]
        psP = [ps(f"psP{q}", [P, KC, P]) for q in range(NQ)]
        psO = [ps(f"psO{q}", [P, 2 * D]) for q in range(NQ)]

        keysT_in = [sem(f"keysT_in{s}") for s in range(2)]
        vals_in = [sem(f"vals_in{s}") for s in range(2)]
        mask_in = [sem(f"mask_in{s}") for s in range(2)]
        bias_in = sem("bias_in")
        khi_done = sem("khi_done")
        klo_done = sem("klo_done")
        vhi_done = sem("vhi_done")
        vlo_done = sem("vlo_done")
        qhi_done = sem("qhi_done")
        qlo_done = sem("qlo_done")
        scores_done = sem("scores_done")
        scores_saved = sem("scores_saved")
        rowmax_done = sem("rowmax_done")
        expbias_done = sem("expbias_done")
        exp_done = sem("exp_done")
        masked = sem("masked")
        pT_done = sem("pT_done")
        phi_done = sem("phi_done")
        plo_done = sem("plo_done")
        pv_done = sem("pv_done")
        rowsum_done = sem("rowsum_done")
        rinv_done = sem("rinv_done")
        olo_done = sem("olo_done")
        o_done = sem("o_done")

        def blocks(b, j):
            return NJ * b + j + 1

        def tiles(b, j, q):
            return NQ * (NJ * b + j) + q + 1

        def slot_loads(b, j):
            return 16 * ((NJ // 2) * b + j // 2 + 1)

        def turns(eng, turn):
            turn(0, True, False)
            turn(1, True, True)
            with eng.Fori(2, B) as i:
                turn(i, True, True)
            turn(B, False, True)

        block = ctx.enter_context(nc.Block())

        @block.sync
        def _(sp):
            sp.dma_start(bias[:], bias_dram.rearrange("(a n) -> a n", a=1).to_broadcast([P, D])).then_inc(bias_in, 16)

            def turn(i, scoring, weighing):
                for j in range(NJ):
                    if scoring:
                        wait(sp, khi_done, blocks(i, j - 2))
                        wait(sp, klo_done, blocks(i, j - 2))
                        sp.dma_start(keysT_raw[:, j % 2], ctxT_v[i, :, :, j * KB:(j + 1) * KB]).then_inc(keysT_in[j % 2], 16)
                    if weighing:
                        wait(sp, vhi_done, blocks(i - 1, j - 2))
                        wait(sp, vlo_done, blocks(i - 1, j - 2))
                        sp.dma_start(vals_raw[:, j % 2], ctx_v[i - 1, j]).then_inc(vals_in[j % 2], 16)
                        wait(sp, masked, tiles(i - 1, j - 2, NQ - 1))
                        sp.dma_start(mask[:, j % 2], mask_v[i - 1, :, :, j * KB:(j + 1) * KB]).then_inc(mask_in[j % 2], 16)
            turns(sp, turn)

        @block.scalar
        def _(act):
            def split_queries(b):
                wait(act, scores_done, tiles(b, -1, NQ - 1))
                nc.scalar.activation(q_hi[:], XNT[:, :, bass.ds(b * (NQ * P), NQ * P)], ACT.Copy).then_inc(qhi_done, 1)

            def split_keys(b, j):
                act.wait_ge(keysT_in[j % 2], slot_loads(b, j))
                wait(act, scores_done, tiles(b, j - 2, NQ - 1))
                nc.scalar.activation(keysT_hi[:, j % 2], keysT_raw[:, j % 2], ACT.Copy).then_inc(khi_done, 1)

            def split_values(b, j):
                act.wait_ge(vals_in[j % 2], slot_loads(b, j))
                wait(act, pv_done, tiles(b, j - 2, NQ - 1))
                nc.scalar.activation(vals[:, j % 2, :, 0, :], vals_raw[:, j % 2], ACT.Copy).then_inc(vhi_done, 1)

            def exponentials(b, j):
                if j == 0:
                    act.wait_ge(expbias_done, b + 1)
                    wait(act, rowsum_done, b)
                wait(act, pT_done, tiles(b, j - 2, NQ - 1))
                for q in range(NQ):
                    nc.scalar.activation(probs[:, j % 2, q, :], S[:, j, q, :], ACT.Exp, bias=expbias[:, q:q + 1],
                                         scale=1.0 / TEMP, accum_out=blocksum[:, q, j:j + 1]).then_inc(exp_done, 1)

            def split_probs(b, j):
                for q in range(NQ):
                    act.wait_ge(pT_done, tiles(b, j, q))
                    wait(act, pv_done, tiles(b, j - 1, q))
                    nc.scalar.activation(pT_hi[:, q], psP[q][:], ACT.Copy).then_inc(phi_done, 1)

            def turn(i, scoring, weighing):
                if scoring:
                    split_queries(i)
                    split_keys(i, 0)
                if weighing:
                    exponentials(i - 1, 0)
                    split_values(i - 1, 0)
                for j in range(NJ):
                    if weighing:
                        if j + 1 < NJ:
                            exponentials(i - 1, j + 1)
                        split_probs(i - 1, j)
                    if j + 1 < NJ:
                        if scoring:
                            split_keys(i, j + 1)
                        if weighing:
                            split_values(i - 1, j + 1)
            turns(act, turn)

        @block.vector
        def _(dve):
            def split_queries(b):
                dve.wait_ge(qhi_done, b + 1)
                nc.vector.tensor_tensor(q_lo[:], XNT[:, :, bass.ds(b * (NQ * P), NQ * P)], q_hi[:].bitcast(F32),
                                        ALU.subtract).then_inc(qlo_done, 1)

            def split_keys(b, j):
                dve.wait_ge(khi_done, blocks(b, j))
                nc.vector.tensor_tensor(keysT_lo[:, j % 2], keysT_raw[:, j % 2], keysT_hi[:, j % 2].bitcast(F32),
                                        ALU.subtract).then_inc(klo_done, 1)

            def split_probs(b, j):
                for q in range(NQ):
                    dve.wait_ge(phi_done, tiles(b, j, q))
                    nc.vector.tensor_tensor(pT_lo[:, q], psP[q][:], pT_hi[:, q].bitcast(F32),
                                            ALU.subtract).then_inc(plo_done, 1)

            def split_values(b, j):
                dve.wait_ge(vhi_done, blocks(b, j))
                dve.wait_ge(vlo_done, blocks(b, j - 1))
                nc.vector.tensor_tensor(vals[:, j % 2, :, 1, :], vals_raw[:, j % 2],
                                        vals[:, j % 2, :, 0, :].bitcast(F32), ALU.subtract).then_inc(vlo_done, 1)

            def save_scores(b, j):
                for q in range(NQ):
                    dve.wait_ge(scores_done, tiles(b, j, q))
                    wait(dve, exp_done, tiles(b - 1, j, q))
                    nc.vector.tensor_scalar(S[:, j, q, :], psS[q][:], 1.0, None, ALU.mult, ALU.max,
                                            accum_out=blockmax[:, q, j:j + 1]).then_inc(scores_saved, 1)

            def row_maximum(b):
                dve.wait_ge(scores_saved, tiles(b, NJ - 1, NQ - 1))
                nc.vector.tensor_reduce(rowmax[:], blockmax[:], AX.X, ALU.max).then_inc(rowmax_done, 1)
                dve.wait_ge(rowmax_done, b + 1)
                wait(dve, exp_done, tiles(b, -1, NQ - 1))
                nc.vector.tensor_scalar(expbias[:], rowmax[:], -1.0 / TEMP, None, ALU.mult).then_inc(expbias_done, 1)

            def row_sums(b):
                dve.wait_ge(exp_done, tiles(b, NJ - 1, NQ - 1))
                nc.vector.tensor_reduce(rowsum[:], blocksum[:], AX.X, ALU.add).then_inc(rowsum_done, 1)
                dve.wait_ge(rowsum_done, b + 1)
                nc.vector.reciprocal(rinv[:], rowsum[:]).then_inc(rinv_done, 1)

            def outputs(b):
                dve.wait_ge(rinv_done, b + 1)
                for q in range(NQ):
                    dve.wait_ge(pv_done, tiles(b, NJ - 1, q))
                    nc.vector.scalar_tensor_tensor(olo[:, q], psO[q][:, D:2 * D], rinv[:, q:q + 1], bias[:],
                                                   ALU.mult, ALU.add).then_inc(olo_done, 1)
                for q in range(NQ):
                    dve.wait_ge(olo_done, NQ * b + q + 1)
                    nc.vector.scalar_tensor_tensor(O[:, bass.ds(b * NQ + q, 1), :].rearrange("p a d -> p (a d)"),
                                                   psO[q][:, 0:D], rinv[:, q:q + 1], olo[:, q],
                                                   ALU.mult, ALU.add).then_inc(o_done, 1)

            dve.wait_ge(bias_in, 16)

            def turn(i, scoring, weighing):
                if scoring:
                    split_queries(i)
                    split_keys(i, 0)
                else:
                    split_values(i - 1, 0)
                for j in range(NJ):
                    if weighing:
                        split_probs(i - 1, j)
                    if scoring:
                        if j + 1 < NJ:
                            split_keys(i, j + 1)
                        save_scores(i, j)
                    elif j + 1 < NJ:
                        split_values(i - 1, j + 1)
                    if weighing and j == NJ - 2:
                        row_sums(i - 1)
                if scoring:
                    row_maximum(i)
                if weighing:
                    outputs(i - 1)
            turns(dve, turn)

        @block.gpsimd
        def _(pool):
            def apply_mask(b, j):
                pool.wait_ge(mask_in[j % 2], slot_loads(b, j))
                for q in range(NQ):
                    pool.wait_ge(exp_done, tiles(b, j, q))
                    nc.gpsimd.tensor_tensor(probs[:, j % 2, q, :], probs[:, j % 2, q, :], mask[:, j % 2, q, :],
                                            ALU.mult).then_inc(masked, 1)

            def split_values(b, j):
                pool.wait_ge(vhi_done, blocks(b, j))
                nc.gpsimd.tensor_tensor(vals[:, j % 2, :, 1, :], vals_raw[:, j % 2],
                                        vals[:, j % 2, :, 0, :].bitcast(F32), ALU.subtract).then_inc(vlo_done, 1)

            def turn(i, scoring, weighing):
                if weighing:
                    for j in range(NJ):
                        apply_mask(i - 1, j)
                        if scoring:
                            split_values(i - 1, j)
            turns(pool, turn)

        @block.tensor
        def _(pe):
            def transpose_probs(b, j):
                for q in range(NQ):
                    pe.wait_ge(masked, tiles(b, j, q))
                    wait(pe, phi_done, tiles(b, j - 1, q))
                    wait(pe, plo_done, tiles(b, j - 1, q))
                    for c in range(KC):
                        last = nc.tensor.transpose(psP[q][:, c, :], probs[:, j % 2, q, c * P:(c + 1) * P], ident[:])
                    last.then_inc(pT_done, 1)

            def scores(b, j):
                if j == 0:
                    pe.wait_ge(qlo_done, b + 1)
                pe.wait_ge(klo_done, blocks(b, j))
                for q in range(NQ):
                    wait(pe, scores_saved, tiles(b, j - 1, q))
                    n = 0
                    for a, k in ((q_hi, keysT_hi), (q_lo, keysT_hi), (q_hi, keysT_lo)):
                        for c in range(DC):
                            last = nc.tensor.matmul(psS[q][:], a[:, c, q * P:(q + 1) * P], k[:, j % 2, c, :],
                                                    start=(n == 0), stop=(n == 3 * DC - 1))
                            n += 1
                    last.then_inc(scores_done, 1)

            def weigh(b, j):
                pe.wait_ge(vlo_done, blocks(b, j))
                for q in range(NQ):
                    pe.wait_ge(plo_done, tiles(b, j, q))
                    if j == 0:
                        wait(pe, o_done, NQ * b)
                    for c in range(KC):
                        wide_first = j == 0 and c == 0
                        for wide in ((True, False) if wide_first else (False, True)):
                            if wide:
                                last = nc.tensor.matmul(psO[q][:], pT_hi[:, q, c, :], vals[:, j % 2, c, :, :],
                                                        start=wide_first, stop=(j == NJ - 1 and c == KC - 1),
                                                        skip_group_check=True)
                            else:
                                last = nc.tensor.matmul(psO[q][:, 0:D], pT_lo[:, q, c, :], vals[:, j % 2, c, 0, :],
                                                        start=False, stop=False, skip_group_check=True)
                    last.then_inc(pv_done, 1)

            def turn(i, scoring, weighing):
                for j in range(NJ):
                    if weighing:
                        transpose_probs(i - 1, j)
                    if scoring:
                        scores(i, j)
                    if weighing:
                        weigh(i - 1, j)
            turns(pe, turn)


def self_attention(nc, X, wqkv_dram, pick_dram, wout_dram, bout_dram, ident):
    HEADS, DH = 16, 16
    NT, D = X.shape[1], X.shape[2]
    DC = D // P
    SQ = 2 * P
    NQ = SQ // P
    B = NT // NQ
    PAIRS = HEADS // 2
    QUADS = HEADS // 4
    ROWS = 4 * DH
    SCALE = float(DH) ** -0.5
    RING = 4

    PHI_LAG, PV_LAG, COPY_LAG, BACK_LAG, NORM_LAG = 1, 3, 5, 6, 9
    TURN_X, QK, TURN_O, PROJECT_O = 1, (3, 4), 7, 9
    TURN_QK = (7, 10, 13, 16)
    MAXIMA = (8, 11, 14, 17)
    VALUES, SPLIT_VALUES = 11, (12, 19)
    TURN_M = (14, 20)

    with ExitStack() as ctx:
        def sb(name, shape, dt=F32):
            return ctx.enter_context(nc.sbuf_tensor(f"sa_{name}", shape, dt))

        def sem(name):
            return ctx.enter_context(nc.semaphore(f"sa_{name}"))

        w_raw = sb("w_raw", [P, DC, 3 * D])
        w_hi = sb("w_hi", [P, DC, 3 * D], F32R)
        w_lo = sb("w_lo", [P, DC, 3 * D], F32R)
        wo_raw = sb("wo_raw", [P, DC, D])
        wo_hi = sb("wo_hi", [P, DC, D], F32R)
        wo_lo = sb("wo_lo", [P, DC, D], F32R)
        bias = sb("bias", [P, 1, D])
        pick = sb("pick", [P, HEADS])
        sel = sb("sel", [P, HEADS, P], F32R)
        identr = sb("identr", [P, P], F32R)
        stats = sb("stats", [P, NT, 6])
        mv = sb("mv", [P, NT, 2])
        vare = sb("vare", [P, NT])
        std = sb("std", [P, NT])
        rstd = sb("rstd", [P, NT])
        newt = sb("newt", [P, NT])
        XN = sb("XN", [P, NQ, D])
        x_hi = sb("x_hi", [P, DC, SQ], F32R)
        x_lo = sb("x_lo", [P, DC, SQ], F32R)
        q4 = sb("q4", [P, NQ, HEADS, 4, DH], F32R)
        k4 = sb("k4", [P, NQ, HEADS, 4, DH], F32R)
        v4 = sb("v4", [P, NQ, HEADS, 2 * ROWS], F32R)
        qz = sb("qz", [P, HEADS, SQ], F32R)
        kT = sb("kT", [P, PAIRS, SQ], F32R)
        negmax = sb("negmax", [P, NQ, HEADS])
        mz = sb("mz", [P, 2, NQ, P], F32R)
        mT = sb("mT", [P, 2, SQ], F32R)
        v_raw = sb("v_raw", [P, NQ, D])
        probs = sb("probs", [P, RING, NQ, SQ])
        p_hi = sb("p_hi", [P, RING, NQ, SQ], F32R)
        p_lo = sb("p_lo", [P, RING, NQ, SQ], F32R)
        aT = sb("aT", [P, 2, SQ])
        rinv = sb("rinv", [P, NQ * 4])
        num = sb("num", [P, NQ * 4, DH])
        O = sb("O", [P, NQ, D])
        oT_hi = sb("oT_hi", [P, DC, SQ], F32R)
        oT_lo = sb("oT_lo", [P, DC, SQ], F32R)

        bank = [ctx.enter_context(nc.psum_tensor(f"sa_bank{k}", [P, BANK], F32)) for k in range(8)]
        psX, psOT, psP, psM = bank[2], bank[2], bank[2], bank[2]
        psQK, psV, psT, psS = bank[0:2], bank[2], bank[0:2], bank[0:2]
        psE, psO, psB = bank[3:5], bank[5], bank[6:8]

        w_in = sem("w_in")
        wo_in = sem("wo_in")
        bias_in = sem("bias_in")
        pick_in = sem("pick_in")
        whi_done = sem("whi_done")
        wlo_done = sem("wlo_done")
        wohi_done = sem("wohi_done")
        wolo_done = sem("wolo_done")
        constants = sem("constants")
        stats_done = sem("stats_done")
        mv_done = sem("mv_done")
        vare_done = sem("vare_done")
        std_done = sem("std_done")
        newton = sem("newton")
        xn_done = sem("xn_done")
        biased = sem("biased")
        xturned = sem("xturned")
        xhi_done = sem("xhi_done")
        xlo_done = sem("xlo_done")
        qk_done = sem("qk_done")
        v_done = sem("v_done")
        qkhi_done = sem("qkhi_done")
        qklo_done = sem("qklo_done")
        vraw_done = sem("vraw_done")
        vhi_done = sem("vhi_done")
        vlo_done = sem("vlo_done")
        turned = sem("turned")
        kT_done = sem("kT_done")
        qz_done = sem("qz_done")
        qz1_done = sem("qz1_done")
        smax_done = sem("smax_done")
        max_done = sem("max_done")
        mhi_done = sem("mhi_done")
        mlo_done = sem("mlo_done")
        m_turned = sem("m_turned")
        mT_done = sem("mT_done")
        st_done = sem("st_done")
        exp_done = sem("exp_done")
        phi_done = sem("phi_done")
        plo_done = sem("plo_done")
        pv_done = sem("pv_done")
        aT_done = sem("aT_done")
        back_done = sem("back_done")
        rinv_done = sem("rinv_done")
        num_done = sem("num_done")
        norm_done = sem("norm_done")
        oturned = sem("oturned")
        othi_done = sem("othi_done")
        otlo_done = sem("otlo_done")
        projected = sem("projected")
        added = sem("added")
        CONSTANTS = 6
        ROUNDS = NQ * PAIRS

        def turns(eng, turn):
            turn(0, True, False, False)
            turn(1, True, True, False)
            with eng.Fori(2, B) as i:
                turn(i, True, True, True)
            turn(B, False, True, True)
            turn(B + 1, False, False, True)

        def behind(i, k, lag, heads, finish):
            if k >= lag:
                return (i - 1, k - lag) if heads else None
            return (i - 2, k - lag + HEADS) if finish else None

        def prepared(i, k, slots, start, heads):
            if k in slots and start:
                return i, slots.index(k)
            if k + HEADS in slots and heads:
                return i - 1, slots.index(k + HEADS)
            return None

        def ring_free(b, h):
            return HEADS * b + h + 1 - RING

        def rounds_of(i, k, start, heads):
            for half in range(2):
                found = prepared(i, k, [s + half for s in MAXIMA], start, heads)
                if found:
                    b, u = found
                    for t in range(NQ):
                        yield b, 4 * u + 2 * half + t, t, 2 * u + half

        def values_of(x, half, s):
            cols = slice(half * D // 2, (half + 1) * D // 2)
            return x[:, :, cols].rearrange("p t (g s d) -> p t g s d", s=2, d=DH)[:, :, :, s, :]

        def value_columns(half, s, first):
            heads_of = slice(half * HEADS // 2 + s, (half + 1) * HEADS // 2, 2)
            return v4[:, :, heads_of, s * ROWS + first:s * ROWS + first + DH]

        def copy_queries(instruction, u, s, *function):
            rows = slice(ROWS * s, ROWS * (s + 1))
            return instruction(qz[rows, 4 * u + s:4 * u + s + 3:2, :],
                               psT[1][rows, :].rearrange("p (g q) -> p g q", g=2), *function)

        block = ctx.enter_context(nc.Block())

        @block.sync
        def _(sp):
            sp.dma_start(w_raw[:], wqkv_dram.rearrange("(c p) n -> p c n", p=P)).then_inc(w_in, 16)
            sp.dma_start(pick[:], pick_dram).then_inc(pick_in, 16)
            sp.dma_start(wo_raw[:], wout_dram.rearrange("(c p) n -> p c n", p=P)).then_inc(wo_in, 16)
            sp.dma_start(bias[:], bout_dram.rearrange("(a b n) -> a b n", a=1, b=1).to_broadcast([P, 1, D])).then_inc(bias_in, 16)

        @block.gpsimd
        def _(pool):
            nc.gpsimd.memset(qz[:].bitcast(F32), 0.0).then_inc(constants, 1)
            nc.gpsimd.memset(mz[:].bitcast(F32), 0.0).then_inc(constants, 1)
            for s in range(2):
                other = slice((1 - s) * ROWS, (2 - s) * ROWS)
                nc.gpsimd.memset(v4[:, :, s::2, other].bitcast(F32), 0.0)
                ones = slice(s * ROWS + 2 * DH, (s + 1) * ROWS)
                last = nc.gpsimd.memset(v4[:, :, s::2, ones].bitcast(F32), 1.0)
                last.then_inc(constants, 1)
            pool.wait_ge(bias_in, 16)

            def turn(i, start, heads, finish):
                for k in range(HEADS):
                    if start and k == 1:
                        pool.wait_ge(xn_done, NQ * (i + 1))
                        x = X[:, bass.ds(NQ * i, NQ), :]
                        nc.gpsimd.tensor_tensor(x, x, bias[:].to_broadcast([P, NQ, D]), ALU.add).then_inc(biased, 1)
                    found = behind(i, k, PHI_LAG, heads, finish)
                    if found:
                        b, h = found
                        r = h % RING
                        pool.wait_ge(phi_done, HEADS * b + h + 1)
                        wait(pool, pv_done, ring_free(b, h))
                        nc.gpsimd.tensor_tensor(p_lo[:, r], probs[:, r], p_hi[:, r].bitcast(F32),
                                                ALU.subtract).then_inc(plo_done, 1)
            turns(pool, turn)

        @block.scalar
        def _(act):
            act.wait_ge(vare_done, 1)
            nc.scalar.activation(std[:], vare[:], ACT.Sqrt).then_inc(std_done, 1)
            act.wait_ge(w_in, 16)
            nc.scalar.activation(w_hi[:], w_raw[:], ACT.Copy).then_inc(whi_done, 1)

            def turn(i, start, heads, finish):
                for k in range(HEADS):
                    found = behind(i, k, COPY_LAG, heads, finish)
                    if found and found[1] % 2 == 0:
                        b, g = found[0], found[1] // 2
                        act.wait_ge(pv_done, HEADS * b + 2 * g + 2)
                        wait(act, back_done, PAIRS * b + g - 1)
                        nc.scalar.activation(aT[:, g % 2, :], psO[:, 0:SQ], ACT.Copy).then_inc(aT_done, 1)
                    if heads:
                        b = i - 1
                        act.wait_ge(st_done, HEADS * b + k + 1)
                        wait(act, plo_done, ring_free(b, k))
                        nc.scalar.activation(probs[:, k % RING], psE[k % 2][:].rearrange("p (t q) -> p t q", t=NQ),
                                             ACT.Exp, scale=SCALE).then_inc(exp_done, 1)
                    found = behind(i, k, PHI_LAG, heads, finish)
                    if found:
                        b, h = found
                        act.wait_ge(exp_done, HEADS * b + h + 1)
                        wait(act, pv_done, ring_free(b, h))
                        nc.scalar.activation(p_hi[:, h % RING], probs[:, h % RING], ACT.Copy).then_inc(phi_done, 1)
                    if start and k == TURN_X:
                        act.wait_ge(xturned, i + 1)
                        nc.scalar.activation(x_hi[:], psX[:].rearrange("p (c q) -> p c q", c=DC), ACT.Copy).then_inc(xhi_done, 1)
                    if finish and k == TURN_O:
                        act.wait_ge(oturned, i - 1)
                        nc.scalar.activation(oT_hi[:], psOT[:].rearrange("p (c q) -> p c q", c=DC), ACT.Copy).then_inc(othi_done, 1)
                    if start and k in QK:
                        t = QK.index(k)
                        act.wait_ge(qk_done, NQ * i + t + 1)
                        for half, (x4, slots) in enumerate(((q4, slice(0, 2)), (k4, slice(0, 4, 2)))):
                            src = psQK[t][:, half * D:(half + 1) * D].rearrange("p (h a d) -> p h a d", a=1, d=DH)
                            nc.scalar.activation(x4[:, t, :, slots, :], src.to_broadcast([P, HEADS, 2, DH]),
                                                 ACT.Copy).then_inc(qkhi_done, 1)
                    found = prepared(i, k, TURN_QK, start, heads)
                    if found:
                        b, u = found
                        act.wait_ge(turned, PAIRS * b + 2 * u + 2)
                        if isinstance(i, int) and i == 0 and u == 0:
                            act.wait_ge(constants, CONSTANTS)
                        copy_queries(nc.scalar.activation, u, 0, ACT.Copy).then_inc(qz_done, 1)
                    if start and k == VALUES:
                        act.wait_ge(v_done, i + 1)
                        wait(act, vlo_done, 4 * i)
                        nc.scalar.activation(v_raw[:], psV[:].rearrange("p (t d) -> p t d", t=NQ), ACT.Copy).then_inc(vraw_done, 1)
                    found = prepared(i, k, SPLIT_VALUES, start, heads)
                    if found:
                        b, half = found
                        act.wait_ge(vraw_done, b + 1)
                        wait(act, pv_done, HEADS * (b - 1) + (half + 1) * HEADS // 2)
                        for s in range(2):
                            nc.scalar.activation(value_columns(half, s, 0), values_of(v_raw, half, s), ACT.Copy).then_inc(vhi_done, 1)
                    found = prepared(i, k, TURN_M, start, heads)
                    if found:
                        b, half = found
                        act.wait_ge(m_turned, 2 * b + half + 1)
                        nc.scalar.activation(mT[:, half, :], psM[:, 0:SQ], ACT.Copy).then_inc(mT_done, 1)
                if isinstance(i, int) and i == 0:
                    act.wait_ge(wo_in, 16)
                    nc.scalar.activation(wo_hi[:], wo_raw[:], ACT.Copy).then_inc(wohi_done, 1)
            turns(act, turn)

        @block.vector
        def _(dve):
            def statistics():
                for t in range(NT):
                    nc.vector.bn_stats(stats[:, t, :], X[:, t, :]).then_inc(stats_done, 1)
                for t in range(NT):
                    dve.wait_ge(stats_done, t + 1)
                    nc.vector.bn_aggr(mv[:, t, :], stats[:, t, :]).then_inc(mv_done, 1)
                dve.wait_ge(mv_done, NT)
                nc.vector.tensor_scalar(vare[:], mv[:, :, 1], EPS, None, ALU.add).then_inc(vare_done, 1)
                dve.wait_ge(std_done, 1)
                nc.vector.reciprocal(rstd[:], std[:]).then_inc(newton, 1)
                dve.wait_ge(newton, 1)
                nc.vector.tensor_tensor(newt[:], rstd[:], rstd[:], ALU.mult).then_inc(newton, 1)
                dve.wait_ge(newton, 2)
                nc.vector.tensor_tensor(newt[:], newt[:], vare[:], ALU.mult).then_inc(newton, 1)
                dve.wait_ge(newton, 3)
                nc.vector.tensor_scalar(newt[:], newt[:], -0.5, 1.5, ALU.mult, ALU.add).then_inc(newton, 1)
                dve.wait_ge(newton, 4)
                nc.vector.tensor_tensor(rstd[:], rstd[:], newt[:], ALU.mult).then_inc(newton, 1)
                dve.wait_ge(newton, 5)

            def layernorm(b):
                wait(dve, xturned, b)
                for t in range(NQ):
                    nc.vector.tensor_scalar(XN[:, t, :], X[:, bass.ds(NQ * b + t, 1), :].rearrange("p a d -> p (a d)"),
                                            mv[:, bass.ds(NQ * b + t, 1), 0], rstd[:, bass.ds(NQ * b + t, 1)],
                                            ALU.subtract, ALU.mult).then_inc(xn_done, 1)

            def normalize(b, quad):
                n = QUADS * b + quad + 1
                dve.wait_ge(back_done, PAIRS * b + 2 * quad + 2)
                out = psB[quad % 2][:].rearrange("p (n r) -> p n r", r=ROWS)
                wait(dve, norm_done, n - 1)
                nc.vector.reciprocal(rinv[:], out[:, :, 2 * DH]).then_inc(rinv_done, 1)
                nc.vector.tensor_reduce(num[:], out[:, :, 0:2 * DH].rearrange("p n (u d) -> p n d u", u=2),
                                        AX.X, ALU.add).then_inc(num_done, 1)
                if quad == 0:
                    wait(dve, oturned, b)
                dve.wait_ge(rinv_done, n)
                dve.wait_ge(num_done, n)
                dst = O[:, :, quad * 4 * DH:(quad + 1) * 4 * DH].rearrange("p t (h d) -> p t h d", d=DH)
                scale = rinv[:].rearrange("p (t h a) -> p t h a", t=NQ, a=1).to_broadcast([P, NQ, 4, DH])
                nc.vector.tensor_tensor(dst, num[:].rearrange("p (t h) d -> p t h d", t=NQ), scale, ALU.mult).then_inc(norm_done, 1)

            nc.vector.tensor_copy(identr[:], ident[:]).then_inc(constants, 1)
            def turn(i, start, heads, finish):
                if isinstance(i, int) and i == 0:
                    statistics()
                if start:
                    layernorm(i)
                if isinstance(i, int) and i == 0:
                    dve.wait_ge(whi_done, 1)
                    nc.vector.tensor_tensor(w_lo[:], w_raw[:], w_hi[:].bitcast(F32), ALU.subtract).then_inc(wlo_done, 1)
                    dve.wait_ge(pick_in, 16)
                    nc.vector.tensor_copy(sel[:], pick[:].rearrange("p (h a) -> p h a", a=1).to_broadcast([P, HEADS, P])).then_inc(constants, 1)
                for k in range(HEADS):
                    if start and k == TURN_X:
                        dve.wait_ge(xhi_done, i + 1)
                        nc.vector.tensor_tensor(x_lo[:], psX[:].rearrange("p (c q) -> p c q", c=DC), x_hi[:].bitcast(F32),
                                                ALU.subtract).then_inc(xlo_done, 1)
                    if finish and k == TURN_O:
                        dve.wait_ge(othi_done, i - 1)
                        nc.vector.tensor_tensor(oT_lo[:], psOT[:].rearrange("p (c q) -> p c q", c=DC), oT_hi[:].bitcast(F32),
                                                ALU.subtract).then_inc(otlo_done, 1)
                    if finish and k == PROJECT_O + 1:
                        b = i - 2
                        dve.wait_ge(projected, b + 1)
                        dve.wait_ge(biased, b + 1)
                        x = X[:, bass.ds(NQ * b, NQ), :]
                        nc.vector.tensor_tensor(x, psP[:].rearrange("p (t e) -> p t e", t=NQ), x, ALU.add).then_inc(added, 1)
                    if start and k in QK:
                        t = QK.index(k)
                        dve.wait_ge(qkhi_done, 2 * (NQ * i + t) + 2)
                        for half, (x4, hi, slots) in enumerate(((q4, 0, slice(2, 4)), (k4, 0, slice(1, 4, 2)))):
                            src = psQK[t][:, half * D:(half + 1) * D].rearrange("p (h a d) -> p h a d", a=1, d=DH)
                            nc.vector.tensor_tensor(x4[:, t, :, slots, :], src.to_broadcast([P, HEADS, 2, DH]),
                                                    x4[:, t, :, hi:hi + 1, :].bitcast(F32).to_broadcast([P, HEADS, 2, DH]),
                                                    ALU.subtract).then_inc(qklo_done, 1)
                    found = prepared(i, k, TURN_QK, start, heads)
                    if found:
                        b, u = found
                        dve.wait_ge(turned, PAIRS * b + 2 * u + 1)
                        nc.vector.tensor_copy(kT[:, 2 * u:2 * u + 2, :], psT[0][:].rearrange("p (g k) -> p g k", g=2)).then_inc(kT_done, 1)
                        dve.wait_ge(turned, PAIRS * b + 2 * u + 2)
                        copy_queries(nc.vector.tensor_copy, u, 1).then_inc(qz1_done, 1)
                    for b, n, t, g in rounds_of(i, k, start, heads):
                        dve.wait_ge(smax_done, ROUNDS * b + n + 1)
                        nc.vector.tensor_reduce(negmax[:, t, 2 * g:2 * g + 2],
                                                psS[n % 2][:].rearrange("p (h k) -> p h k", h=2),
                                                AX.X, ALU.max, negate=True).then_inc(max_done, 1)
                    found = prepared(i, k, (MAXIMA[1] + 1, MAXIMA[3] + 1), start, heads)
                    if found:
                        b, half = found
                        own = slice(half * HEADS // 2, (half + 1) * HEADS // 2)
                        low = slice(HEADS + half * HEADS // 2, HEADS + (half + 1) * HEADS // 2)
                        dve.wait_ge(max_done, ROUNDS * b + (half + 1) * ROUNDS // 2)
                        wait(dve, m_turned, 2 * b + half - 1)
                        nc.vector.tensor_copy(mz[:, half, :, own], negmax[:, :, own]).then_inc(mhi_done, 1)
                        dve.wait_ge(mhi_done, 2 * b + half + 1)
                        nc.vector.tensor_tensor(mz[:, half, :, low], negmax[:, :, own], mz[:, half, :, own].bitcast(F32),
                                                ALU.subtract).then_inc(mlo_done, 1)
                    found = prepared(i, k, SPLIT_VALUES, start, heads)
                    if found:
                        b, half = found
                        dve.wait_ge(vhi_done, 4 * b + 2 * half + 2)
                        for s in range(2):
                            nc.vector.tensor_tensor(value_columns(half, s, DH), values_of(v_raw, half, s),
                                                    value_columns(half, s, 0).bitcast(F32), ALU.subtract).then_inc(vlo_done, 1)
                    found = behind(i, k, NORM_LAG, heads, finish)
                    if found and found[1] % 4 == 0:
                        normalize(found[0], found[1] // 4)
                if isinstance(i, int) and i == 0:
                    dve.wait_ge(wohi_done, 1)
                    nc.vector.tensor_tensor(wo_lo[:], wo_raw[:], wo_hi[:].bitcast(F32), ALU.subtract).then_inc(wolo_done, 1)
            turns(dve, turn)

        @block.tensor
        def _(pe):
            def project_qkv(t, ps, cols):
                n = 0
                for x, w in ((x_hi, w_hi), (x_lo, w_hi), (x_hi, w_lo)):
                    for c in range(DC):
                        last = nc.tensor.matmul(ps, x[:, c, t * P:(t + 1) * P], w[:, c, cols],
                                                start=(n == 0), stop=(n == 3 * DC - 1), skip_group_check=True)
                        n += 1
                return last

            def turn(i, start, heads, finish):
                for k in range(HEADS):
                    if heads:
                        b, h = i - 1, k
                        if k in (0, HEADS // 2):
                            pe.wait_ge(mT_done, 2 * b + k // (HEADS // 2) + 1)
                        wait(pe, exp_done, HEADS * b + h - 1)
                        for t in range(NQ):
                            ps = psE[h % 2][:, t * SQ:(t + 1) * SQ]
                            nc.tensor.matmul(ps, kT[:, h // 2, t * P:(t + 1) * P], qz[:, h, :], start=True, stop=False)
                            last = nc.tensor.matmul(ps, sel[:, h, :], mT[:, h // (HEADS // 2), :], start=False, stop=True)
                        last.then_inc(st_done, 1)
                    if start and k == TURN_X:
                        pe.wait_ge(xn_done, NQ * (i + 1))
                        wait(pe, mT_done, 2 * i - 1)
                        for c in range(DC):
                            for t in range(NQ):
                                last = nc.tensor.transpose(psX[:, c * SQ + t * P:c * SQ + (t + 1) * P],
                                                           XN[:, t, c * P:(c + 1) * P], ident[:])
                        last.then_inc(xturned, 1)
                    if finish and k == TURN_O:
                        b = i - 2
                        pe.wait_ge(norm_done, QUADS * (b + 1))
                        pe.wait_ge(mT_done, 2 * (min(i, B) if isinstance(i, int) else i))
                        for c in range(DC):
                            for t in range(NQ):
                                last = nc.tensor.transpose(psOT[:, c * SQ + t * P:c * SQ + (t + 1) * P],
                                                           O[:, t, c * P:(c + 1) * P], ident[:])
                        last.then_inc(oturned, 1)
                    if finish and k == PROJECT_O:
                        b = i - 2
                        pe.wait_ge(otlo_done, b + 1)
                        pe.wait_ge(wolo_done, 1)
                        for t in range(NQ):
                            n = 0
                            for a, w in ((oT_hi, wo_hi), (oT_lo, wo_hi), (oT_hi, wo_lo)):
                                for c in range(DC):
                                    last = nc.tensor.matmul(psP[:, t * D:(t + 1) * D], a[:, c, t * P:(t + 1) * P], w[:, c, :],
                                                            start=(n == 0), stop=(n == 3 * DC - 1))
                                    n += 1
                        last.then_inc(projected, 1)
                    if start and k in QK:
                        t = QK.index(k)
                        pe.wait_ge(xlo_done, i + 1)
                        if t == 0 and isinstance(i, int) and i == 0:
                            pe.wait_ge(wlo_done, 1)
                        wait(pe, max_done, ROUNDS * i)
                        project_qkv(t, psQK[t][:], slice(0, 2 * D)).then_inc(qk_done, 1)
                    found = prepared(i, k, TURN_QK, start, heads)
                    if found:
                        b, u = found
                        if u == 0 and isinstance(i, int) and i == 0:
                            pe.wait_ge(constants, CONSTANTS)
                        pe.wait_ge(qklo_done, 2 * NQ * (b + 1))
                        wait(pe, max_done, ROUNDS * b + 4 * u)
                        for half, x4 in enumerate((k4, q4)):
                            for g in range(2):
                                for t in range(NQ):
                                    pair = x4[:, t, 4 * u + 2 * g:4 * u + 2 * g + 2].rearrange("p h a d -> p (h a d)")
                                    last = nc.tensor.transpose(
                                        psT[half][:, (NQ * g + t) * P:(NQ * g + t + 1) * P].bitcast(F32R), pair, identr[:])
                            last.then_inc(turned, 1)
                    for b, n, t, g in rounds_of(i, k, start, heads):
                        pe.wait_ge(kT_done, QUADS * b + g // 2 + 1)
                        pe.wait_ge(qz_done, QUADS * b + g // 2 + 1)
                        pe.wait_ge(qz1_done, QUADS * b + g // 2 + 1)
                        wait(pe, max_done, ROUNDS * b + n - 1)
                        for s in range(2):
                            last = nc.tensor.matmul(psS[n % 2][:, s * SQ:(s + 1) * SQ], qz[:, 2 * g + s, t * P:(t + 1) * P],
                                                    kT[:, g, :], start=True, stop=True)
                        last.then_inc(smax_done, 1)
                    if start and k == VALUES:
                        wait(pe, mT_done, 2 * i)
                        if finish:
                            pe.wait_ge(added, i - 1)
                        for t in range(NQ):
                            last = project_qkv(t, psV[:, t * D:(t + 1) * D], slice(2 * D, 3 * D))
                        last.then_inc(v_done, 1)
                    found = behind(i, k, PV_LAG, heads, finish)
                    if found:
                        b, h = found
                        g = h // 2
                        pe.wait_ge(plo_done, HEADS * b + h + 1)
                        if h in (0, HEADS // 2):
                            pe.wait_ge(vlo_done, 4 * b + 2 * (h // (HEADS // 2)) + 2)
                        if h % 2 == 0:
                            wait(pe, aT_done, PAIRS * b + g)
                        n = 4 * (h % 2)
                        for part in (p_hi, p_lo):
                            for t in range(NQ):
                                last = nc.tensor.matmul(psO[:, 0:SQ], v4[:, t, h, :], part[:, h % RING, t, :],
                                                        start=(n == 0), stop=(n == 7))
                                n += 1
                        last.then_inc(pv_done, 1)
                    found = behind(i, k, BACK_LAG, heads, finish)
                    if found and found[1] % 2 == 0:
                        b, g = found[0], found[1] // 2
                        pe.wait_ge(aT_done, PAIRS * b + g + 1)
                        if g % 2 == 0:
                            wait(pe, norm_done, QUADS * b + g // 2 - 1)
                        for t in range(NQ):
                            last = nc.tensor.transpose(psB[(g // 2) % 2][:, (2 * t + g % 2) * P:(2 * t + g % 2 + 1) * P],
                                                       aT[:, g % 2, t * P:(t + 1) * P], ident[:])
                        last.then_inc(back_done, 1)
                    found = prepared(i, k, TURN_M, start, heads)
                    if found:
                        b, half = found
                        pe.wait_ge(mlo_done, 2 * b + half + 1)
                        if half == 0:
                            pe.wait_ge(vraw_done, b + 1)
                        else:
                            pe.wait_ge(mT_done, 2 * b + 1)
                            if start:
                                pe.wait_ge(xlo_done, i + 1)
                        for t in range(NQ):
                            last = nc.tensor.transpose(psM[:, t * P:(t + 1) * P].bitcast(F32R), mz[:, half, t, :], identr[:])
                        last.then_inc(m_turned, 1)
            turns(pe, turn)


def routed_ffn(nc, X, xT_hi, xT_lo, w, out_v, ident):
    NT, D = X.shape[1], X.shape[2]
    DC = D // P
    T = NT * P
    E = 64
    NG = 64
    TQ = T // NG
    BUDGET = TQ * 16
    NC = w["up_gate"].shape[0]
    HT = T // 2
    TH = T // BANK
    BIG = 3.0e38

    with ExitStack() as ctx:
        def sb(name, shape, dt=F32, ctx=ctx):
            return ctx.enter_context(nc.sbuf_tensor(f"ff_{name}", shape, dt))

        def sem(name, ctx=ctx):
            return ctx.enter_context(nc.semaphore(f"ff_{name}"))

        G = sb("G", [P, NC, T])
        FT = sb("FT", [E, T])
        fs_dram = nc.dram_tensor("fs_scratch", (E, T), F32, kind="Internal").ap()
        fnorm = sb("fnorm", [P, NT])

        with ExitStack() as one:
            def sb1(name, shape, dt=F32):
                return sb(name, shape, dt, one)

            def sem1(name):
                return sem(name, one)

            wr_raw = sb1("wr_raw", [P, DC, E])
            wr_hi = sb1("wr_hi", [P, DC, E], F32R)
            wr_lo = sb1("wr_lo", [P, DC, E], F32R)
            br = sb1("br", [E, 1])
            bup = sb1("bup", [P, NC])
            bgate = sb1("bgate", [P, NC])
            diag = sb1("diag", [P, E])
            tq_of = sb1("tq_of", [P, TQ // 2])
            w_raw = sb1("w_raw", [P, 2, 2, DC, P])
            w_hi = sb1("w_hi", [P, 2, 2, DC, P], F32R)
            w_lo = sb1("w_lo", [P, 2, 2, DC, P], F32R)
            gate = sb1("gate", [P, 2, T])
            buf_a = sb1("buf_a", [P, T])
            buf_b = sb1("buf_b", [P, T])
            buf_c = sb1("buf_c", [P, T])
            buf_d = sb1("buf_d", [P, T])
            RT = sb1("RT", [E, T])
            R = sb1("R", [P, NT, E])
            sort_x = sb1("sort_x", [P, HT])
            sort_y = sb1("sort_y", [P, HT])
            small = sb1("small", [P, 16, 8])
            ones = sb1("ones", [P, P])
            rowcount = sb1("rowcount", [P, E])
            psU = one.enter_context(nc.psum_tensor("ff_psU", [P, T], F32))
            psG = one.enter_context(nc.psum_tensor("ff_psG", [P, T], F32))
            psR = one.enter_context(nc.psum_tensor("ff_psR", [P, T], F32))
            psL = one.enter_context(nc.psum_tensor("ff_psL", [P, BANK], F32))
            psD = one.enter_context(nc.psum_tensor("ff_psD", [P, BANK], F32))

            small_in = sem1("small_in")
            w_in = [sem1(f"w_in{s}") for s in range(2)]
            wr_hi_done = sem1("wr_hi_done")
            wr_lo_done = sem1("wr_lo_done")
            ones_done = sem1("ones_done")
            whi_done = sem1("whi_done")
            wlo_done = sem1("wlo_done")
            up_done = sem1("up_done")
            gate_done = sem1("gate_done")
            silu_done = sem1("silu_done")
            biased_done = sem1("biased_done")
            gated = sem1("gated")
            logits_done = sem1("logits_done")
            logits_saved = sem1("logits_saved")
            logits_turned = sem1("logits_turned")
            shifted = sem1("shifted")
            router_exp = sem1("router_exp")
            scores_ready = sem1("scores_ready")
            scores_turned = sem1("scores_turned")
            step = sem1("step")
            spread_ready = sem1("spread_ready")
            spread_done = sem1("spread_done")
            kept_ready = sem1("kept_ready")
            fsum_done = sem1("fsum_done")
            fs_stored = sem1("fs_stored")

            SPREAD, SPREAD_MAX, SUM = 12, 16, 24

            block = one.enter_context(nc.Block())

            @block.sync
            def _(sp):
                sp.dma_start(wr_raw[:], w["router"].rearrange("(c p) e -> p c e", p=P)).then_inc(small_in, 16)
                for dst, src in ((br, "router_bias"), (bup, "up_bias"), (bgate, "gate_bias"), (diag, "diag"), (tq_of, "tq_of")):
                    sp.dma_start(dst[:], w[src]).then_inc(small_in, 16)

                def load(c):
                    wait(sp, whi_done, c - 1)
                    wait(sp, wlo_done, c - 1)
                    s = c % 2
                    sp.dma_start(w_raw[:, s], w["up_gate"][c]).then_inc(w_in[s], 16)

                load(0)
                load(1)
                with sp.Fori(1, NC // 2) as pair:
                    c = 2 * pair
                    for s in range(2):
                        sp.wait_ge(whi_done, c + s - 1)
                        sp.wait_ge(wlo_done, c + s - 1)
                        sp.dma_start(w_raw[:, s], w["up_gate"][c + s]).then_inc(w_in[s], 16)
                sp.wait_ge(kept_ready, 1)
                sp.dma_start(fs_dram, FT[:]).then_inc(fs_stored, 16)
                sp.wait_ge(fs_stored, 16)

            @block.scalar
            def _(act):
                def split(c, s):
                    act.wait_ge(w_in[s], 8 * (c - s) + 16)
                    wait(act, gate_done, c - 1)
                    nc.scalar.activation(w_hi[:, s], w_raw[:, s], ACT.Copy).then_inc(whi_done, 1)

                def gates(c, s):
                    act.wait_ge(up_done, c + 1)
                    nc.scalar.activation(G[:, bass.ds(c, 1), :].rearrange("p a t -> p (a t)"), psU[:], ACT.Silu,
                                         bias=bup[:, bass.ds(c, 1)]).then_inc(silu_done, 1)
                    act.wait_ge(gate_done, c + 1)
                    wait(act, gated, c - 1)
                    nc.scalar.activation(gate[:, s], psG[:], ACT.Identity, bias=bgate[:, bass.ds(c, 1)]).then_inc(biased_done, 1)

                act.wait_ge(small_in, 96)
                nc.scalar.activation(wr_hi[:], wr_raw[:], ACT.Copy).then_inc(wr_hi_done, 1)
                split(0, 0)
                act.wait_ge(logits_done, 1)
                nc.scalar.activation(buf_a[0:E, :], psR[0:E, :], ACT.Identity, bias=br[:]).then_inc(logits_saved, 1)
                split(1, 1)
                act.wait_ge(shifted, 1)
                nc.scalar.activation(R[:], R[:], ACT.Exp).then_inc(router_exp, 1)
                gates(0, 0)
                split(2, 0)
                gates(1, 1)
                with act.Fori(1, (NC - 2) // 2) as pair:
                    c = 2 * pair
                    split(c + 1, 1)
                    gates(c, 0)
                    split(c + 2, 0)
                    gates(c + 1, 1)
                split(NC - 1, 1)
                gates(NC - 2, 0)
                gates(NC - 1, 1)

            @block.gpsimd
            def _(pool):
                nc.gpsimd.memset(ones[:], 1.0).then_inc(ones_done, 1)

                def split(c, s):
                    pool.wait_ge(whi_done, c + 1)
                    nc.gpsimd.tensor_tensor(w_lo[:, s], w_raw[:, s], w_hi[:, s].bitcast(F32), ALU.subtract).then_inc(wlo_done, 1)

                def product(c, s):
                    pool.wait_ge(silu_done, c + 1)
                    pool.wait_ge(biased_done, c + 1)
                    row = G[:, bass.ds(c, 1), :].rearrange("p a t -> p (a t)")
                    nc.gpsimd.tensor_tensor(row, row, gate[:, s], ALU.mult).then_inc(gated, 1)

                split(0, 0)
                split(1, 1)
                product(0, 0)
                split(2, 0)
                product(1, 1)
                with pool.Fori(1, (NC - 2) // 2) as pair:
                    c = 2 * pair
                    split(c + 1, 1)
                    product(c, 0)
                    split(c + 2, 0)
                    product(c + 1, 1)
                split(NC - 1, 1)
                product(NC - 2, 0)
                product(NC - 1, 1)

            @block.tensor
            def _(pe):
                def hidden(c, s):
                    pe.wait_ge(wlo_done, c + 1)
                    for u, (ps, done, left) in enumerate(((psU, up_done, silu_done), (psG, gate_done, biased_done))):
                        wait(pe, left, c)
                        for h in range(TH):
                            cols = slice(h * BANK, (h + 1) * BANK)
                            n = 0
                            for a, b in ((w_hi, xT_hi), (w_hi, xT_lo), (w_lo, xT_hi)):
                                for k in range(DC):
                                    last = nc.tensor.matmul(ps[:, cols], a[:, s, u, k, :], b[:, k, cols],
                                                            start=(n == 0), stop=(n == 3 * DC - 1))
                                    n += 1
                        last.then_inc(done, 1)

                def run(first, last):
                    with pe.Fori(first // 2, last // 2) as pair:
                        c = 2 * pair
                        hidden(c, 0)
                        hidden(c + 1, 1)

                pe.wait_ge(wr_lo_done, 1)
                for h in range(TH):
                    cols = slice(h * BANK, (h + 1) * BANK)
                    n = 0
                    for a, b in ((wr_hi, xT_hi), (wr_hi, xT_lo), (wr_lo, xT_hi)):
                        for k in range(DC):
                            last = nc.tensor.matmul(psR[0:E, cols], a[:, k, :], b[:, k, cols],
                                                    start=(n == 0), stop=(n == 3 * DC - 1))
                            n += 1
                last.then_inc(logits_done, 1)
                pe.wait_ge(logits_saved, 1)
                for t in range(NT):
                    last = nc.tensor.transpose(psL[:, t * E:(t + 1) * E], buf_a[0:E, t * P:(t + 1) * P], ident[0:E, 0:E])
                last.then_inc(logits_turned, 1)
                hidden(0, 0)
                pe.wait_ge(scores_ready, 1)
                for t in range(NT):
                    last = nc.tensor.transpose(psR[0:E, t * P:(t + 1) * P], R[:, t, :], ident[:])
                last.then_inc(scores_turned, 1)
                hidden(1, 1)
                run(2, SPREAD)
                pe.wait_ge(ones_done, 1)
                pe.wait_ge(spread_ready, 1)
                for h in range(TH):
                    cols = slice(h * BANK, (h + 1) * BANK)
                    last = nc.tensor.matmul(psR[:, cols], ones[:], buf_b[:, cols], start=True, stop=True)
                last.then_inc(spread_done, 1)
                run(SPREAD, SPREAD_MAX)
                pe.wait_ge(spread_ready, 2)
                nc.tensor.matmul(psL[:, 0:P], ones[:], buf_b[:, 0:P], start=True, stop=True).then_inc(spread_done, 1)
                run(SPREAD_MAX, SUM)
                pe.wait_ge(kept_ready, 1)
                for t in range(NT):
                    last = nc.tensor.matmul(psD[:, 2 * t:2 * t + 2], FT[:, t * P:(t + 1) * P], ones[0:E, 0:2],
                                            start=True, stop=True)
                last.then_inc(fsum_done, 1)
                run(SUM, NC)

            @block.vector
            def _(dve):
                steps = [0]

                def tick():
                    steps[0] += 1
                    return 1

                def col(k, n=1):
                    return small[:, k, 0:n]

                dve.wait_ge(wr_hi_done, 1)
                nc.vector.tensor_tensor(wr_lo[:], wr_raw[:], wr_hi[:].bitcast(F32), ALU.subtract).then_inc(wr_lo_done, 1)

                dve.wait_ge(logits_turned, 1)
                logits = psL[:].rearrange("p (t e) -> p t e", e=E)

                def over_experts(k):
                    return small[:, k, 0:NT].rearrange("p (t a) -> p t a", a=1).to_broadcast([P, NT, E])

                nc.vector.tensor_reduce(small[:, 0, 0:NT], logits, AX.X, ALU.max).then_inc(step, tick())
                dve.wait_ge(step, steps[0])
                nc.vector.tensor_tensor(R[:], logits, over_experts(0), ALU.subtract).then_inc(shifted, 1)
                dve.wait_ge(router_exp, 1)
                nc.vector.tensor_reduce(small[:, 1, 0:NT], R[:], AX.X, ALU.add).then_inc(step, tick())
                dve.wait_ge(step, steps[0])
                nc.vector.reciprocal(small[:, 2, 0:NT], small[:, 1, 0:NT]).then_inc(step, tick())
                dve.wait_ge(step, steps[0])
                nc.vector.tensor_tensor(R[:], R[:], over_experts(2), ALU.mult).then_inc(scores_ready, 1)

                dve.wait_ge(scores_turned, 1)
                nc.vector.tensor_copy(RT[:], psR[0:E, :]).then_inc(step, tick())
                nc.vector.tensor_copy(sort_x[0:E, :], psR[0:E, 0:HT]).then_inc(step, tick())
                nc.vector.tensor_copy(sort_x[E:P, :], psR[0:E, HT:T]).then_inc(step, tick())

                src, dst = sort_x, sort_y

                def compare(a, b, big, less):
                    nonlocal src, dst
                    dve.wait_ge(step, steps[0])
                    nc.vector.tensor_tensor(big, a, b, ALU.max).then_inc(step, tick())
                    nc.vector.tensor_tensor(less, a, b, ALU.min).then_inc(step, tick())
                    src, dst = dst, src

                def by_distance(j):
                    a = src[:].rearrange("p (n u j) -> p n u j", u=2, j=j)
                    b = dst[:].rearrange("p (n u j) -> p n u j", u=2, j=j)
                    compare(a[:, :, 0, :], a[:, :, 1, :], b[:, :, 0, :], b[:, :, 1, :])

                k = 2
                while k <= HT:
                    a = src[:].rearrange("p (n k) -> p n k", k=k)
                    b = dst[:].rearrange("p (n k) -> p n k", k=k)
                    mirrored = slice(k - 1, k // 2 - 1, -1)
                    compare(a[:, :, 0:k // 2], a[:, :, mirrored], b[:, :, 0:k // 2], b[:, :, mirrored])
                    j = k // 4
                    while j:
                        by_distance(j)
                        j //= 2
                    k *= 2
                dve.wait_ge(step, steps[0])
                nc.vector.tensor_copy(dst[0:E, :], src[E:P, :]).then_inc(step, tick())
                nc.vector.tensor_copy(dst[E:P, :], src[0:E, :]).then_inc(step, tick())
                dve.wait_ge(step, steps[0])
                nc.vector.tensor_tensor(buf_a[0:E, 0:HT], src[0:E, :], dst[0:E, ::-1], ALU.max).then_inc(step, tick())
                nc.vector.tensor_tensor(buf_a[E:P, 0:HT], src[E:P, :], dst[E:P, ::-1], ALU.min).then_inc(step, tick())
                src = buf_a[:, 0:HT]
                ring = [sort_x[:], sort_y[:], sort_x[:]]
                for n, j in enumerate((HT // 2, HT // 4, NG)):
                    a = src.rearrange("p (n u j) -> p n u j", u=2, j=j)
                    b = ring[n].rearrange("p (n u j) -> p n u j", u=2, j=j)
                    dve.wait_ge(step, steps[0])
                    nc.vector.tensor_tensor(b[:, :, 0, :], a[:, :, 0, :], a[:, :, 1, :], ALU.max).then_inc(step, tick())
                    nc.vector.tensor_tensor(b[:, :, 1, :], a[:, :, 0, :], a[:, :, 1, :], ALU.min).then_inc(step, tick())
                    src = ring[n]
                dve.wait_ge(step, steps[0])
                H8 = TQ // 2
                groups = src.rearrange("p (g n) -> p g n", n=NG)
                gsum, gmin = small[:, 3, 0:H8], small[:, 4, 0:H8]
                nc.vector.tensor_reduce(gmin, groups, AX.X, ALU.min).then_inc(step, tick())
                dve.wait_ge(step, steps[0])
                nc.vector.tensor_reduce(gsum, groups, AX.X, ALU.add).then_inc(step, tick())
                dve.wait_ge(step, steps[0])

                nc.vector.tensor_tensor(buf_b[:].rearrange("p (g q) -> p g q", g=H8),
                                        gsum.rearrange("p (g a) -> p g a", a=1).to_broadcast([P, H8, P]),
                                        ident[:].rearrange("p (a q) -> p a q", a=1).to_broadcast([P, H8, P]),
                                        ALU.mult).then_inc(spread_ready, 1)
                dve.wait_ge(spread_done, 1)
                allsums = buf_c
                nc.vector.tensor_copy(allsums[:].rearrange("p (h g e) -> p h g e", h=2, g=H8),
                                      psR[:].rearrange("p (g h e) -> p h g e", h=2, g=H8)).then_inc(step, tick())
                dve.wait_ge(step, steps[0])
                for g in range(H8):
                    nc.vector.tensor_scalar(buf_d[:], allsums[:], small[:, 3, g:g + 1], None, ALU.is_ge, ALU.add,
                                            accum_out=small[:, 5, g:g + 1]).then_inc(step, tick())
                    dve.wait_ge(step, steps[0])
                nc.vector.scalar_tensor_tensor(small[:, 6, 0:H8], small[:, 5, 0:H8], float(BUDGET), gsum,
                                               ALU.is_ge, ALU.mult).then_inc(step, tick())
                dve.wait_ge(step, steps[0])
                nc.vector.tensor_reduce(col(7), small[:, 6, 0:H8], AX.X, ALU.max).then_inc(step, tick())
                dve.wait_ge(step, steps[0])
                nc.vector.tensor_scalar(buf_b[:, 0:P], ident[:], col(7), None, ALU.mult).then_inc(spread_ready, 1)
                dve.wait_ge(spread_done, 2)
                threshold = col(8)
                nc.vector.tensor_reduce(threshold, psL[:, 0:P], AX.X, ALU.max).then_inc(step, tick())
                dve.wait_ge(step, steps[0])
                above, equal, upto = buf_d, buf_a, buf_b
                nc.vector.tensor_scalar(above[:], allsums[:], threshold, None, ALU.is_gt, ALU.add, accum_out=col(10)).then_inc(step, tick())
                nc.vector.tensor_scalar(equal[:], allsums[:], threshold, None, ALU.is_equal).then_inc(step, tick())
                dve.wait_ge(step, steps[0])
                nc.vector.tensor_scalar(col(11), col(10), -1.0, float(BUDGET), ALU.mult, ALU.add).then_inc(step, tick())
                nc.vector.tensor_tensor_scan(upto[:], equal[:], equal[:], 0.0, ALU.add, ALU.max).then_inc(step, tick())
                dve.wait_ge(step, steps[0])
                nc.vector.scalar_tensor_tensor(equal[:], upto[:], col(11), equal[:], ALU.is_le, ALU.mult).then_inc(step, tick())
                dve.wait_ge(step, steps[0])
                nc.vector.tensor_tensor(above[:], above[:], equal[:], ALU.add).then_inc(step, tick())
                dve.wait_ge(step, steps[0])
                nc.vector.tensor_reduce(rowcount[:], above[:].rearrange("p (q e) -> p e q", e=E), AX.X, ALU.add).then_inc(step, tick())
                dve.wait_ge(step, steps[0])
                nc.vector.tensor_tensor(rowcount[:], rowcount[:], diag[:], ALU.mult).then_inc(step, tick())
                dve.wait_ge(step, steps[0])
                nc.vector.tensor_reduce(col(12), rowcount[:], AX.X, ALU.add).then_inc(step, tick())
                dve.wait_ge(step, steps[0])
                nc.vector.tensor_scalar(small[:, 13, 0:H8], tq_of[:], col(12), BIG, ALU.is_ge, ALU.mult).then_inc(step, tick())
                dve.wait_ge(step, steps[0])
                nc.vector.tensor_tensor(small[:, 13, 0:H8], small[:, 13, 0:H8], gmin, ALU.max).then_inc(step, tick())
                dve.wait_ge(step, steps[0])
                nc.vector.tensor_reduce(col(14), small[:, 13, 0:H8], AX.X, ALU.min).then_inc(step, tick())
                dve.wait_ge(step, steps[0])
                nc.vector.tensor_copy(small[0:E, 15, 0:1], small[E:P, 14, 0:1]).then_inc(step, tick())
                dve.wait_ge(step, steps[0])
                nc.vector.tensor_tensor(small[0:E, 15, 1:2], small[0:E, 15, 0:1], small[0:E, 14, 0:1], ALU.min).then_inc(step, tick())
                dve.wait_ge(step, steps[0])
                least = small[0:E, 15, 1:2]
                nc.vector.tensor_scalar(above[0:E, :], RT[:], least, None, ALU.is_gt, ALU.add, accum_out=small[0:E, 15, 2:3]).then_inc(step, tick())
                nc.vector.tensor_scalar(equal[0:E, :], RT[:], least, None, ALU.is_equal).then_inc(step, tick())
                nc.vector.tensor_scalar(small[0:E, 15, 3:4], small[0:E, 12, 0:1], float(NG), None, ALU.mult).then_inc(step, tick())
                dve.wait_ge(step, steps[0])
                nc.vector.tensor_tensor(small[0:E, 15, 4:5], small[0:E, 15, 3:4], small[0:E, 15, 2:3], ALU.subtract).then_inc(step, tick())
                nc.vector.tensor_tensor_scan(upto[0:E, :], equal[0:E, :], equal[0:E, :], 0.0, ALU.add, ALU.max).then_inc(step, tick())
                dve.wait_ge(step, steps[0])
                nc.vector.scalar_tensor_tensor(equal[0:E, :], upto[0:E, :], small[0:E, 15, 4:5], equal[0:E, :],
                                               ALU.is_le, ALU.mult).then_inc(step, tick())
                dve.wait_ge(step, steps[0])
                nc.vector.tensor_tensor(above[0:E, :], above[0:E, :], equal[0:E, :], ALU.add).then_inc(step, tick())
                dve.wait_ge(step, steps[0])
                nc.vector.tensor_tensor(FT[:], RT[:], above[0:E, :], ALU.mult).then_inc(kept_ready, 1)
                dve.wait_ge(fsum_done, 1)
                nc.vector.tensor_scalar(small[:, 0, 0:NT], psD[:, 0:2 * NT:2], 1e-6, None, ALU.add).then_inc(step, tick())
                dve.wait_ge(step, steps[0])
                nc.vector.reciprocal(fnorm[:], small[:, 0, 0:NT])

        with ExitStack() as two:
            def sb2(name, shape, dt=F32):
                return sb(name, shape, dt, two)

            def sem2(name):
                return sem(name, two)

            bdown = sb2("bdown", [E, D])
            scores = sb2("scores", [P, 2, T])
            d_raw = sb2("d_raw", [P, 2, D])
            d_hi = sb2("d_hi", [P, 2, D], F32R)
            d_lo = sb2("d_lo", [P, 2, D], F32R)
            h_hi = sb2("h_hi", [P, 2, T], F32R)
            h_lo = sb2("h_lo", [P, 2, T], F32R)
            outT = sb2("outT", [P, DC, T])
            psOut = [[two.enter_context(nc.psum_tensor(f"ff_psOut{d}_{h}", [P, BANK], F32)) for h in range(TH)]
                     for d in range(DC)]
            psX = [two.enter_context(nc.psum_tensor(f"ff_psX{k}", [P, D], F32)) for k in range(4)]

            bdown_in = sem2("bdown_in")
            scores_in = [sem2(f"scores_in{s}") for s in range(2)]
            d_in = [sem2(f"d_in{s}") for s in range(2)]
            dhi_done = sem2("dhi_done")
            dlo_done = sem2("dlo_done")
            scaled = sem2("scaled")
            hhi_done = sem2("hhi_done")
            hlo_done = sem2("hlo_done")
            down_done = sem2("down_done")
            all_done = sem2("all_done")
            outT_done = sem2("outT_done")
            x_turned = sem2("x_turned")
            x_done = sem2("x_done")
            out_stored = sem2("out_stored")

            block = two.enter_context(nc.Block())

            @block.sync
            def _(sp):
                sp.dma_start(bdown[:], w["down_bias"]).then_inc(bdown_in, 16)

                def load(c, s):
                    wait(sp, scaled, c - 1)
                    for e in range(2):
                        sp.dma_start(scores[e * NG:(e + 1) * NG, s], fs_dram[bass.ds(2 * c + e, 1), :].to_broadcast([NG, T])
                                     ).then_inc(scores_in[s], 16)
                    wait(sp, dhi_done, c - 1)
                    wait(sp, dlo_done, c - 1)
                    sp.dma_start(d_raw[:, s], w["down"][c]).then_inc(d_in[s], 16)

                load(0, 0)
                load(1, 1)
                with sp.Fori(1, NC // 2) as pair:
                    c = 2 * pair
                    load(c, 0)
                    load(c + 1, 1)
                for t in range(NT):
                    sp.wait_ge(x_done, t + 1)
                    sp.dma_start(out_v[:, t, :], X[:, t, :]).then_inc(out_stored, 16)
                sp.wait_ge(out_stored, 16 * NT)

            @block.vector
            def _(dve):
                def row(c):
                    return G[:, bass.ds(c, 1), :].rearrange("p a t -> p (a t)")

                def scale(c, s):
                    dve.wait_ge(scores_in[s], 16 * (c - s) + 32)
                    nc.vector.tensor_tensor(row(c), row(c), scores[:, s], ALU.mult).then_inc(scaled, 1)

                def split(c, s):
                    dve.wait_ge(hhi_done, c + 1)
                    wait(dve, down_done, c - 1)
                    nc.vector.tensor_tensor(h_lo[:, s], row(c), h_hi[:, s].bitcast(F32), ALU.subtract).then_inc(hlo_done, 1)

                scale(0, 0)
                scale(1, 1)
                split(0, 0)
                scale(2, 0)
                split(1, 1)
                with dve.Fori(1, NC // 2 - 1) as pair:
                    c = 2 * pair
                    scale(c + 1, 1)
                    split(c, 0)
                    scale(c + 2, 0)
                    split(c + 1, 1)
                scale(NC - 1, 1)
                split(NC - 2, 0)
                split(NC - 1, 1)
                dve.wait_ge(all_done, 1)
                nc.vector.tensor_copy(outT[:, 1, 0:BANK], psOut[1][0][:]).then_inc(outT_done, 1)
                nc.vector.tensor_copy(outT[:, 1, BANK:T], psOut[1][1][:]).then_inc(outT_done, 1)
                for t in range(NT):
                    dve.wait_ge(x_turned, t + 1)
                    nc.vector.scalar_tensor_tensor(X[:, t, :], psX[t % 4][:], fnorm[:, t:t + 1], X[:, t, :],
                                                   ALU.mult, ALU.add).then_inc(x_done, 1)

            @block.scalar
            def _(act):
                def turn(c, s):
                    act.wait_ge(d_in[s], 8 * (c - s) + 16)
                    wait(act, down_done, c - 1)
                    nc.scalar.activation(d_hi[:, s], d_raw[:, s], ACT.Copy).then_inc(dhi_done, 1)
                    act.wait_ge(scaled, c + 1)
                    row = G[:, bass.ds(c, 1), :].rearrange("p a t -> p (a t)")
                    nc.scalar.activation(h_hi[:, s], row, ACT.Copy).then_inc(hhi_done, 1)

                turn(0, 0)
                turn(1, 1)
                with act.Fori(1, NC // 2) as pair:
                    c = 2 * pair
                    turn(c, 0)
                    turn(c + 1, 1)
                act.wait_ge(all_done, 1)
                nc.scalar.activation(outT[:, 0, 0:BANK], psOut[0][0][:], ACT.Copy).then_inc(outT_done, 1)
                nc.scalar.activation(outT[:, 0, BANK:T], psOut[0][1][:], ACT.Copy).then_inc(outT_done, 1)

            @block.gpsimd
            def _(pool):
                def turn(c, s):
                    pool.wait_ge(dhi_done, c + 1)
                    nc.gpsimd.tensor_tensor(d_lo[:, s], d_raw[:, s], d_hi[:, s].bitcast(F32), ALU.subtract).then_inc(dlo_done, 1)

                with pool.Fori(0, NC // 2) as pair:
                    c = 2 * pair
                    turn(c, 0)
                    turn(c + 1, 1)

            @block.tensor
            def _(pe):
                pe.wait_ge(bdown_in, 16)
                for d in range(DC):
                    for h in range(TH):
                        nc.tensor.matmul(psOut[d][h][:], bdown[:, d * P:(d + 1) * P], FT[:, h * BANK:(h + 1) * BANK],
                                         start=True, stop=False)

                def turn(s, c, last_one=False):
                    pe.wait_ge(dlo_done, c + 1)
                    pe.wait_ge(hhi_done, c + 1)
                    for n, (a, b) in enumerate(((d_hi, h_hi), (d_lo, h_hi), (d_hi, h_lo))):
                        if n == 2:
                            pe.wait_ge(hlo_done, c + 1)
                        for d in range(DC):
                            for h in range(TH):
                                last = nc.tensor.matmul(psOut[d][h][:], a[:, s, d * P:(d + 1) * P],
                                                        b[:, s, h * BANK:(h + 1) * BANK],
                                                        start=False, stop=(last_one and n == 2))
                    last.then_inc(all_done if last_one else down_done, 1)

                with pe.Fori(0, (NC - 2) // 2) as pair:
                    c = 2 * pair
                    turn(0, c)
                    turn(1, c + 1)
                turn(0, NC - 2)
                turn(1, NC - 1, last_one=True)
                pe.wait_ge(outT_done, 2 * DC)
                for t in range(NT):
                    wait(pe, x_done, t - 3)
                    for d in range(DC):
                        last = nc.tensor.transpose(psX[t % 4][:, d * P:(d + 1) * P], outT[:, d, t * P:(t + 1) * P], ident[:])
                    last.then_inc(x_turned, 1)


def perceiver_kernel(nc, x, ctx_, ctxT, mask, xw, xb, wqkv, wout, bout, ident_c, pick_c, ffn, out, stages=9):
    B, S, D = x.shape
    NT = B * S // P
    with ExitStack() as ctx:
        X = ctx.enter_context(nc.sbuf_tensor("X", [P, NT, D], F32))
        ident = ctx.enter_context(nc.sbuf_tensor("ident", [P, P], F32))
        x_in = ctx.enter_context(nc.semaphore("x_in"))
        out_done = ctx.enter_context(nc.semaphore("out_done"))
        x_v = x.rearrange("b (q p) d -> p (b q) d", p=P)
        out_v = out.rearrange("b (q p) d -> p (b q) d", p=P)
        with nc.Block() as block:
            @block.sync
            def _(sp):
                sp.dma_start(X[:], x_v).then_inc(x_in, 16)
                sp.dma_start(ident[:], ident_c).then_inc(x_in, 16)
                sp.wait_ge(x_in, 32)
        with nc.sbuf_tensor("O", [P, NT, D], F32) as O:
            with nc.sbuf_tensor("XNT1", [P, D // P, NT * P], F32) as XNT:
                ln_transpose(nc, X, XNT, ident, "ln1")
                cross_attention(nc, XNT, ctxT, ctx_, mask, xb, ident, O)
            project_add(nc, X, O, xw, None, ident, "xo")
        if stages > 1:
            self_attention(nc, X, wqkv, pick_c, wout, bout, ident)
        if stages > 2:
            with nc.sbuf_tensor("xT_hi", [P, D // P, NT * P], F32R) as xT_hi, \
                    nc.sbuf_tensor("xT_lo", [P, D // P, NT * P], F32R) as xT_lo:
                ln_transpose(nc, X, None, ident, "ln3", split=(xT_hi, xT_lo))
                routed_ffn(nc, X, xT_hi, xT_lo, ffn, out_v, ident)
            return
        with nc.Block() as block:
            @block.sync
            def _(sp):
                sp.dma_start(out_v, X[:]).then_inc(out_done, 16)
                sp.wait_ge(out_done, 16)


FFN_INPUTS = ("router", "router_bias", "up_bias", "gate_bias", "diag", "tq_of", "up_gate", "down", "down_bias")


def kernel(**inputs):
    import numpy as np
    import concourse.bacc as bacc
    from concourse.bass_utils import run_bass_kernel_spmd

    i = {name: np.asarray(a) for name, a in inputs.items()}

    def ffn(name):
        return i[f"L0_ffn_{name}"]

    E, D, H = ffn("Wup").shape
    NC = E * H // P
    EC = P // H
    heads = 16
    tokens = i["x"].shape[0] * i["x"].shape[1]
    pick = np.zeros((P, heads), np.float32)
    for h in range(heads):
        pick[h, h] = pick[heads + h, h] = 1
    up_gate = np.stack([ffn("Wup"), ffn("Wgate")]).reshape(2, NC, EC, D // P, P, H)
    arrays = {
        "x": i["x"],
        "ctx_": i["ctx_1024"],
        "ctxT": i["ctx_1024"].transpose(0, 2, 1),
        "mask": i["mask_BxSxS2_fk0"],
        "xw": i["L0_xattn_weights"],
        "xb": i["L0_xattn_bias"],
        "wqkv": np.concatenate([i["L0_attn_Wq"].T, i["L0_attn_Wk"].T, i["L0_attn_Wv"].T], 1),
        "wout": i["L0_attn_Wout"].T,
        "bout": i["L0_attn_bout"],
        "ident_c": np.eye(P, dtype=np.float32),
        "pick_c": pick,
        "router": ffn("Wr"),
        "router_bias": ffn("br").reshape(E, 1),
        "up_bias": ffn("bup").reshape(NC, P).T,
        "gate_bias": ffn("bgate").reshape(NC, P).T,
        "diag": np.tile(np.eye(E, dtype=np.float32), (2, 1)),
        "tq_of": ((np.arange(P) // E)[:, None] * (tokens // 128) + np.arange(tokens // 128)).astype(np.float32),
        "up_gate": up_gate.transpose(1, 4, 0, 3, 2, 5).reshape(NC, P, 2, D // P, P),
        "down": ffn("Wdown").reshape(NC, P, D),
        "down_bias": ffn("bdown"),
    }
    nc = bacc.Bacc("TRN2", target_bir_lowering=False, num_devices=1)
    feeds, args = {}, {}
    for name, a in arrays.items():
        a = np.ascontiguousarray(a)
        feeds[f"in_{name}"] = a
        args[name] = nc.dram_tensor(f"in_{name}", a.shape, mybir.dt.from_np(a.dtype), kind="ExternalInput").ap()
    args["out"] = nc.dram_tensor("out_0", i["x"].shape, F32, kind="ExternalOutput").ap()
    args["ffn"] = {name: args.pop(name) for name in FFN_INPUTS}
    perceiver_kernel(nc, **args)
    result = run_bass_kernel_spmd(nc, [feeds], core_ids=[0])
    return result.results[0]["out_0"]
```

```python
from contextlib import ExitStack

import concourse.bass as bass
from concourse import mybir

F32 = mybir.dt.float32
F32R = mybir.dt.float32r
ALU = mybir.AluOpType
ACT = mybir.ActivationFunctionType
AX = mybir.AxisListType

P = 128
BANK = 512
EPS = 1e-5


def wait(eng, sem, n):
    if isinstance(n, int) and n <= 0:
        return
    eng.wait_ge(sem, n)


class Layernorm:

    def __init__(self, nc, X, sb, sem):
        NT = X.shape[1]
        self.nc, self.X = nc, X
        self.stats = sb("ln_stats", [P, NT, 6])
        self.mv = sb("ln_mv", [P, NT, 2])
        self.vare = sb("ln_vare", [P, NT])
        self.std = sb("ln_std", [P, NT])
        self.rstd = sb("ln_rstd", [P, NT])
        self.newt = sb("ln_newt", [P, NT])
        self.stats_done = sem("ln_stats_done")
        self.mv_done = sem("ln_mv_done")
        self.vare_done = sem("ln_vare_done")
        self.std_done = sem("ln_std_done")
        self.newton = sem("ln_newton")

    def moments(self, dve, first, last):
        for t in range(first, last):
            self.nc.vector.bn_stats(self.stats[:, t, :], self.X[:, t, :]).then_inc(self.stats_done, 1)
        for t in range(first, last):
            dve.wait_ge(self.stats_done, t + 1)
            self.nc.vector.bn_aggr(self.mv[:, t, :], self.stats[:, t, :]).then_inc(self.mv_done, 1)

    def variances(self, dve, first, last):
        dve.wait_ge(self.mv_done, last)
        self.nc.vector.tensor_scalar(self.vare[:, first:last], self.mv[:, first:last, 1], EPS, None, ALU.add
                                     ).then_inc(self.vare_done, 1)

    def inverses(self, dve, first, last, group):
        nc, own, n = self.nc, slice(first, last), 5 * group
        dve.wait_ge(self.std_done, group + 1)
        nc.vector.reciprocal(self.rstd[:, own], self.std[:, own]).then_inc(self.newton, 1)
        dve.wait_ge(self.newton, n + 1)
        nc.vector.tensor_tensor(self.newt[:, own], self.rstd[:, own], self.rstd[:, own], ALU.mult).then_inc(self.newton, 1)
        dve.wait_ge(self.newton, n + 2)
        nc.vector.tensor_tensor(self.newt[:, own], self.newt[:, own], self.vare[:, own], ALU.mult).then_inc(self.newton, 1)
        dve.wait_ge(self.newton, n + 3)
        nc.vector.tensor_scalar(self.newt[:, own], self.newt[:, own], -0.5, 1.5, ALU.mult, ALU.add).then_inc(self.newton, 1)
        dve.wait_ge(self.newton, n + 4)
        nc.vector.tensor_tensor(self.rstd[:, own], self.rstd[:, own], self.newt[:, own], ALU.mult).then_inc(self.newton, 1)
        dve.wait_ge(self.newton, n + 5)

    def statistics(self, dve, first, last, group):
        self.moments(dve, first, last)
        self.variances(dve, first, last)
        self.inverses(dve, first, last, group)

    def roots(self, act, group, tiles):
        act.wait_ge(self.vare_done, group + 1)
        self.nc.scalar.activation(self.std[:, tiles], self.vare[:, tiles], ACT.Sqrt).then_inc(self.std_done, 1)

    def normalize(self, dst, tile):
        return self.nc.vector.tensor_scalar(dst, self.X[:, bass.ds(tile, 1), :].rearrange("p a d -> p (a d)"),
                                            self.mv[:, bass.ds(tile, 1), 0], self.rstd[:, bass.ds(tile, 1)],
                                            ALU.subtract, ALU.mult)


class Preparation:

    HEADS, DH = 16, 16

    def __init__(self, nc, ctx, X, ident):
        def sb(name, shape, dt=F32):
            return ctx.enter_context(nc.sbuf_tensor(f"pr_{name}", shape, dt))

        def sem(name):
            return ctx.enter_context(nc.semaphore(f"pr_{name}"))

        NT, D = X.shape[1], X.shape[2]
        HEADS, DH = self.HEADS, self.DH
        self.nc, self.ident, self.D = nc, ident, D
        self.DC = D // P
        self.SQ = 2 * P
        self.NQ = self.SQ // P
        self.PAIRS = HEADS // 2
        self.QUADS = HEADS // 4
        self.ROWS = 4 * DH
        self.ROUNDS = self.NQ * self.PAIRS
        DC, SQ, NQ = self.DC, self.SQ, self.NQ

        self.ln = Layernorm(nc, X, sb, sem)
        self.pick = sb("pick", [P, HEADS])
        self.w_hi = sb("w_hi", [P, DC, 3 * D], F32R)
        self.w_lo = sb("w_lo", [P, DC, 3 * D], F32R)
        self.identr = sb("identr", [P, P], F32R)
        self.XN = sb("XN", [P, NQ, D])
        self.x_hi = sb("x_hi", [P, DC, SQ], F32R)
        self.x_lo = sb("x_lo", [P, DC, SQ], F32R)
        self.q4 = sb("q4", [P, NQ, HEADS, 4, DH], F32R)
        self.k4 = sb("k4", [P, NQ, HEADS, 4, DH], F32R)
        self.qz = sb("qz", [P, HEADS, SQ], F32R)
        self.kT = sb("kT", [P, self.PAIRS, SQ], F32R)
        self.negmax = sb("negmax", [P, NQ, HEADS])
        self.mz = sb("mz", [P, 2, NQ, P], F32R)
        self.mT = sb("mT", [P, 2, SQ], F32R)
        self.v_raw = sb("v_raw", [P, NQ, D])

        self.pick_in = sem("pick_in")
        self.wlo_done = sem("wlo_done")
        self.zeros_done = sem("zeros_done")
        self.identr_done = sem("identr_done")
        self.xn_done = sem("xn_done")
        self.xturned = sem("xturned")
        self.xhi_done = sem("xhi_done")
        self.xlo_done = sem("xlo_done")
        self.qk_done = sem("qk_done")
        self.v_done = sem("v_done")
        self.qkhi_done = sem("qkhi_done")
        self.qklo_done = sem("qklo_done")
        self.vraw_done = sem("vraw_done")
        self.turned = sem("turned")
        self.kT_done = sem("kT_done")
        self.qz_done = sem("qz_done")
        self.qz1_done = sem("qz1_done")
        self.smax_done = sem("smax_done")
        self.max_done = sem("max_done")
        self.mhi_done = sem("mhi_done")
        self.mlo_done = sem("mlo_done")
        self.m_turned = sem("m_turned")
        self.mT_done = sem("mT_done")

    def use_banks(self, psX, psQK, psV, psM):
        self.psX, self.psQK, self.psV, self.psM = psX, psQK, psV, psM
        self.psT = self.psS = psQK


    def layernorm(self, dve, b):
        wait(dve, self.xturned, b)
        for t in range(self.NQ):
            self.ln.normalize(self.XN[:, t, :], self.NQ * b + t).then_inc(self.xn_done, 1)

    def x_lo_part(self, dve, b):
        dve.wait_ge(self.xhi_done, b + 1)
        self.nc.vector.tensor_tensor(self.x_lo[:], self.psX[:].rearrange("p (c q) -> p c q", c=self.DC),
                                     self.x_hi[:].bitcast(F32), ALU.subtract).then_inc(self.xlo_done, 1)

    def qk_lo_parts(self, dve, b, t):
        D, DH, HEADS = self.D, self.DH, self.HEADS
        dve.wait_ge(self.qkhi_done, 2 * (self.NQ * b + t) + 2)
        for half, (x4, hi, slots) in enumerate(((self.q4, 0, slice(2, 4)), (self.k4, 0, slice(1, 4, 2)))):
            src = self.psQK[t][:, half * D:(half + 1) * D].rearrange("p (h a d) -> p h a d", a=1, d=DH)
            self.nc.vector.tensor_tensor(x4[:, t, :, slots, :], src.to_broadcast([P, HEADS, 2, DH]),
                                         x4[:, t, :, hi:hi + 1, :].bitcast(F32).to_broadcast([P, HEADS, 2, DH]),
                                         ALU.subtract).then_inc(self.qklo_done, 1)

    def copy_keys_and_queries(self, dve, b, u):
        dve.wait_ge(self.turned, self.PAIRS * b + 2 * u + 1)
        self.nc.vector.tensor_copy(self.kT[:, 2 * u:2 * u + 2, :], self.psT[0][:].rearrange("p (g k) -> p g k", g=2)
                                   ).then_inc(self.kT_done, 1)
        dve.wait_ge(self.turned, self.PAIRS * b + 2 * u + 2)
        if isinstance(b, int) and b == 0 and u == 0:
            dve.wait_ge(self.zeros_done, 2)
        self.copy_queries(self.nc.vector.tensor_copy, u, 1).then_inc(self.qz1_done, 1)

    def copy_queries(self, instruction, u, s, *function):
        rows = slice(self.ROWS * s, self.ROWS * (s + 1))
        return instruction(self.qz[rows, 4 * u + s:4 * u + s + 3:2, :],
                           self.psT[1][rows, :].rearrange("p (g q) -> p g q", g=2), *function)

    def maximum(self, dve, b, n, t, g):
        dve.wait_ge(self.smax_done, self.ROUNDS * b + n + 1)
        self.nc.vector.tensor_reduce(self.negmax[:, t, 2 * g:2 * g + 2],
                                     self.psS[n % 2][:].rearrange("p (h k) -> p h k", h=2),
                                     AX.X, ALU.max, negate=True).then_inc(self.max_done, 1)

    def split_maxima(self, dve, b, half):
        HEADS, ROUNDS = self.HEADS, self.ROUNDS
        own = slice(half * HEADS // 2, (half + 1) * HEADS // 2)
        low = slice(HEADS + half * HEADS // 2, HEADS + (half + 1) * HEADS // 2)
        dve.wait_ge(self.max_done, ROUNDS * b + (half + 1) * ROUNDS // 2)
        if isinstance(b, int) and b == 0:
            dve.wait_ge(self.zeros_done, 2)
        wait(dve, self.m_turned, 2 * b + half - 1)
        self.nc.vector.tensor_copy(self.mz[:, half, :, own], self.negmax[:, :, own]).then_inc(self.mhi_done, 1)
        dve.wait_ge(self.mhi_done, 2 * b + half + 1)
        self.nc.vector.tensor_tensor(self.mz[:, half, :, low], self.negmax[:, :, own],
                                     self.mz[:, half, :, own].bitcast(F32), ALU.subtract).then_inc(self.mlo_done, 1)


    def x_hi_part(self, act, b):
        act.wait_ge(self.xturned, b + 1)
        self.nc.scalar.activation(self.x_hi[:], self.psX[:].rearrange("p (c q) -> p c q", c=self.DC), ACT.Copy
                                  ).then_inc(self.xhi_done, 1)

    def qk_hi_parts(self, act, b, t):
        D, DH, HEADS = self.D, self.DH, self.HEADS
        act.wait_ge(self.qk_done, self.NQ * b + t + 1)
        for half, (x4, slots) in enumerate(((self.q4, slice(0, 2)), (self.k4, slice(0, 4, 2)))):
            src = self.psQK[t][:, half * D:(half + 1) * D].rearrange("p (h a d) -> p h a d", a=1, d=DH)
            self.nc.scalar.activation(x4[:, t, :, slots, :], src.to_broadcast([P, HEADS, 2, DH]),
                                      ACT.Copy).then_inc(self.qkhi_done, 1)

    def copy_other_queries(self, act, b, u):
        act.wait_ge(self.turned, self.PAIRS * b + 2 * u + 2)
        if isinstance(b, int) and b == 0 and u == 0:
            act.wait_ge(self.zeros_done, 2)
        self.copy_queries(self.nc.scalar.activation, u, 0, ACT.Copy).then_inc(self.qz_done, 1)

    def save_values(self, act, b):
        act.wait_ge(self.v_done, b + 1)
        self.nc.scalar.activation(self.v_raw[:], self.psV[:].rearrange("p (t d) -> p t d", t=self.NQ), ACT.Copy
                                  ).then_inc(self.vraw_done, 1)

    def save_maxima(self, act, b, half):
        act.wait_ge(self.m_turned, 2 * b + half + 1)
        self.nc.scalar.activation(self.mT[:, half, :], self.psM[:, 0:self.SQ], ACT.Copy).then_inc(self.mT_done, 1)


    def turn_x(self, pe, b):
        SQ = self.SQ
        pe.wait_ge(self.xn_done, self.NQ * (b + 1))
        wait(pe, self.mT_done, 2 * b - 1)
        for c in range(self.DC):
            for t in range(self.NQ):
                last = self.nc.tensor.transpose(self.psX[:, c * SQ + t * P:c * SQ + (t + 1) * P],
                                                self.XN[:, t, c * P:(c + 1) * P], self.ident[:])
        last.then_inc(self.xturned, 1)

    def project(self, t, ps, cols):
        n = 0
        for x, w in ((self.x_hi, self.w_hi), (self.x_lo, self.w_hi), (self.x_hi, self.w_lo)):
            for c in range(self.DC):
                last = self.nc.tensor.matmul(ps, x[:, c, t * P:(t + 1) * P], w[:, c, cols],
                                             start=(n == 0), stop=(n == 3 * self.DC - 1), skip_group_check=True)
                n += 1
        return last

    def project_qk(self, pe, b, t):
        pe.wait_ge(self.xlo_done, b + 1)
        if isinstance(b, int) and b == 0:
            pe.wait_ge(self.wlo_done, 1)
        wait(pe, self.max_done, self.ROUNDS * b)
        self.project(t, self.psQK[t][:], slice(0, 2 * self.D)).then_inc(self.qk_done, 1)

    def turn_qk(self, pe, b, u):
        if isinstance(b, int) and b == 0 and u == 0:
            pe.wait_ge(self.identr_done, 1)
        pe.wait_ge(self.qklo_done, 2 * self.NQ * (b + 1))
        wait(pe, self.max_done, self.ROUNDS * b + 4 * u)
        for half, x4 in enumerate((self.k4, self.q4)):
            for g in range(2):
                for t in range(self.NQ):
                    pair = x4[:, t, 4 * u + 2 * g:4 * u + 2 * g + 2].rearrange("p h a d -> p (h a d)")
                    last = self.nc.tensor.transpose(
                        self.psT[half][:, (self.NQ * g + t) * P:(self.NQ * g + t + 1) * P].bitcast(F32R), pair, self.identr[:])
            last.then_inc(self.turned, 1)

    def score(self, pe, b, n, t, g):
        SQ = self.SQ
        pe.wait_ge(self.kT_done, self.QUADS * b + g // 2 + 1)
        pe.wait_ge(self.qz_done, self.QUADS * b + g // 2 + 1)
        pe.wait_ge(self.qz1_done, self.QUADS * b + g // 2 + 1)
        wait(pe, self.max_done, self.ROUNDS * b + n - 1)
        for s in range(2):
            last = self.nc.tensor.matmul(self.psS[n % 2][:, s * SQ:(s + 1) * SQ], self.qz[:, 2 * g + s, t * P:(t + 1) * P],
                                         self.kT[:, g, :], start=True, stop=True)
        last.then_inc(self.smax_done, 1)

    def project_values(self, pe, b):
        D = self.D
        wait(pe, self.mT_done, 2 * b)
        for t in range(self.NQ):
            last = self.project(t, self.psV[:, t * D:(t + 1) * D], slice(2 * D, 3 * D))
        last.then_inc(self.v_done, 1)

    def turn_maxima(self, pe, b, half):
        pe.wait_ge(self.mlo_done, 2 * b + half + 1)
        for t in range(self.NQ):
            last = self.nc.tensor.transpose(self.psM[:, t * P:(t + 1) * P].bitcast(F32R), self.mz[:, half, t, :], self.identr[:])
        last.then_inc(self.m_turned, 1)


def cross_attention(nc, X, x_dram, ident_dram, ctxT_dram, ctx_dram, mask_dram, w_dram, bias_dram, ident,
                    split, prep, wqkv_dram, pick_dram):
    TEMP = 0.72
    B, NJ, _, DC, KB = ctxT_dram.shape
    D = DC * P
    KC = KB // P
    NQ = mask_dram.shape[3]
    SQ = NQ * P

    x_v = x_dram.rearrange("b (q p) d -> p (b q) d", p=P)

    with ExitStack() as ctx:
        def sb(name, shape, dt=F32):
            return ctx.enter_context(nc.sbuf_tensor(f"xa_{name}", shape, dt))

        def ps(name, shape):
            return ctx.enter_context(nc.psum_tensor(f"xa_{name}", shape, F32))

        def sem(name):
            return ctx.enter_context(nc.semaphore(f"xa_{name}"))

        ln = Layernorm(nc, X, sb, sem)
        w_raw = sb("w_raw", [P, DC, D])
        w_hi = sb("w_hi", [P, DC, D], F32R)
        w_lo = sb("w_lo", [P, DC, D], F32R)
        bias = sb("bias", [P, DC])
        bias_cols = sb("bias_cols", [P, DC, P])
        bias_w = sb("bias_w", [P, 1, D])
        wqkv_raw = sb("wqkv_raw", [P, DC, 3 * D])
        XN, q_hi, q_lo = prep.XN, prep.x_hi, prep.x_lo
        keysT_raw = sb("keysT_raw", [P, 2, DC, KB])
        keysT_hi, keysT_lo = split
        vals_raw = sb("vals_raw", [P, 2, KC, D])
        vals_hi = sb("vals_hi", [P, 2, KC, D], F32R)
        vals_lo = sb("vals_lo", [P, 2, KC, D], F32R)
        mask = sb("mask", [P, 2, NQ, KB])
        S = sb("S", [P, NJ, NQ, KB])
        probs = sb("probs", [P, 2, NQ, KB])
        pT_hi = sb("pT_hi", [P, 2, KC, SQ], F32R)
        pT_lo = sb("pT_lo", [P, 2, KC, SQ], F32R)
        oT_hi = sb("oT_hi", [P, DC, SQ], F32R)
        oT_lo = sb("oT_lo", [P, DC, SQ], F32R)
        blockmax = sb("blockmax", [P, NQ, NJ])
        rowmax = sb("rowmax", [P, NQ])
        expbias = sb("expbias", [P, NQ])
        blocksum = sb("blocksum", [P, NQ, NJ])
        rowsum = sb("rowsum", [P, NQ])
        rinv = sb("rinv", [P, NQ])
        psS = [ps(f"psS{q}", [P, KB]) for q in range(NQ)]
        psP = [[ps(f"psP{s}_{q}", [P, KB]) for q in range(NQ)] for s in range(2)]
        psOT = [ps(f"psOT{d}", [P, BANK]) for d in range(DC)]
        psX, psW = psP[0][1], psP[1][0]
        prep.use_banks(psX=psS[0], psQK=psS, psV=psS[0], psM=psS[1])

        x_in = [sem(f"x_in{b}") for b in range(B)]
        ident_in = sem("ident_in")
        w_in = sem("w_in")
        wqkv_in = sem("wqkv_in")
        wqkvhi_done = sem("wqkvhi_done")
        bias_in = sem("bias_in")
        keysT_in = [sem(f"keysT_in{s}") for s in range(2)]
        vals_in = [sem(f"vals_in{s}") for s in range(2)]
        mask_in = [sem(f"mask_in{s}") for s in range(2)]
        bias_cols_done = sem("bias_cols_done")
        bias_product = sem("bias_product")
        bias_w_done = sem("bias_w_done")
        biased = sem("biased")
        whi_done = sem("whi_done")
        wlo_done = sem("wlo_done")
        xn_done = sem("xn_done")
        xturned = sem("xturned")
        khi_done = sem("khi_done")
        klo_done = sem("klo_done")
        klo1_done = sem("klo1_done")
        vhi_done = sem("vhi_done")
        vlo_done = sem("vlo_done")
        qhi_done = sem("qhi_done")
        qlo_done = sem("qlo_done")
        scores_done = sem("scores_done")
        scores_saved = sem("scores_saved")
        rowmax_done = sem("rowmax_done")
        expbias_done = sem("expbias_done")
        exp_done = sem("exp_done")
        masked = sem("masked")
        pT_done = sem("pT_done")
        phi_done = sem("phi_done")
        plo_done = sem("plo_done")
        pv_done = sem("pv_done")
        rowsum_done = sem("rowsum_done")
        rinv_done = sem("rinv_done")
        othi_done = sem("othi_done")
        otlo_done = sem("otlo_done")
        projected = sem("projected")
        updated = sem("updated")

        def blocks(b, j):
            return NJ * b + j + 1

        def tiles(b, j, q):
            return NQ * (NJ * b + j) + q + 1

        def slot_loads(b, j):
            return 16 * ((NJ // 2) * b + j // 2 + 1)

        def turns(eng, turn):
            turn(0, True, False, False, True)
            turn(1, True, True, False, True)
            with eng.Fori(2, B - 1) as i:
                turn(i, True, True, True, True)
            turn(B - 1, True, True, True, False)
            turn(B, False, True, True, False)

        STEPS = {(0, 0): ("x", "qk0", "qk1"), (1, 0): ("turn0",), (2, 0): ("round0",), (2, 1): ("round2",),
                 (3, 0): ("turn1",), (4, 0): ("round4",), (4, 1): ("round6",), (5, 0): ("values",),
                 (5, 1): ("maxima",), (6, 0): ("turn2",), (7, 0): ("round8",), (7, 1): ("round10",)}

        def round_of(n):
            return n % NQ, n // NQ

        block = ctx.enter_context(nc.Block())

        @block.sync
        def _(sp):
            sp.dma_start(X[:, 0:NQ, :], x_v[:, 0:NQ, :]).then_inc(x_in[0], 16)
            sp.dma_start(ident[:], ident_dram).then_inc(ident_in, 16)

            def turn(i, scoring, weighing, finishing, more):
                for j in range(NJ):
                    if scoring:
                        wait(sp, khi_done, blocks(i, j - 2))
                        wait(sp, klo_done, blocks(i, j - 2))
                        if isinstance(i, int) and blocks(i, j - 2) <= NJ:
                            wait(sp, klo1_done, blocks(i, j - 2))
                        sp.dma_start(keysT_raw[:, j % 2], ctxT_dram[i, j]).then_inc(keysT_in[j % 2], 16)
                    if isinstance(i, int) and i == 0:
                        if 1 <= j < B:
                            own = slice(NQ * j, NQ * (j + 1))
                            sp.dma_start(X[:, own, :], x_v[:, own, :]).then_inc(x_in[j], 16)
                        if j == B:
                            sp.dma_start(bias[:], bias_dram).then_inc(bias_in, 16)
                            sp.dma_start(w_raw[:], w_dram.rearrange("(c p) n -> p c n", p=P)).then_inc(w_in, 16)
                    if isinstance(i, int) and i == 1 and j < 3:
                        own = slice(j * D, (j + 1) * D)
                        sp.dma_start(wqkv_raw[:, :, own], wqkv_dram.rearrange("(c p) n -> p c n", p=P)[:, :, own]).then_inc(wqkv_in, 16)
                        if j == 0:
                            sp.dma_start(prep.pick[:], pick_dram).then_inc(prep.pick_in, 16)
                    if weighing:
                        wait(sp, masked, tiles(i - 1, j - 2, NQ - 1))
                        sp.dma_start(mask[:, j % 2], mask_dram[i - 1, j]).then_inc(mask_in[j % 2], 16)
                        wait(sp, vhi_done, blocks(i - 1, j - 2))
                        wait(sp, vlo_done, blocks(i - 1, j - 2))
                        sp.dma_start(vals_raw[:, j % 2], ctx_dram[i - 1, j]).then_inc(vals_in[j % 2], 16)
            turns(sp, turn)

        @block.scalar
        def _(act):
            def split_queries(b):
                act.wait_ge(xturned, b + 1)
                wait(act, scores_done, tiles(b, -1, NQ - 1))
                nc.scalar.activation(q_hi[:], psX[:].rearrange("p (c q) -> p c q", c=DC), ACT.Copy).then_inc(qhi_done, 1)

            def split_keys(b, j):
                act.wait_ge(keysT_in[j % 2], slot_loads(b, j))
                wait(act, scores_done, tiles(b, j - 2, NQ - 1))
                nc.scalar.activation(keysT_hi[:, j % 2], keysT_raw[:, j % 2], ACT.Copy).then_inc(khi_done, 1)

            def split_values(b, j):
                act.wait_ge(vals_in[j % 2], slot_loads(b, j))
                wait(act, pv_done, blocks(b, j - 2))
                nc.scalar.activation(vals_hi[:, j % 2], vals_raw[:, j % 2], ACT.Copy).then_inc(vhi_done, 1)

            def exponentials(b, j):
                if j == 0:
                    act.wait_ge(expbias_done, b + 1)
                    wait(act, rowsum_done, b)
                wait(act, pT_done, tiles(b, j - 2, NQ - 1))
                for q in range(NQ):
                    nc.scalar.activation(probs[:, j % 2, q, :], S[:, j, q, :], ACT.Exp, bias=expbias[:, q:q + 1],
                                         scale=1.0 / TEMP, accum_out=blocksum[:, q, j:j + 1]).then_inc(exp_done, 1)

            def split_probs(b, j):
                wait(act, pv_done, blocks(b, j - 2))
                for q in range(NQ):
                    act.wait_ge(pT_done, tiles(b, j, q))
                    nc.scalar.activation(pT_hi[:, j % 2, :, q * P:(q + 1) * P], psP[j % 2][q][:].rearrange("p (c q) -> p c q", c=KC),
                                         ACT.Copy).then_inc(phi_done, 1)

            def split_outputs(b):
                act.wait_ge(pv_done, blocks(b, NJ - 1))
                for d in range(DC):
                    nc.scalar.activation(oT_hi[:, d, :], psOT[d][:, 0:SQ], ACT.Copy).then_inc(othi_done, 1)

            def turn(i, scoring, weighing, finishing, more):
                if isinstance(i, int) and i == 0:
                    ln.roots(act, 0, slice(0, NQ))
                    split_keys(0, 0)
                    split_queries(0)
                    split_keys(0, 1)
                if weighing:
                    exponentials(i - 1, 0)
                    split_values(i - 1, 0)
                if finishing:
                    split_outputs(i - 2)
                if not scoring:
                    exponentials(i - 1, 1)
                for j in range(NJ):
                    if weighing:
                        if scoring and j + 1 < NJ:
                            exponentials(i - 1, j + 1)
                        split_probs(i - 1, j)
                        if not scoring:
                            if j + 2 < NJ:
                                exponentials(i - 1, j + 2)
                            prepare(j, 0)
                    if j + 1 < NJ:
                        if scoring and j > 0:
                            split_keys(i, j + 1)
                        if weighing:
                            split_values(i - 1, j + 1)
                    if not scoring:
                        prepare(j, 1)
                    if isinstance(i, int) and i == 0:
                        if j == B - 1:
                            ln.roots(act, 1, slice(NQ, NQ * B))
                        if j == B:
                            act.wait_ge(w_in, 16)
                            nc.scalar.activation(w_hi[:], w_raw[:], ACT.Copy).then_inc(whi_done, 1)
                            nc.scalar.activation(prep.identr[:], ident[:], ACT.Copy).then_inc(prep.identr_done, 1)
                    if isinstance(i, int) and i == 1 and j == 4:
                        act.wait_ge(wqkv_in, 16 * 3)
                        nc.scalar.activation(prep.w_hi[:], wqkv_raw[:], ACT.Copy).then_inc(wqkvhi_done, 1)
                if more:
                    split_queries(i + 1)
                    split_keys(i + 1, 0)
                    split_keys(i + 1, 1)
                elif scoring:
                    prep.ln.roots(act, 0, slice(0, 2 * NQ))
                else:
                    split_outputs(B - 1)

            def prepare(j, behind):
                for step in STEPS.get((j, behind), ()):
                    if step == "x":
                        prep.x_hi_part(act, 0)
                    elif step[:2] == "qk":
                        prep.qk_hi_parts(act, 0, int(step[2:]))
                    elif step[:4] == "turn":
                        prep.copy_other_queries(act, 0, int(step[4:]))
                    elif step == "values":
                        prep.save_values(act, 0)
                    elif step == "maxima":
                        prep.save_maxima(act, 0, 0)
            turns(act, turn)

        @block.vector
        def _(dve):
            def layernorm(b):
                wait(dve, xturned, b)
                for t in range(NQ):
                    ln.normalize(XN[:, t, :], NQ * b + t).then_inc(xn_done, 1)

            def split_queries(b):
                dve.wait_ge(qhi_done, b + 1)
                nc.vector.tensor_tensor(q_lo[:], psX[:].rearrange("p (c q) -> p c q", c=DC), q_hi[:].bitcast(F32),
                                        ALU.subtract).then_inc(qlo_done, 1)

            def split_keys(b, j):
                own = slice(0, 1 if isinstance(b, int) and b == 0 else DC)
                dve.wait_ge(khi_done, blocks(b, j))
                nc.vector.tensor_tensor(keysT_lo[:, j % 2, own], keysT_raw[:, j % 2, own], keysT_hi[:, j % 2, own].bitcast(F32),
                                        ALU.subtract).then_inc(klo_done, 1)

            def split_probs(b, j):
                for q in range(NQ):
                    dve.wait_ge(phi_done, tiles(b, j, q))
                    cols = slice(q * P, (q + 1) * P)
                    nc.vector.tensor_tensor(pT_lo[:, j % 2, :, cols], psP[j % 2][q][:].rearrange("p (c q) -> p c q", c=KC),
                                            pT_hi[:, j % 2, :, cols].bitcast(F32), ALU.subtract).then_inc(plo_done, 1)

            def split_values(b, j):
                dve.wait_ge(vhi_done, blocks(b, j))
                dve.wait_ge(vlo_done, blocks(b, j - 1))
                nc.vector.tensor_tensor(vals_lo[:, j % 2], vals_raw[:, j % 2], vals_hi[:, j % 2].bitcast(F32),
                                        ALU.subtract).then_inc(vlo_done, 1)

            def save_scores(b, j):
                for q in range(NQ):
                    dve.wait_ge(scores_done, tiles(b, j, q))
                    wait(dve, exp_done, tiles(b - 1, j, q))
                    nc.vector.tensor_scalar(S[:, j, q, :], psS[q][:], 1.0, None, ALU.mult, ALU.max,
                                            accum_out=blockmax[:, q, j:j + 1]).then_inc(scores_saved, 1)

            def row_maximum(b):
                dve.wait_ge(scores_saved, tiles(b, NJ - 1, NQ - 1))
                nc.vector.tensor_reduce(rowmax[:], blockmax[:], AX.X, ALU.max).then_inc(rowmax_done, 1)
                dve.wait_ge(rowmax_done, b + 1)
                wait(dve, exp_done, tiles(b, -1, NQ - 1))
                nc.vector.tensor_scalar(expbias[:], rowmax[:], -1.0 / TEMP, None, ALU.mult).then_inc(expbias_done, 1)

            def row_sums(b):
                dve.wait_ge(exp_done, tiles(b, NJ - 1, NQ - 1))
                nc.vector.tensor_reduce(rowsum[:], blocksum[:], AX.X, ALU.add).then_inc(rowsum_done, 1)
                dve.wait_ge(rowsum_done, b + 1)
                nc.vector.reciprocal(rinv[:], rowsum[:]).then_inc(rinv_done, 1)

            def split_outputs(b):
                for d in range(DC):
                    dve.wait_ge(othi_done, DC * b + d + 1)
                    nc.vector.tensor_tensor(oT_lo[:, d, :], psOT[d][:, 0:SQ], oT_hi[:, d, :].bitcast(F32),
                                            ALU.subtract).then_inc(otlo_done, 1)

            def update(b):
                dve.wait_ge(projected, b + 1)
                dve.wait_ge(rinv_done, b + 1)
                dve.wait_ge(biased, b + 1)
                for t in range(NQ):
                    x = X[:, bass.ds(NQ * b + t, 1), :].rearrange("p a d -> p (a d)")
                    nc.vector.scalar_tensor_tensor(x, psW[:, t * D:(t + 1) * D], rinv[:, t:t + 1], x,
                                                   ALU.mult, ALU.add).then_inc(updated, 1)

            def turn(i, scoring, weighing, finishing, more):
                first = isinstance(i, int) and i == 0
                if first:
                    dve.wait_ge(x_in[0], 16)
                    ln.statistics(dve, 0, NQ, 0)
                    layernorm(0)
                    split_keys(0, 0)
                    split_queries(0)
                    split_keys(0, 1)
                if not scoring:
                    split_values(i - 1, 0)
                    prep.layernorm(dve, 0)
                for j in range(NJ):
                    if finishing and j == 0:
                        split_outputs(i - 2)
                    if weighing and j > 0:
                        split_probs(i - 1, j)
                    if scoring:
                        if 0 < j < NJ - 1:
                            split_keys(i, j + 1)
                        save_scores(i, j)
                    elif j > 0:
                        prepare(j, 0)
                    if weighing and j == 0:
                        split_probs(i - 1, 0)
                        if finishing:
                            update(i - 2)
                    if not scoring:
                        if j == 0:
                            prepare(j, 0)
                        if j + 1 < NJ:
                            split_values(i - 1, j + 1)
                        prepare(j, 1)
                    if first and 1 <= j < B:
                        dve.wait_ge(x_in[j], 16)
                        ln.moments(dve, j * NQ, (j + 1) * NQ)
                        if j == B - 1:
                            ln.variances(dve, NQ, NQ * B)
                    if first and j == B + 1:
                        ln.inverses(dve, NQ, NQ * B, 1)
                    if first and j == B + 1:
                        dve.wait_ge(whi_done, 1)
                        nc.vector.tensor_tensor(w_lo[:], w_raw[:], w_hi[:].bitcast(F32), ALU.subtract).then_inc(wlo_done, 1)
                        dve.wait_ge(bias_in, 16)
                        nc.vector.tensor_copy(bias_cols[:], bias[:].rearrange("p (c a) -> p c a", a=1).to_broadcast([P, DC, P])
                                              ).then_inc(bias_cols_done, 1)
                    if isinstance(i, int) and i == 1 and j == 5:
                        dve.wait_ge(wqkvhi_done, 1)
                        nc.vector.tensor_tensor(prep.w_lo[:], wqkv_raw[:], prep.w_hi[:].bitcast(F32), ALU.subtract
                                                ).then_inc(prep.wlo_done, 1)
                    if weighing and j == NJ - 2:
                        row_sums(i - 1)
                    if more and j == NJ - 2:
                        layernorm(i + 1)
                    if scoring and not more and j == NJ - 2:
                        prep.ln.statistics(dve, 0, 2 * NQ, 0)
                if scoring:
                    row_maximum(i)
                if more:
                    split_queries(i + 1)
                    split_keys(i + 1, 0)
                    split_keys(i + 1, 1)
                if first:
                    dve.wait_ge(bias_product, 1)
                    nc.vector.tensor_copy(bias_w[:, 0, :], psOT[0][:, 0:D]).then_inc(bias_w_done, 1)
                if not scoring:
                    split_outputs(B - 1)
                    update(B - 1)

            def prepare(j, behind):
                for step in STEPS.get((j, behind), ()):
                    if step == "x":
                        prep.x_lo_part(dve, 0)
                    elif step[:2] == "qk":
                        prep.qk_lo_parts(dve, 0, int(step[2:]))
                    elif step[:4] == "turn":
                        prep.copy_keys_and_queries(dve, 0, int(step[4:]))
                    elif step[:5] == "round":
                        for n in range(int(step[5:]), int(step[5:]) + 2):
                            prep.maximum(dve, 0, n, *round_of(n))
                        if n == 7:
                            prep.split_maxima(dve, 0, 0)
            turns(dve, turn)

        @block.gpsimd
        def _(pool):
            def apply_mask(b, j):
                pool.wait_ge(mask_in[j % 2], slot_loads(b, j))
                for q in range(NQ):
                    pool.wait_ge(exp_done, tiles(b, j, q))
                    nc.gpsimd.tensor_tensor(probs[:, j % 2, q, :], probs[:, j % 2, q, :], mask[:, j % 2, q, :],
                                            ALU.mult).then_inc(masked, 1)

            def split_values(b, j):
                pool.wait_ge(vhi_done, blocks(b, j))
                nc.gpsimd.tensor_tensor(vals_lo[:, j % 2], vals_raw[:, j % 2],
                                        vals_hi[:, j % 2].bitcast(F32), ALU.subtract).then_inc(vlo_done, 1)

            def add_bias(b):
                if isinstance(b, int) and b == 0:
                    pool.wait_ge(bias_w_done, 1)
                pool.wait_ge(xn_done, NQ * (b + 1))
                x = X[:, bass.ds(NQ * b, NQ), :]
                nc.gpsimd.tensor_tensor(x, x, bias_w[:].to_broadcast([P, NQ, D]), ALU.add).then_inc(biased, 1)

            for j in range(NJ):
                pool.wait_ge(khi_done, j + 1)
                nc.gpsimd.tensor_tensor(keysT_lo[:, j % 2, 1:DC], keysT_raw[:, j % 2, 1:DC],
                                        keysT_hi[:, j % 2, 1:DC].bitcast(F32), ALU.subtract).then_inc(klo1_done, 1)
            nc.gpsimd.memset(prep.qz[:].bitcast(F32), 0.0).then_inc(prep.zeros_done, 1)
            nc.gpsimd.memset(prep.mz[:].bitcast(F32), 0.0).then_inc(prep.zeros_done, 1)

            def turn(i, scoring, weighing, finishing, more):
                if weighing:
                    for j in range(NJ):
                        apply_mask(i - 1, j)
                        if scoring:
                            split_values(i - 1, j)
                        if j == 1:
                            add_bias(i - 1)
            turns(pool, turn)

        @block.tensor
        def _(pe):
            def turn_queries(b):
                pe.wait_ge(xn_done, NQ * (b + 1))
                if isinstance(b, int) and b == 0:
                    pe.wait_ge(ident_in, 16)
                wait(pe, plo_done, tiles(b - 2, NJ - 2, NQ - 1))
                for c in range(DC):
                    for t in range(NQ):
                        last = nc.tensor.transpose(psX[:, c * SQ + t * P:c * SQ + (t + 1) * P], XN[:, t, c * P:(c + 1) * P], ident[:])
                last.then_inc(xturned, 1)

            def transpose_probs(b, j):
                for q in range(NQ):
                    pe.wait_ge(masked, tiles(b, j, q))
                    wait(pe, phi_done, tiles(b, j - 2, q))
                    wait(pe, plo_done, tiles(b, j - 2, q))
                    for c in range(KC):
                        last = nc.tensor.transpose(psP[j % 2][q][:, c * P:(c + 1) * P], probs[:, j % 2, q, c * P:(c + 1) * P], ident[:])
                    last.then_inc(pT_done, 1)

            def scores(b, j):
                if j == 0:
                    pe.wait_ge(qlo_done, b + 1)
                pe.wait_ge(klo_done, blocks(b, j))
                if isinstance(b, int) and b == 0:
                    pe.wait_ge(klo1_done, j + 1)
                for q in range(NQ):
                    wait(pe, scores_saved, tiles(b, j - 1, q))
                    n = 0
                    for a, k in ((q_hi, keysT_hi), (q_lo, keysT_hi), (q_hi, keysT_lo)):
                        for c in range(DC):
                            last = nc.tensor.matmul(psS[q][:], a[:, c, q * P:(q + 1) * P], k[:, j % 2, c, :],
                                                    start=(n == 0), stop=(n == 3 * DC - 1))
                            n += 1
                    last.then_inc(scores_done, 1)

            def weigh(b, j):
                pe.wait_ge(vlo_done, blocks(b, j))
                pe.wait_ge(plo_done, tiles(b, j, NQ - 1))
                if j == 0:
                    wait(pe, otlo_done, DC * b)
                    if isinstance(b, int) and b == 0:
                        pe.wait_ge(bias_w_done, 1)
                n = 0
                for v, p in ((vals_hi, pT_hi), (vals_lo, pT_hi), (vals_hi, pT_lo)):
                    for c in range(KC):
                        for d in range(DC):
                            last = nc.tensor.matmul(psOT[d][:, 0:SQ], v[:, j % 2, c, d * P:(d + 1) * P], p[:, j % 2, c, :],
                                                    start=(j == 0 and n == 0), stop=(j == NJ - 1 and n == 3 * KC - 1))
                        n += 1
                last.then_inc(pv_done, 1)

            def project(b):
                pe.wait_ge(otlo_done, DC * (b + 1))
                pe.wait_ge(wlo_done, 1)
                for t in range(NQ):
                    n = 0
                    for a, w in ((oT_hi, w_hi), (oT_lo, w_hi), (oT_hi, w_lo)):
                        for c in range(DC):
                            last = nc.tensor.matmul(psW[:, t * D:(t + 1) * D], a[:, c, t * P:(t + 1) * P], w[:, c, :],
                                                    start=(n == 0), stop=(n == 3 * DC - 1))
                            n += 1
                last.then_inc(projected, 1)

            def turn(i, scoring, weighing, finishing, more):
                if isinstance(i, int) and i == 0:
                    turn_queries(0)
                if not scoring:
                    transpose_probs(i - 1, 0)
                    project(i - 2)
                for j in range(NJ):
                    if scoring:
                        if j == 0:
                            scores(i, 0)
                        if weighing:
                            if j == 1 and finishing:
                                pe.wait_ge(updated, NQ * (i - 1))
                            transpose_probs(i - 1, j)
                        if j > 0:
                            scores(i, j)
                        if j == 0 and finishing:
                            project(i - 2)
                    elif j + 1 < NJ:
                        if j == 0:
                            pe.wait_ge(updated, NQ * (i - 1))
                        transpose_probs(i - 1, j + 1)
                    if not scoring:
                        prepare(j, 0)
                    if more and j == NJ - 1:
                        turn_queries(i + 1)
                    if weighing:
                        weigh(i - 1, j)
                    if not scoring:
                        prepare(j, 1)
                    if isinstance(i, int) and i == 0 and j == NJ - 1:
                        pe.wait_ge(bias_cols_done, 1)
                        for c in range(DC):
                            last = nc.tensor.matmul(psOT[0][:, 0:D], bias_cols[:, c, :], w_raw[:, c, :],
                                                    start=(c == 0), stop=(c == DC - 1))
                        last.then_inc(bias_product, 1)
                if not scoring:
                    project(B - 1)

            def prepare(j, behind):
                for step in STEPS.get((j, behind), ()):
                    if step == "x":
                        pe.wait_ge(scores_saved, tiles(B - 1, NJ - 1, NQ - 1))
                        prep.turn_x(pe, 0)
                    elif step[:2] == "qk":
                        prep.project_qk(pe, 0, int(step[2:]))
                    elif step[:4] == "turn":
                        if step == "turn2":
                            pe.wait_ge(prep.vraw_done, 1)
                            pe.wait_ge(prep.mT_done, 1)
                        prep.turn_qk(pe, 0, int(step[4:]))
                    elif step[:5] == "round":
                        for n in range(int(step[5:]), int(step[5:]) + 2):
                            prep.score(pe, 0, n, *round_of(n))
                    elif step == "values":
                        pe.wait_ge(prep.max_done, 8)
                        prep.project_values(pe, 0)
                    elif step == "maxima":
                        prep.turn_maxima(pe, 0, 0)
            turns(pe, turn)


class FeedForwardInput:

    def __init__(self, nc, ctx, X, ident, split):
        def sb(name, shape, dt=F32):
            return ctx.enter_context(nc.sbuf_tensor(f"fx_{name}", shape, dt))

        def sem(name):
            return ctx.enter_context(nc.semaphore(f"fx_{name}"))

        NT, D = X.shape[1], X.shape[2]
        self.nc, self.ident, self.DC = nc, ident, D // P
        self.NQ = 2
        self.ln = Layernorm(nc, X, sb, sem)
        self.hi, self.lo = [s[:].rearrange("p r c k -> p (r c k)")[:, 0:D * NT].rearrange("p (c t) -> p c t", c=D // P)
                            for s in split]
        self.xn_done = sem("xn_done")
        self.turned = sem("turned")
        self.hi_done = sem("hi_done")
        self.lo_done = sem("lo_done")

    def part(self, x, b):
        return x[:, :, b * self.NQ * P:(b + 1) * self.NQ * P]

    def layernorm(self, b, XN):
        for t in range(self.NQ):
            self.ln.normalize(XN[:, t, :], self.NQ * b + t).then_inc(self.xn_done, 1)

    def turn(self, pe, b, XN, ps):
        pe.wait_ge(self.xn_done, self.NQ * (b + 1))
        for c in range(self.DC):
            for t in range(self.NQ):
                n = self.NQ * c + t
                last = self.nc.tensor.transpose(ps[:, n * P:(n + 1) * P], XN[:, t, c * P:(c + 1) * P], self.ident[:])
        last.then_inc(self.turned, 1)

    def hi_part(self, act, b, ps):
        act.wait_ge(self.turned, b + 1)
        self.nc.scalar.activation(self.part(self.hi, b), ps.rearrange("p (c q) -> p c q", c=self.DC), ACT.Copy
                                  ).then_inc(self.hi_done, 1)

    def lo_part(self, dve, b, ps):
        dve.wait_ge(self.hi_done, b + 1)
        self.nc.vector.tensor_tensor(self.part(self.lo, b), ps.rearrange("p (c q) -> p c q", c=self.DC),
                                     self.part(self.hi, b).bitcast(F32), ALU.subtract).then_inc(self.lo_done, 1)


def self_attention(nc, X, prep, ffx, wout_dram, bout_dram, ident):
    HEADS, DH, DC, SQ, NQ, PAIRS, QUADS, ROWS, ROUNDS = (prep.HEADS, prep.DH, prep.DC, prep.SQ, prep.NQ, prep.PAIRS,
                                                         prep.QUADS, prep.ROWS, prep.ROUNDS)
    NT, D = X.shape[1], X.shape[2]
    B = NT // NQ
    SCALE = float(DH) ** -0.5
    RING = 4

    PHI_LAG, PV_LAG, COPY_LAG, BACK_LAG, NORM_LAG = 1, 3, 5, 6, 9
    TURN_X, QK, TURN_O, PROJECT_O = 2, (4, 5), 7, 8
    TURN_QK = (7, 10, 13, 16)
    MAXIMA = (8, 11, 14, 17)
    VALUES, SPLIT_VALUES = 10, (17, 19)
    FIRST_REST = 1
    FEED_ROOT, FEED_NORM, FEED_TURN, FEED_SPLIT = 0, (1, 1, 2), (4, 5, 6), (8, 8, 8)
    TURN_M = (13, 21)

    with ExitStack() as ctx:
        def sb(name, shape, dt=F32):
            return ctx.enter_context(nc.sbuf_tensor(f"sa_{name}", shape, dt))

        def sem(name):
            return ctx.enter_context(nc.semaphore(f"sa_{name}"))

        wo_raw = sb("wo_raw", [P, DC, D])
        wo_hi = sb("wo_hi", [P, DC, D], F32R)
        wo_lo = sb("wo_lo", [P, DC, D], F32R)
        bias = sb("bias", [P, 1, D])
        sel = sb("sel", [P, HEADS, P], F32R)
        v4 = sb("v4", [P, NQ, HEADS, 2 * ROWS], F32R)
        probs = sb("probs", [P, RING, NQ, SQ])
        p_hi = sb("p_hi", [P, RING, NQ, SQ], F32R)
        p_lo = sb("p_lo", [P, RING, NQ, SQ], F32R)
        aT = sb("aT", [P, 2, SQ])
        rinv = sb("rinv", [P, NQ * 4])
        num = sb("num", [P, NQ * 4, DH])
        O = sb("O", [P, NQ, D])
        oT_hi = sb("oT_hi", [P, DC, SQ], F32R)
        oT_lo = sb("oT_lo", [P, DC, SQ], F32R)

        bank = [ctx.enter_context(nc.psum_tensor(f"sa_bank{k}", [P, BANK], F32)) for k in range(8)]
        psOT, psP = bank[2], bank[2]
        prep.use_banks(psX=bank[2], psQK=bank[0:2], psV=bank[2], psM=bank[2])
        XF = sb("XF", [P, NT - NQ, D])
        psF = [bank[0], bank[1], bank[3]]
        ln, v_raw = prep.ln, prep.v_raw
        psE, psO, psB = bank[3:5], bank[5], bank[6:8]

        wo_in = sem("wo_in")
        bias_in = sem("bias_in")
        wohi_done = sem("wohi_done")
        wolo_done = sem("wolo_done")
        constants = sem("constants")
        sel_done = sem("sel_done")
        biased = sem("biased")
        vhi_done = sem("vhi_done")
        vlo_done = sem("vlo_done")
        st_done = sem("st_done")
        exp_done = sem("exp_done")
        phi_done = sem("phi_done")
        plo_done = sem("plo_done")
        pv_done = sem("pv_done")
        aT_done = sem("aT_done")
        back_done = sem("back_done")
        rinv_done = sem("rinv_done")
        num_done = sem("num_done")
        norm_done = sem("norm_done")
        oturned = sem("oturned")
        othi_done = sem("othi_done")
        otlo_done = sem("otlo_done")
        projected = sem("projected")
        added = sem("added")

        def turns(eng, turn):
            turn(1, True, True, False)
            with eng.Fori(2, B) as i:
                turn(i, True, True, True)
            turn(B, False, True, True)
            turn(B + 1, False, False, True)

        def last_turn(i):
            return isinstance(i, int) and i == B + 1

        def behind(i, k, lag, heads, finish):
            if k >= lag:
                return (i - 1, k - lag) if heads else None
            return (i - 2, k - lag + HEADS) if finish else None

        def prepared(i, k, slots, start, heads):
            if k in slots and start:
                return i, slots.index(k)
            if k + HEADS in slots and heads:
                return i - 1, slots.index(k + HEADS)
            return None

        def slots_of(slots, k):
            return [b for b, slot in enumerate(slots) if slot == k]

        def ring_free(b, h):
            return HEADS * b + h + 1 - RING

        def rounds_of(i, k, start, heads):
            for half in range(2):
                found = prepared(i, k, [s + half for s in MAXIMA], start, heads)
                if found:
                    b, u = found
                    for t in range(NQ):
                        yield b, 4 * u + 2 * half + t, t, 2 * u + half

        def values_of(x, half, s):
            cols = slice(half * D // 2, (half + 1) * D // 2)
            return x[:, :, cols].rearrange("p t (g s d) -> p t g s d", s=2, d=DH)[:, :, :, s, :]

        def value_columns(half, s, first):
            heads_of = slice(half * HEADS // 2 + s, (half + 1) * HEADS // 2, 2)
            return v4[:, :, heads_of, s * ROWS + first:s * ROWS + first + DH]

        block = ctx.enter_context(nc.Block())

        @block.sync
        def _(sp):
            sp.dma_start(wo_raw[:], wout_dram.rearrange("(c p) n -> p c n", p=P)).then_inc(wo_in, 16)
            sp.dma_start(bias[:], bout_dram.rearrange("(a b n) -> a b n", a=1, b=1).to_broadcast([P, 1, D])).then_inc(bias_in, 16)

        @block.gpsimd
        def _(pool):
            for s in range(2):
                other = slice((1 - s) * ROWS, (2 - s) * ROWS)
                nc.gpsimd.memset(v4[:, :, s::2, other].bitcast(F32), 0.0)
                ones = slice(s * ROWS + 2 * DH, (s + 1) * ROWS)
                last = nc.gpsimd.memset(v4[:, :, s::2, ones].bitcast(F32), 1.0)
                last.then_inc(constants, 1)
            pool.wait_ge(bias_in, 16)

            def add_bias(b):
                pool.wait_ge(prep.xn_done, NQ * (b + 1))
                x = X[:, bass.ds(NQ * b, NQ), :]
                nc.gpsimd.tensor_tensor(x, x, bias[:].to_broadcast([P, NQ, D]), ALU.add).then_inc(biased, 1)

            def turn(i, start, heads, finish):
                for k in range(HEADS):
                    if k == 1 and isinstance(i, int) and i == 1:
                        add_bias(0)
                    if k == 1 and start:
                        add_bias(i)
                    found = behind(i, k, PHI_LAG, heads, finish)
                    if found:
                        b, h = found
                        r = h % RING
                        pool.wait_ge(phi_done, HEADS * b + h + 1)
                        wait(pool, pv_done, ring_free(b, h))
                        nc.gpsimd.tensor_tensor(p_lo[:, r], probs[:, r], p_hi[:, r].bitcast(F32),
                                                ALU.subtract).then_inc(plo_done, 1)
            turns(pool, turn)

        @block.scalar
        def _(act):
            ln.roots(act, 1, slice(2 * NQ, NT))

            def turn(i, start, heads, finish):
                for k in range(HEADS):
                    found = behind(i, k, COPY_LAG, heads, finish)
                    if found and found[1] % 2 == 0:
                        b, g = found[0], found[1] // 2
                        act.wait_ge(pv_done, HEADS * b + 2 * g + 2)
                        wait(act, back_done, PAIRS * b + g - 1)
                        nc.scalar.activation(aT[:, g % 2, :], psO[:, 0:SQ], ACT.Copy).then_inc(aT_done, 1)
                    if heads:
                        b = i - 1
                        act.wait_ge(st_done, HEADS * b + k + 1)
                        wait(act, plo_done, ring_free(b, k))
                        nc.scalar.activation(probs[:, k % RING], psE[k % 2][:].rearrange("p (t q) -> p t q", t=NQ),
                                             ACT.Exp, scale=SCALE).then_inc(exp_done, 1)
                    found = behind(i, k, PHI_LAG, heads, finish)
                    if found:
                        b, h = found
                        act.wait_ge(exp_done, HEADS * b + h + 1)
                        wait(act, pv_done, ring_free(b, h))
                        nc.scalar.activation(p_hi[:, h % RING], probs[:, h % RING], ACT.Copy).then_inc(phi_done, 1)
                    if last_turn(i):
                        if k == FEED_ROOT:
                            ffx.ln.roots(act, 0, slice(0, NT - NQ))
                        for b in slots_of(FEED_SPLIT, k):
                            ffx.hi_part(act, b, psF[b][:])
                    if start and k == TURN_X:
                        prep.x_hi_part(act, i)
                    if finish and k == TURN_O:
                        act.wait_ge(oturned, i - 1)
                        nc.scalar.activation(oT_hi[:], psOT[:].rearrange("p (c q) -> p c q", c=DC), ACT.Copy).then_inc(othi_done, 1)
                    if start and k in QK:
                        prep.qk_hi_parts(act, i, QK.index(k))
                    found = prepared(i, k, TURN_QK, start, heads)
                    if found:
                        prep.copy_other_queries(act, *found)
                    if start and k == VALUES:
                        act.wait_ge(vlo_done, 4 * i)
                        prep.save_values(act, i)
                    found = prepared(i, k, SPLIT_VALUES, start, heads)
                    if found:
                        b, half = found
                        act.wait_ge(prep.vraw_done, b + 1)
                        if isinstance(i, int) and i == 1:
                            act.wait_ge(constants, 2)
                        wait(act, pv_done, HEADS * (b - 1) + (half + 1) * HEADS // 2)
                        for s in range(2):
                            nc.scalar.activation(value_columns(half, s, 0), values_of(v_raw, half, s), ACT.Copy).then_inc(vhi_done, 1)
                    found = prepared(i, k, TURN_M, start, heads)
                    if found:
                        prep.save_maxima(act, *found)
                if isinstance(i, int) and i == 1:
                    act.wait_ge(wo_in, 16)
                    nc.scalar.activation(wo_hi[:], wo_raw[:], ACT.Copy).then_inc(wohi_done, 1)
            turns(act, turn)

        @block.vector
        def _(dve):
            def normalize(b, quad):
                n = QUADS * b + quad + 1
                dve.wait_ge(back_done, PAIRS * b + 2 * quad + 2)
                out = psB[quad % 2][:].rearrange("p (n r) -> p n r", r=ROWS)
                wait(dve, norm_done, n - 1)
                nc.vector.reciprocal(rinv[:], out[:, :, 2 * DH]).then_inc(rinv_done, 1)
                nc.vector.tensor_reduce(num[:], out[:, :, 0:2 * DH].rearrange("p n (u d) -> p n d u", u=2),
                                        AX.X, ALU.add).then_inc(num_done, 1)
                if quad == 0:
                    wait(dve, oturned, b)
                dve.wait_ge(rinv_done, n)
                dve.wait_ge(num_done, n)
                dst = O[:, :, quad * 4 * DH:(quad + 1) * 4 * DH].rearrange("p t (h d) -> p t h d", d=DH)
                scale = rinv[:].rearrange("p (t h a) -> p t h a", t=NQ, a=1).to_broadcast([P, NQ, 4, DH])
                nc.vector.tensor_tensor(dst, num[:].rearrange("p (t h) d -> p t h d", t=NQ), scale, ALU.mult).then_inc(norm_done, 1)

            def spread_selectors(half):
                own = slice(half * HEADS // 2, (half + 1) * HEADS // 2)
                source = prep.pick[:, own].rearrange("p (h a) -> p h a", a=1).to_broadcast([P, HEADS // 2, P])
                nc.vector.tensor_copy(sel[:, own], source).then_inc(sel_done, 1)

            dve.wait_ge(prep.pick_in, 16)
            spread_selectors(0)
            ln.moments(dve, 2 * NQ, NT)
            ln.variances(dve, 2 * NQ, NT)

            def turn(i, start, heads, finish):
                if start:
                    prep.layernorm(dve, i)
                for k in range(HEADS):
                    if isinstance(i, int) and i == 1 and k == FIRST_REST:
                        spread_selectors(1)
                        ln.inverses(dve, 2 * NQ, NT, 1)
                    if isinstance(i, int) and i == B:
                        if k == TURN_O:
                            dve.wait_ge(added, B - 2)
                            ffx.ln.moments(dve, 0, (B - 2) * NQ)
                        if k == PROJECT_O + 2:
                            dve.wait_ge(added, B - 1)
                            ffx.ln.moments(dve, (B - 2) * NQ, (B - 1) * NQ)
                            ffx.ln.variances(dve, 0, (B - 1) * NQ)
                    if start and k == TURN_X:
                        prep.x_lo_part(dve, i)
                    if finish and k == TURN_O:
                        dve.wait_ge(othi_done, i - 1)
                        nc.vector.tensor_tensor(oT_lo[:], psOT[:].rearrange("p (c q) -> p c q", c=DC), oT_hi[:].bitcast(F32),
                                                ALU.subtract).then_inc(otlo_done, 1)
                    if finish and k == PROJECT_O + 1:
                        b = i - 2
                        dve.wait_ge(projected, b + 1)
                        dve.wait_ge(biased, b + 1)
                        x = X[:, bass.ds(NQ * b, NQ), :]
                        nc.vector.tensor_tensor(x, psP[:].rearrange("p (t e) -> p t e", t=NQ), x, ALU.add).then_inc(added, 1)
                    if start and k in QK:
                        prep.qk_lo_parts(dve, i, QK.index(k))
                    found = prepared(i, k, TURN_QK, start, heads)
                    if found:
                        prep.copy_keys_and_queries(dve, *found)
                    for b, n, t, g in rounds_of(i, k, start, heads):
                        prep.maximum(dve, b, n, t, g)
                    found = prepared(i, k, (MAXIMA[1] + 1, MAXIMA[3] + 1), start, heads)
                    if found:
                        prep.split_maxima(dve, *found)
                    found = prepared(i, k, SPLIT_VALUES, start, heads)
                    if found:
                        b, half = found
                        dve.wait_ge(vhi_done, 4 * b + 2 * half + 2)
                        for s in range(2):
                            nc.vector.tensor_tensor(value_columns(half, s, DH), values_of(v_raw, half, s),
                                                    value_columns(half, s, 0).bitcast(F32), ALU.subtract).then_inc(vlo_done, 1)
                    found = behind(i, k, NORM_LAG, heads, finish)
                    if found and found[1] % 4 == 0:
                        normalize(found[0], found[1] // 4)
                    if last_turn(i):
                        if k == FEED_NORM[0]:
                            ffx.ln.inverses(dve, 0, NT - NQ, 0)
                        for b in slots_of(FEED_NORM, k):
                            ffx.layernorm(b, XF[:, NQ * b:NQ * (b + 1)])
                        for b in slots_of(FEED_SPLIT, k):
                            ffx.lo_part(dve, b, psF[b][:])
                if isinstance(i, int) and i == 1:
                    dve.wait_ge(wohi_done, 1)
                    nc.vector.tensor_tensor(wo_lo[:], wo_raw[:], wo_hi[:].bitcast(F32), ALU.subtract).then_inc(wolo_done, 1)
            turns(dve, turn)

        @block.tensor
        def _(pe):
            def turn(i, start, heads, finish):
                for k in range(HEADS):
                    if heads:
                        b, h = i - 1, k
                        if k in (0, HEADS // 2) and isinstance(i, int) and i == 1:
                            pe.wait_ge(sel_done, k // (HEADS // 2) + 1)
                        if k in (0, HEADS // 2):
                            pe.wait_ge(prep.mT_done, 2 * b + k // (HEADS // 2) + 1)
                        wait(pe, exp_done, HEADS * b + h - 1)
                        for t in range(NQ):
                            ps = psE[h % 2][:, t * SQ:(t + 1) * SQ]
                            nc.tensor.matmul(ps, prep.kT[:, h // 2, t * P:(t + 1) * P], prep.qz[:, h, :], start=True, stop=False)
                            last = nc.tensor.matmul(ps, sel[:, h, :], prep.mT[:, h // (HEADS // 2), :], start=False, stop=True)
                        last.then_inc(st_done, 1)
                    if last_turn(i):
                        for b in slots_of(FEED_TURN, k):
                            ffx.turn(pe, b, XF[:, NQ * b:NQ * (b + 1)], psF[b])
                    if start and k == TURN_X:
                        prep.turn_x(pe, i)
                    if finish and k == TURN_O:
                        b = i - 2
                        pe.wait_ge(norm_done, QUADS * (b + 1))
                        pe.wait_ge(prep.mT_done, 2 * (min(i, B) if isinstance(i, int) else i))
                        for c in range(DC):
                            for t in range(NQ):
                                last = nc.tensor.transpose(psOT[:, c * SQ + t * P:c * SQ + (t + 1) * P],
                                                           O[:, t, c * P:(c + 1) * P], ident[:])
                        last.then_inc(oturned, 1)
                    if finish and k == PROJECT_O:
                        b = i - 2
                        pe.wait_ge(otlo_done, b + 1)
                        pe.wait_ge(wolo_done, 1)
                        for t in range(NQ):
                            n = 0
                            for a, w in ((oT_hi, wo_hi), (oT_lo, wo_hi), (oT_hi, wo_lo)):
                                for c in range(DC):
                                    last = nc.tensor.matmul(psP[:, t * D:(t + 1) * D], a[:, c, t * P:(t + 1) * P], w[:, c, :],
                                                            start=(n == 0), stop=(n == 3 * DC - 1))
                                    n += 1
                        last.then_inc(projected, 1)
                    if start and k in QK:
                        prep.project_qk(pe, i, QK.index(k))
                    found = prepared(i, k, TURN_QK, start, heads)
                    if found:
                        prep.turn_qk(pe, *found)
                    for b, n, t, g in rounds_of(i, k, start, heads):
                        prep.score(pe, b, n, t, g)
                    if start and k == VALUES:
                        if finish:
                            pe.wait_ge(added, i - 1)
                        prep.project_values(pe, i)
                    found = behind(i, k, PV_LAG, heads, finish)
                    if found:
                        b, h = found
                        g = h // 2
                        pe.wait_ge(plo_done, HEADS * b + h + 1)
                        if h in (0, HEADS // 2):
                            pe.wait_ge(vlo_done, 4 * b + 2 * (h // (HEADS // 2)) + 2)
                        if h % 2 == 0:
                            wait(pe, aT_done, PAIRS * b + g)
                        n = 4 * (h % 2)
                        for part in (p_hi, p_lo):
                            for t in range(NQ):
                                last = nc.tensor.matmul(psO[:, 0:SQ], v4[:, t, h, :], part[:, h % RING, t, :],
                                                        start=(n == 0), stop=(n == 7))
                                n += 1
                        last.then_inc(pv_done, 1)
                    found = behind(i, k, BACK_LAG, heads, finish)
                    if found and found[1] % 2 == 0:
                        b, g = found[0], found[1] // 2
                        pe.wait_ge(aT_done, PAIRS * b + g + 1)
                        if g % 2 == 0:
                            wait(pe, norm_done, QUADS * b + g // 2 - 1)
                        for t in range(NQ):
                            last = nc.tensor.transpose(psB[(g // 2) % 2][:, (2 * t + g % 2) * P:(2 * t + g % 2 + 1) * P],
                                                       aT[:, g % 2, t * P:(t + 1) * P], ident[:])
                        last.then_inc(back_done, 1)
                    found = prepared(i, k, TURN_M, start, heads)
                    if found:
                        b, half = found
                        if half == 0:
                            pe.wait_ge(prep.vraw_done, b + 1)
                        else:
                            pe.wait_ge(prep.mT_done, 2 * b + 1)
                            if start:
                                pe.wait_ge(prep.xlo_done, i + 1)
                        prep.turn_maxima(pe, b, half)
            turns(pe, turn)


def routed_ffn(nc, X, ffx, w, out_v, ident):
    NT, D = X.shape[1], X.shape[2]
    DC = D // P
    T = NT * P
    E = 64
    NG = 64
    TQ = T // NG
    BUDGET = TQ * 16
    NC = w["up_gate"].shape[0]
    HT = T // 2
    TH = T // BANK
    BIG = 3.0e38

    with ExitStack() as ctx:
        def sb(name, shape, dt=F32, ctx=ctx):
            return ctx.enter_context(nc.sbuf_tensor(f"ff_{name}", shape, dt))

        def sem(name, ctx=ctx):
            return ctx.enter_context(nc.semaphore(f"ff_{name}"))

        G = sb("G", [P, NC, T])
        RT = sb("RT", [E, T])
        fs_dram = nc.dram_tensor("fs_scratch", (E, T), F32, kind="Internal").ap()
        fnorm = sb("fnorm", [P, NT])
        bdown = sb("bdown", [E, D])
        scores = sb("scores", [P, 2, T])
        d_raw = sb("d_raw", [P, 2, D])
        gate = sb("gate", [P, 2, T])
        gated = sem("gated")

        bdown_in = sem("bdown_in")
        scores_in = [sem(f"scores_in{s}") for s in range(2)]
        d_in = [sem(f"d_in{s}") for s in range(2)]
        scaled = sem("scaled")

        def row(c):
            return G[:, bass.ds(c, 1), :].rearrange("p a t -> p (a t)")

        def gate_product(c, s):
            return nc.gpsimd.tensor_tensor(row(c), row(c), gate[:, s], ALU.mult)

        def load_scores(sp, c, s):
            for e in range(2):
                sp.dma_start(scores[e * NG:(e + 1) * NG, s], fs_dram[bass.ds(2 * c + e, 1), :].to_broadcast([NG, T])
                             ).then_inc(scores_in[s], 16)

        def scale(dve, c, s):
            dve.wait_ge(scores_in[s], 16 * (c - s) + 32)
            nc.vector.tensor_tensor(row(c), row(c), scores[:, s], ALU.mult).then_inc(scaled, 1)

        with ExitStack() as one:
            def sb1(name, shape, dt=F32):
                return sb(name, shape, dt, one)

            def sem1(name):
                return sem(name, one)

            xT_hi, xT_lo = ffx.hi, ffx.lo
            wr_raw = sb1("wr_raw", [P, DC, E])
            wr_hi = sb1("wr_hi", [P, DC, E], F32R)
            wr_lo = sb1("wr_lo", [P, DC, E], F32R)
            br = sb1("br", [E, 1])
            bup = sb1("bup", [P, NC])
            bgate = sb1("bgate", [P, NC])
            diag = sb1("diag", [P, E])
            tq_of = sb1("tq_of", [P, TQ // 2])
            w_raw = sb1("w_raw", [P, 2, 2, DC, P])
            w_hi = sb1("w_hi", [P, 2, 2, DC, P], F32R)
            w_lo = sb1("w_lo", [P, 2, 2, DC, P], F32R)
            buf_a = sb1("buf_a", [P, T])
            buf_b = sb1("buf_b", [P, T])
            buf_c = sb1("buf_c", [P, T])
            buf_d = sb1("buf_d", [P, T])
            XN = gate[:, 0, 0:ffx.NQ * D].rearrange("p (t d) -> p t d", d=D)
            R = buf_b[:, 0:NT * E].rearrange("p (t e) -> p t e", e=E)
            sort_x, sort_y = buf_c[:, 0:HT], buf_c[:, HT:T]
            small = sb1("small", [P, 16, 8])
            ones = sb1("ones", [P, P])
            rowcount = sb1("rowcount", [P, E])
            psU = one.enter_context(nc.psum_tensor("ff_psU", [P, T], F32))
            psG = one.enter_context(nc.psum_tensor("ff_psG", [P, T], F32))
            psR = one.enter_context(nc.psum_tensor("ff_psR", [P, T], F32))
            psL = one.enter_context(nc.psum_tensor("ff_psL", [P, BANK], F32))
            psD = one.enter_context(nc.psum_tensor("ff_psD", [P, BANK], F32))

            LAST = NT // ffx.NQ - 1
            psX = psL[:]

            router_in = sem1("router_in")
            small_in = sem1("small_in")
            w_in = [sem1(f"w_in{s}") for s in range(2)]
            wr_hi_done = sem1("wr_hi_done")
            wr_lo_done = sem1("wr_lo_done")
            ones_done = sem1("ones_done")
            whi_done = sem1("whi_done")
            wlo_done = sem1("wlo_done")
            up_done = sem1("up_done")
            gate_done = sem1("gate_done")
            silu_done = sem1("silu_done")
            biased_done = sem1("biased_done")
            logits_done = sem1("logits_done")
            logits_saved = sem1("logits_saved")
            logits_turned = sem1("logits_turned")
            shifted = sem1("shifted")
            router_exp = sem1("router_exp")
            scores_ready = sem1("scores_ready")
            scores_turned = sem1("scores_turned")
            step = sem1("step")
            spread_ready = sem1("spread_ready")
            spread_done = sem1("spread_done")
            kept_ready = sem1("kept_ready")
            fsum_done = sem1("fsum_done")
            fs_stored = sem1("fs_stored")

            SPREAD, SPREAD_MAX, SUM = 12, 16, 24

            block = one.enter_context(nc.Block())

            @block.sync
            def _(sp):
                def load(c):
                    wait(sp, whi_done, c - 1)
                    wait(sp, wlo_done, c - 1)
                    s = c % 2
                    sp.dma_start(w_raw[:, s], w["up_gate"][c]).then_inc(w_in[s], 16)

                sp.dma_start(wr_raw[:], w["router"].rearrange("(c p) e -> p c e", p=P)).then_inc(router_in, 16)
                load(0)
                load(1)
                for dst, src in ((br, "router_bias"), (bup, "up_bias"), (bgate, "gate_bias"), (diag, "diag"), (tq_of, "tq_of")):
                    sp.dma_start(dst[:], w[src]).then_inc(small_in, 16)
                with sp.Fori(1, NC // 2) as pair:
                    c = 2 * pair
                    for s in range(2):
                        sp.wait_ge(whi_done, c + s - 1)
                        sp.wait_ge(wlo_done, c + s - 1)
                        sp.dma_start(w_raw[:, s], w["up_gate"][c + s]).then_inc(w_in[s], 16)
                sp.wait_ge(kept_ready, 1)
                sp.dma_start(fs_dram, RT[:]).then_inc(fs_stored, 16)
                sp.dma_start(bdown[:], w["down_bias"]).then_inc(bdown_in, 16)
                for s in range(2):
                    sp.dma_start(d_raw[:, s], w["down"][s]).then_inc(d_in[s], 16)
                sp.wait_ge(fs_stored, 16)
                for s in range(2):
                    load_scores(sp, s, s)

            @block.scalar
            def _(act):
                def split(c, s):
                    act.wait_ge(w_in[s], 8 * (c - s) + 16)
                    wait(act, gate_done, c - 1)
                    nc.scalar.activation(w_hi[:, s], w_raw[:, s], ACT.Copy).then_inc(whi_done, 1)

                def gates(c, s):
                    act.wait_ge(up_done, c + 1)
                    nc.scalar.activation(G[:, bass.ds(c, 1), :].rearrange("p a t -> p (a t)"), psU[:], ACT.Silu,
                                         bias=bup[:, bass.ds(c, 1)]).then_inc(silu_done, 1)
                    act.wait_ge(gate_done, c + 1)
                    wait(act, gated, c - 1)
                    nc.scalar.activation(gate[:, s], psG[:], ACT.Identity, bias=bgate[:, bass.ds(c, 1)]).then_inc(biased_done, 1)

                ffx.ln.roots(act, 1, slice(NT - ffx.NQ, NT))
                act.wait_ge(router_in, 16)
                nc.scalar.activation(wr_hi[:], wr_raw[:], ACT.Copy).then_inc(wr_hi_done, 1)
                split(0, 0)
                ffx.hi_part(act, LAST, psX)
                act.wait_ge(small_in, 80)
                act.wait_ge(logits_done, 1)
                nc.scalar.activation(buf_a[0:E, :], psR[0:E, :], ACT.Identity, bias=br[:]).then_inc(logits_saved, 1)
                split(1, 1)
                gates(0, 0)
                act.wait_ge(shifted, 1)
                nc.scalar.activation(R, R, ACT.Exp).then_inc(router_exp, 1)
                split(2, 0)
                gates(1, 1)
                with act.Fori(1, (NC - 2) // 2) as pair:
                    c = 2 * pair
                    split(c + 1, 1)
                    gates(c, 0)
                    split(c + 2, 0)
                    gates(c + 1, 1)
                split(NC - 1, 1)
                gates(NC - 2, 0)
                gates(NC - 1, 1)

            @block.gpsimd
            def _(pool):
                nc.gpsimd.memset(ones[:], 1.0).then_inc(ones_done, 1)

                def split(c, s):
                    pool.wait_ge(whi_done, c + 1)
                    nc.gpsimd.tensor_tensor(w_lo[:, s], w_raw[:, s], w_hi[:, s].bitcast(F32), ALU.subtract).then_inc(wlo_done, 1)

                def product(c, s):
                    pool.wait_ge(silu_done, c + 1)
                    pool.wait_ge(biased_done, c + 1)
                    gate_product(c, s).then_inc(gated, 1)

                split(0, 0)
                split(1, 1)
                product(0, 0)
                split(2, 0)
                product(1, 1)
                with pool.Fori(1, (NC - 2) // 2) as pair:
                    c = 2 * pair
                    split(c + 1, 1)
                    product(c, 0)
                    split(c + 2, 0)
                    product(c + 1, 1)
                split(NC - 1, 1)
                product(NC - 2, 0)

            @block.tensor
            def _(pe):
                def router(h):
                    cols = slice(h * BANK, (h + 1) * BANK)
                    n = 0
                    for a, b in ((wr_hi, xT_hi), (wr_hi, xT_lo), (wr_lo, xT_hi)):
                        for k in range(DC):
                            last = nc.tensor.matmul(psR[0:E, cols], a[:, k, :], b[:, k, cols],
                                                    start=(n == 0), stop=(n == 3 * DC - 1))
                            n += 1
                    return last

                def project(ps, s, u, h):
                    cols = slice(h * BANK, (h + 1) * BANK)
                    n = 0
                    for a, b in ((w_hi, xT_hi), (w_hi, xT_lo), (w_lo, xT_hi)):
                        for k in range(DC):
                            last = nc.tensor.matmul(ps[:, cols], a[:, s, u, k, :], b[:, k, cols],
                                                    start=(n == 0), stop=(n == 3 * DC - 1))
                            n += 1
                    return last

                def hidden(c, s):
                    pe.wait_ge(wlo_done, c + 1)
                    for u, (ps, done, left) in enumerate(((psU, up_done, silu_done), (psG, gate_done, biased_done))):
                        wait(pe, left, c)
                        for h in range(TH):
                            last = project(ps, s, u, h)
                        last.then_inc(done, 1)

                def run(first, last):
                    with pe.Fori(first // 2, last // 2) as pair:
                        c = 2 * pair
                        hidden(c, 0)
                        hidden(c + 1, 1)

                ffx.turn(pe, LAST, XN, psX)
                pe.wait_ge(ffx.lo_done, LAST)
                pe.wait_ge(wr_lo_done, 1)
                router(0)
                pe.wait_ge(wlo_done, 1)
                project(psU, 0, 0, 0)
                project(psG, 0, 1, 0)
                pe.wait_ge(ffx.lo_done, LAST + 1)
                router(1).then_inc(logits_done, 1)
                project(psU, 0, 0, 1).then_inc(up_done, 1)
                project(psG, 0, 1, 1).then_inc(gate_done, 1)
                pe.wait_ge(logits_saved, 1)
                for t in range(NT):
                    last = nc.tensor.transpose(psL[:, t * E:(t + 1) * E], buf_a[0:E, t * P:(t + 1) * P], ident[0:E, 0:E])
                last.then_inc(logits_turned, 1)
                hidden(1, 1)
                pe.wait_ge(scores_ready, 1)
                for t in range(NT):
                    last = nc.tensor.transpose(psR[0:E, t * P:(t + 1) * P], R[:, t, :], ident[:])
                last.then_inc(scores_turned, 1)
                run(2, SPREAD)
                pe.wait_ge(ones_done, 1)
                pe.wait_ge(spread_ready, 1)
                for h in range(TH):
                    cols = slice(h * BANK, (h + 1) * BANK)
                    last = nc.tensor.matmul(psR[:, cols], ones[:], buf_b[:, cols], start=True, stop=True)
                last.then_inc(spread_done, 1)
                run(SPREAD, SPREAD_MAX)
                pe.wait_ge(spread_ready, 2)
                nc.tensor.matmul(psL[:, 0:P], ones[:], buf_b[:, 0:P], start=True, stop=True).then_inc(spread_done, 1)
                run(SPREAD_MAX, SUM)
                pe.wait_ge(kept_ready, 1)
                for t in range(NT):
                    last = nc.tensor.matmul(psD[:, 2 * t:2 * t + 2], RT[:, t * P:(t + 1) * P], ones[0:E, 0:2],
                                            start=True, stop=True)
                last.then_inc(fsum_done, 1)
                run(SUM, NC)

            @block.vector
            def _(dve):
                steps = [0]

                def tick():
                    steps[0] += 1
                    return 1

                def col(k, n=1):
                    return small[:, k, 0:n]

                ffx.ln.statistics(dve, NT - ffx.NQ, NT, 1)
                ffx.layernorm(LAST, XN)
                dve.wait_ge(wr_hi_done, 1)
                nc.vector.tensor_tensor(wr_lo[:], wr_raw[:], wr_hi[:].bitcast(F32), ALU.subtract).then_inc(wr_lo_done, 1)
                ffx.lo_part(dve, LAST, psX)

                dve.wait_ge(logits_turned, 1)
                logits = psL[:].rearrange("p (t e) -> p t e", e=E)

                def over_experts(k):
                    return small[:, k, 0:NT].rearrange("p (t a) -> p t a", a=1).to_broadcast([P, NT, E])

                nc.vector.tensor_reduce(small[:, 0, 0:NT], logits, AX.X, ALU.max).then_inc(step, tick())
                dve.wait_ge(step, steps[0])
                nc.vector.tensor_tensor(R, logits, over_experts(0), ALU.subtract).then_inc(shifted, 1)
                dve.wait_ge(router_exp, 1)
                nc.vector.tensor_reduce(small[:, 1, 0:NT], R, AX.X, ALU.add).then_inc(step, tick())
                dve.wait_ge(step, steps[0])
                nc.vector.reciprocal(small[:, 2, 0:NT], small[:, 1, 0:NT]).then_inc(step, tick())
                dve.wait_ge(step, steps[0])
                nc.vector.tensor_tensor(R, R, over_experts(2), ALU.mult).then_inc(scores_ready, 1)

                dve.wait_ge(scores_turned, 1)
                nc.vector.tensor_copy(RT[:], psR[0:E, :]).then_inc(step, tick())
                nc.vector.tensor_copy(sort_x[0:E, :], psR[0:E, 0:HT]).then_inc(step, tick())
                nc.vector.tensor_copy(sort_x[E:P, :], psR[0:E, HT:T]).then_inc(step, tick())

                src, dst = sort_x, sort_y

                def compare(a, b, big, less):
                    nonlocal src, dst
                    dve.wait_ge(step, steps[0])
                    nc.vector.tensor_tensor(big, a, b, ALU.max).then_inc(step, tick())
                    nc.vector.tensor_tensor(less, a, b, ALU.min).then_inc(step, tick())
                    src, dst = dst, src

                def by_distance(j):
                    a = src[:].rearrange("p (n u j) -> p n u j", u=2, j=j)
                    b = dst[:].rearrange("p (n u j) -> p n u j", u=2, j=j)
                    compare(a[:, :, 0, :], a[:, :, 1, :], b[:, :, 0, :], b[:, :, 1, :])

                k = 2
                while k <= HT:
                    a = src[:].rearrange("p (n k) -> p n k", k=k)
                    b = dst[:].rearrange("p (n k) -> p n k", k=k)
                    mirrored = slice(k - 1, k // 2 - 1, -1)
                    compare(a[:, :, 0:k // 2], a[:, :, mirrored], b[:, :, 0:k // 2], b[:, :, mirrored])
                    j = k // 4
                    while j:
                        by_distance(j)
                        j //= 2
                    k *= 2
                dve.wait_ge(step, steps[0])
                nc.vector.tensor_copy(dst[0:E, :], src[E:P, :]).then_inc(step, tick())
                nc.vector.tensor_copy(dst[E:P, :], src[0:E, :]).then_inc(step, tick())
                dve.wait_ge(step, steps[0])
                nc.vector.tensor_tensor(buf_a[0:E, 0:HT], src[0:E, :], dst[0:E, ::-1], ALU.max).then_inc(step, tick())
                nc.vector.tensor_tensor(buf_a[E:P, 0:HT], src[E:P, :], dst[E:P, ::-1], ALU.min).then_inc(step, tick())
                src = buf_a[:, 0:HT]
                ring = [sort_x[:], sort_y[:], sort_x[:]]
                for n, j in enumerate((HT // 2, HT // 4, NG)):
                    a = src.rearrange("p (n u j) -> p n u j", u=2, j=j)
                    b = ring[n].rearrange("p (n u j) -> p n u j", u=2, j=j)
                    dve.wait_ge(step, steps[0])
                    nc.vector.tensor_tensor(b[:, :, 0, :], a[:, :, 0, :], a[:, :, 1, :], ALU.max).then_inc(step, tick())
                    nc.vector.tensor_tensor(b[:, :, 1, :], a[:, :, 0, :], a[:, :, 1, :], ALU.min).then_inc(step, tick())
                    src = ring[n]
                dve.wait_ge(step, steps[0])
                H8 = TQ // 2
                groups = src.rearrange("p (g n) -> p g n", n=NG)
                gsum, gmin = small[:, 3, 0:H8], small[:, 4, 0:H8]
                nc.vector.tensor_reduce(gmin, groups, AX.X, ALU.min).then_inc(step, tick())
                dve.wait_ge(step, steps[0])
                nc.vector.tensor_reduce(gsum, groups, AX.X, ALU.add).then_inc(step, tick())
                dve.wait_ge(step, steps[0])

                nc.vector.tensor_tensor(buf_b[:].rearrange("p (g q) -> p g q", g=H8),
                                        gsum.rearrange("p (g a) -> p g a", a=1).to_broadcast([P, H8, P]),
                                        ident[:].rearrange("p (a q) -> p a q", a=1).to_broadcast([P, H8, P]),
                                        ALU.mult).then_inc(spread_ready, 1)
                dve.wait_ge(spread_done, 1)
                allsums = buf_c
                nc.vector.tensor_copy(allsums[:].rearrange("p (h g e) -> p h g e", h=2, g=H8),
                                      psR.rearrange("p (g h e) -> p h g e", h=2, g=H8)).then_inc(step, tick())
                dve.wait_ge(step, steps[0])
                for g in range(H8):
                    nc.vector.tensor_scalar(buf_d[:], allsums[:], small[:, 3, g:g + 1], None, ALU.is_ge, ALU.add,
                                            accum_out=small[:, 5, g:g + 1]).then_inc(step, tick())
                    dve.wait_ge(step, steps[0])
                nc.vector.scalar_tensor_tensor(small[:, 6, 0:H8], small[:, 5, 0:H8], float(BUDGET), gsum,
                                               ALU.is_ge, ALU.mult).then_inc(step, tick())
                dve.wait_ge(step, steps[0])
                nc.vector.tensor_reduce(col(7), small[:, 6, 0:H8], AX.X, ALU.max).then_inc(step, tick())
                dve.wait_ge(step, steps[0])
                nc.vector.tensor_scalar(buf_b[:, 0:P], ident[:], col(7), None, ALU.mult).then_inc(spread_ready, 1)
                dve.wait_ge(spread_done, 2)
                threshold = col(8)
                nc.vector.tensor_reduce(threshold, psL[:, 0:P], AX.X, ALU.max).then_inc(step, tick())
                dve.wait_ge(step, steps[0])
                above, equal, upto = buf_d, buf_a, buf_b
                nc.vector.tensor_scalar(above[:], allsums[:], threshold, None, ALU.is_gt, ALU.add, accum_out=col(10)).then_inc(step, tick())
                nc.vector.tensor_scalar(equal[:], allsums[:], threshold, None, ALU.is_equal).then_inc(step, tick())
                dve.wait_ge(step, steps[0])
                nc.vector.tensor_scalar(col(11), col(10), -1.0, float(BUDGET), ALU.mult, ALU.add).then_inc(step, tick())
                nc.vector.tensor_tensor_scan(upto[:], equal[:], equal[:], 0.0, ALU.add, ALU.max).then_inc(step, tick())
                dve.wait_ge(step, steps[0])
                nc.vector.scalar_tensor_tensor(equal[:], upto[:], col(11), equal[:], ALU.is_le, ALU.mult).then_inc(step, tick())
                dve.wait_ge(step, steps[0])
                nc.vector.tensor_tensor(above[:], above[:], equal[:], ALU.add).then_inc(step, tick())
                dve.wait_ge(step, steps[0])
                nc.vector.tensor_reduce(rowcount[:], above[:].rearrange("p (q e) -> p e q", e=E), AX.X, ALU.add).then_inc(step, tick())
                dve.wait_ge(step, steps[0])
                nc.vector.tensor_tensor(rowcount[:], rowcount[:], diag[:], ALU.mult).then_inc(step, tick())
                dve.wait_ge(step, steps[0])
                nc.vector.tensor_reduce(col(12), rowcount[:], AX.X, ALU.add).then_inc(step, tick())
                dve.wait_ge(step, steps[0])
                nc.vector.tensor_scalar(small[:, 13, 0:H8], tq_of[:], col(12), BIG, ALU.is_ge, ALU.mult).then_inc(step, tick())
                dve.wait_ge(step, steps[0])
                nc.vector.tensor_tensor(small[:, 13, 0:H8], small[:, 13, 0:H8], gmin, ALU.max).then_inc(step, tick())
                dve.wait_ge(step, steps[0])
                nc.vector.tensor_reduce(col(14), small[:, 13, 0:H8], AX.X, ALU.min).then_inc(step, tick())
                dve.wait_ge(step, steps[0])
                nc.vector.tensor_copy(small[0:E, 15, 0:1], small[E:P, 14, 0:1]).then_inc(step, tick())
                dve.wait_ge(step, steps[0])
                nc.vector.tensor_tensor(small[0:E, 15, 1:2], small[0:E, 15, 0:1], small[0:E, 14, 0:1], ALU.min).then_inc(step, tick())
                dve.wait_ge(step, steps[0])
                least = small[0:E, 15, 1:2]
                nc.vector.tensor_scalar(above[0:E, :], RT[:], least, None, ALU.is_gt, ALU.add, accum_out=small[0:E, 15, 2:3]).then_inc(step, tick())
                nc.vector.tensor_scalar(equal[0:E, :], RT[:], least, None, ALU.is_equal).then_inc(step, tick())
                nc.vector.tensor_scalar(small[0:E, 15, 3:4], small[0:E, 12, 0:1], float(NG), None, ALU.mult).then_inc(step, tick())
                dve.wait_ge(step, steps[0])
                nc.vector.tensor_tensor(small[0:E, 15, 4:5], small[0:E, 15, 3:4], small[0:E, 15, 2:3], ALU.subtract).then_inc(step, tick())
                nc.vector.tensor_tensor_scan(upto[0:E, :], equal[0:E, :], equal[0:E, :], 0.0, ALU.add, ALU.max).then_inc(step, tick())
                dve.wait_ge(step, steps[0])
                nc.vector.scalar_tensor_tensor(equal[0:E, :], upto[0:E, :], small[0:E, 15, 4:5], equal[0:E, :],
                                               ALU.is_le, ALU.mult).then_inc(step, tick())
                dve.wait_ge(step, steps[0])
                nc.vector.tensor_tensor(above[0:E, :], above[0:E, :], equal[0:E, :], ALU.add).then_inc(step, tick())
                dve.wait_ge(step, steps[0])
                nc.vector.tensor_tensor(RT[:], RT[:], above[0:E, :], ALU.mult).then_inc(kept_ready, 1)
                dve.wait_ge(fsum_done, 1)
                nc.vector.tensor_scalar(small[:, 0, 0:NT], psD[:, 0:2 * NT:2], 1e-6, None, ALU.add).then_inc(step, tick())
                dve.wait_ge(step, steps[0])
                nc.vector.reciprocal(fnorm[:], small[:, 0, 0:NT])
                for s in range(2):
                    dve.wait_ge(gated, s + 1)
                    scale(dve, s, s)

        with ExitStack() as two:
            def sb2(name, shape, dt=F32):
                return sb(name, shape, dt, two)

            def sem2(name):
                return sem(name, two)

            d_hi = sb2("d_hi", [P, 2, D], F32R)
            d_lo = sb2("d_lo", [P, 2, D], F32R)
            h_hi = sb2("h_hi", [P, 2, T], F32R)
            h_lo = sb2("h_lo", [P, 2, T], F32R)
            outT = sb2("outT", [P, DC, T])
            psOut = [[two.enter_context(nc.psum_tensor(f"ff_psOut{d}_{h}", [P, BANK], F32)) for h in range(TH)]
                     for d in range(DC)]
            psX = [two.enter_context(nc.psum_tensor(f"ff_psX{k}", [P, D], F32)) for k in range(4)]

            dhi_done = sem2("dhi_done")
            dlo_done = sem2("dlo_done")
            hhi_done = sem2("hhi_done")
            hlo_done = sem2("hlo_done")
            down_done = sem2("down_done")
            all_done = sem2("all_done")
            out0_done = sem2("out0_done")
            out1_done = sem2("out1_done")
            x_turned = sem2("x_turned")
            x_done = sem2("x_done")
            out_stored = sem2("out_stored")

            block = two.enter_context(nc.Block())

            @block.sync
            def _(sp):
                def load(c, s):
                    wait(sp, scaled, c - 1)
                    load_scores(sp, c, s)
                    wait(sp, dhi_done, c - 1)
                    wait(sp, dlo_done, c - 1)
                    sp.dma_start(d_raw[:, s], w["down"][c]).then_inc(d_in[s], 16)

                with sp.Fori(1, NC // 2) as pair:
                    c = 2 * pair
                    load(c, 0)
                    load(c + 1, 1)
                for t in range(NT):
                    sp.wait_ge(x_done, t + 1)
                    sp.dma_start(out_v[:, t, :], X[:, t, :]).then_inc(out_stored, 16)
                sp.wait_ge(out_stored, 16 * NT)

            @block.vector
            def _(dve):
                def split(c, s):
                    dve.wait_ge(hhi_done, c + 1)
                    wait(dve, down_done, c - 1)
                    nc.vector.tensor_tensor(h_lo[:, s], row(c), h_hi[:, s].bitcast(F32), ALU.subtract).then_inc(hlo_done, 1)

                split(0, 0)
                scale(dve, 2, 0)
                split(1, 1)
                with dve.Fori(1, NC // 2 - 1) as pair:
                    c = 2 * pair
                    scale(dve, c + 1, 1)
                    split(c, 0)
                    scale(dve, c + 2, 0)
                    split(c + 1, 1)
                dve.wait_ge(gated, NC)
                scale(dve, NC - 1, 1)
                split(NC - 2, 0)
                split(NC - 1, 1)
                for h in range(TH):
                    dve.wait_ge(all_done, h + 1)
                    nc.vector.tensor_copy(outT[:, 1, h * BANK:(h + 1) * BANK], psOut[1][h][:]).then_inc(out1_done, 1)
                for t in range(NT):
                    dve.wait_ge(x_turned, t + 1)
                    nc.vector.scalar_tensor_tensor(X[:, t, :], psX[t % 4][:], fnorm[:, t:t + 1], X[:, t, :],
                                                   ALU.mult, ALU.add).then_inc(x_done, 1)

            @block.scalar
            def _(act):
                def turn(c, s):
                    act.wait_ge(d_in[s], 8 * (c - s) + 16)
                    wait(act, down_done, c - 1)
                    nc.scalar.activation(d_hi[:, s], d_raw[:, s], ACT.Copy).then_inc(dhi_done, 1)
                    act.wait_ge(scaled, c + 1)
                    row = G[:, bass.ds(c, 1), :].rearrange("p a t -> p (a t)")
                    nc.scalar.activation(h_hi[:, s], row, ACT.Copy).then_inc(hhi_done, 1)

                turn(0, 0)
                turn(1, 1)
                with act.Fori(1, NC // 2) as pair:
                    c = 2 * pair
                    turn(c, 0)
                    turn(c + 1, 1)
                for h in range(TH):
                    act.wait_ge(all_done, h + 1)
                    nc.scalar.activation(outT[:, 0, h * BANK:(h + 1) * BANK], psOut[0][h][:], ACT.Copy).then_inc(out0_done, 1)

            @block.gpsimd
            def _(pool):
                def turn(c, s):
                    pool.wait_ge(dhi_done, c + 1)
                    nc.gpsimd.tensor_tensor(d_lo[:, s], d_raw[:, s], d_hi[:, s].bitcast(F32), ALU.subtract).then_inc(dlo_done, 1)

                turn(0, 0)
                turn(1, 1)
                gate_product(NC - 1, 1).then_inc(gated, 1)
                with pool.Fori(1, NC // 2) as pair:
                    c = 2 * pair
                    turn(c, 0)
                    turn(c + 1, 1)

            @block.tensor
            def _(pe):
                pe.wait_ge(bdown_in, 16)
                for d in range(DC):
                    for h in range(TH):
                        nc.tensor.matmul(psOut[d][h][:], bdown[:, d * P:(d + 1) * P], RT[:, h * BANK:(h + 1) * BANK],
                                         start=True, stop=False)

                def ready(c):
                    pe.wait_ge(dlo_done, c + 1)
                    pe.wait_ge(hhi_done, c + 1)

                def turn(c, s):
                    ready(c)
                    for n, (a, b) in enumerate(((d_hi, h_hi), (d_lo, h_hi), (d_hi, h_lo))):
                        if n == 2:
                            pe.wait_ge(hlo_done, c + 1)
                        for d in range(DC):
                            for h in range(TH):
                                last = nc.tensor.matmul(psOut[d][h][:], a[:, s, d * P:(d + 1) * P],
                                                        b[:, s, h * BANK:(h + 1) * BANK], start=False, stop=False)
                    last.then_inc(down_done, 1)

                with pe.Fori(0, (NC - 2) // 2) as pair:
                    turn(2 * pair, 0)
                    turn(2 * pair + 1, 1)
                turn(NC - 2, 0)
                ready(NC - 1)
                for h in range(TH):
                    for n, (a, b) in enumerate(((d_hi, h_hi), (d_lo, h_hi), (d_hi, h_lo))):
                        if n == 2:
                            pe.wait_ge(hlo_done, NC)
                        for d in range(DC):
                            last = nc.tensor.matmul(psOut[d][h][:], a[:, 1, d * P:(d + 1) * P],
                                                    b[:, 1, h * BANK:(h + 1) * BANK], start=False, stop=(n == 2))
                    last.then_inc(all_done, 1)
                for t in range(NT):
                    if t % (NT // TH) == 0:
                        pe.wait_ge(out0_done, t // (NT // TH) + 1)
                        pe.wait_ge(out1_done, t // (NT // TH) + 1)
                    wait(pe, x_done, t - 3)
                    for d in range(DC):
                        last = nc.tensor.transpose(psX[t % 4][:, d * P:(d + 1) * P], outT[:, d, t * P:(t + 1) * P], ident[:])
                    last.then_inc(x_turned, 1)


def perceiver_kernel(nc, x, ctx_, ctxT, mask, xw, xb, wqkv, wout, bout, ident_c, pick_c, ffn, out):
    B, S, D = x.shape
    NT = B * S // P
    with ExitStack() as ctx:
        X = ctx.enter_context(nc.sbuf_tensor("X", [P, NT, D], F32))
        ident = ctx.enter_context(nc.sbuf_tensor("ident", [P, P], F32))
        out_v = out.rearrange("b (q p) d -> p (b q) d", p=P)
        split = [ctx.enter_context(nc.sbuf_tensor(f"split_{part}", [P, 2, D // P, BANK], F32R)) for part in ("hi", "lo")]
        ffx = FeedForwardInput(nc, ctx, X, ident, split)
        with ExitStack() as attention:
            prep = Preparation(nc, attention, X, ident)
            cross_attention(nc, X, x, ident_c, ctxT, ctx_, mask, xw, xb, ident, split, prep, wqkv, pick_c)
            self_attention(nc, X, prep, ffx, wout, bout, ident)
        routed_ffn(nc, X, ffx, ffn, out_v, ident)


FFN_INPUTS = ("router", "router_bias", "up_bias", "gate_bias", "diag", "tq_of", "up_gate", "down", "down_bias")


def kernel(**inputs):
    import numpy as np
    import concourse.bacc as bacc
    from concourse.bass_utils import run_bass_kernel_spmd

    i = {name: np.asarray(a) for name, a in inputs.items()}

    def ffn(name):
        return i[f"L0_ffn_{name}"]

    E, D, H = ffn("Wup").shape
    NC = E * H // P
    EC = P // H
    heads = 16
    tokens = i["x"].shape[0] * i["x"].shape[1]
    pick = np.zeros((P, heads), np.float32)
    for h in range(heads):
        pick[h, h] = pick[heads + h, h] = 1
    up_gate = np.stack([ffn("Wup"), ffn("Wgate")]).reshape(2, NC, EC, D // P, P, H)
    B, SK, _ = i["ctx_1024"].shape
    NJ = SK // BANK
    ctx_blocks = i["ctx_1024"].reshape(B, NJ, BANK // P, P, D).transpose(0, 1, 3, 2, 4)
    ctxT_blocks = i["ctx_1024"].reshape(B, NJ, BANK, D // P, P).transpose(0, 1, 4, 3, 2)
    mask_blocks = i["mask_BxSxS2_fk0"].reshape(B, -1, P, NJ, BANK).transpose(0, 3, 2, 1, 4)
    arrays = {
        "x": i["x"],
        "ctx_": ctx_blocks,
        "ctxT": ctxT_blocks,
        "mask": mask_blocks,
        "xw": i["L0_xattn_weights"],
        "xb": i["L0_xattn_bias"].reshape(-1, P).T,
        "wqkv": np.concatenate([i["L0_attn_Wq"].T, i["L0_attn_Wk"].T, i["L0_attn_Wv"].T], 1),
        "wout": i["L0_attn_Wout"].T,
        "bout": i["L0_attn_bout"],
        "ident_c": np.eye(P, dtype=np.float32),
        "pick_c": pick,
        "router": ffn("Wr"),
        "router_bias": ffn("br").reshape(E, 1),
        "up_bias": ffn("bup").reshape(NC, P).T,
        "gate_bias": ffn("bgate").reshape(NC, P).T,
        "diag": np.tile(np.eye(E, dtype=np.float32), (2, 1)),
        "tq_of": ((np.arange(P) // E)[:, None] * (tokens // 128) + np.arange(tokens // 128)).astype(np.float32),
        "up_gate": up_gate.transpose(1, 4, 0, 3, 2, 5).reshape(NC, P, 2, D // P, P),
        "down": ffn("Wdown").reshape(NC, P, D),
        "down_bias": ffn("bdown"),
    }
    nc = bacc.Bacc("TRN2", target_bir_lowering=False, num_devices=1)
    feeds, args = {}, {}
    for name, a in arrays.items():
        a = np.ascontiguousarray(a)
        feeds[f"in_{name}"] = a
        args[name] = nc.dram_tensor(f"in_{name}", a.shape, mybir.dt.from_np(a.dtype), kind="ExternalInput").ap()
    args["out"] = nc.dram_tensor("out_0", i["x"].shape, F32, kind="ExternalOutput").ap()
    args["ffn"] = {name: args.pop(name) for name in FFN_INPUTS}
    perceiver_kernel(nc, **args)
    result = run_bass_kernel_spmd(nc, [feeds], core_ids=[0])
    return result.results[0]["out_0"]
```
